# Optimizing a Trainium2 kernel written in Bass

```python
import numpy as np
import jax
import jax.numpy as jnp

def _softmax(x, axis=-1):
    return jax.nn.softmax(x, axis=axis)

def _gelu(x):
    return jax.nn.gelu(x, approximate=True)

def _silu(x):
    return jax.nn.silu(x)

def _sigmoid(x):
    return jax.nn.sigmoid(x)

def _layernorm(x, axis=-1, eps=1e-05):
    m = jnp.mean(x, axis=axis, keepdims=True)
    v = jnp.var(x, axis=axis, keepdims=True)
    return (x - m) / jnp.sqrt(v + eps)

def _scatter_add(tgt, idx, src, axis=0):
    return tgt.at[idx].add(src)

def _segment_sum(src, seg, n):
    return jax.ops.segment_sum(src, seg, n)
kernel_name = 'mk_gnn_resnorm_d2_gnn_r64_2c0baa'

def setup_inputs(seed: int=0):
    np.random.seed(seed)
    _w = jnp.asarray

    def _rec_inputs():
        import jax
        import jax.numpy as jnp
        _gk = jax.random.key(seed)
        x = -0.000202 + 1 * jax.random.normal(jax.random.fold_in(_gk, 1), (50000, 128), jnp.float32)
        src = jax.random.randint(jax.random.fold_in(_gk, 2), (12500,), 0, 50000, jnp.int32)
        dst = jax.random.randint(jax.random.fold_in(_gk, 3), (12500,), 0, 50000, jnp.int32)
        _o = jnp.argsort(dst, stable=True)
        src = src[_o]
        dst = dst[_o]
        edge_attr_128 = 0.000279952 + 1.00013 * jax.random.normal(jax.random.fold_in(_gk, 12), (12500, 128), jnp.float32)
        return (x, src, dst, edge_attr_128)
    x, src, dst, edge_attr_128 = _rec_inputs()

    def _L0_gnn_setup():
        import jax, jax.numpy as jnp
        import numpy as np
        N_NODES = 50000
        N_EDGES = 9375
        DIMS = [128, 128, 128]

        def _sage_mean(h, src, dst, W_self, W_neigh, b):
            agg = jax.ops.segment_sum(h[src], dst, num_segments=N_NODES)
            deg = jax.ops.segment_sum(jnp.ones((src.shape[0],), h.dtype), dst, num_segments=N_NODES)
            mean_neigh = agg / jnp.maximum(deg, 1.0)[:, None]
            return h @ W_self + mean_neigh @ W_neigh + b
        key = jax.random.key(seed)
        ks = jax.random.split(key, 10)
        inp = {'h': jax.random.normal(ks[0], (N_NODES, DIMS[0]), dtype=jnp.float32), 'src': jax.random.randint(ks[1], (N_EDGES,), 0, N_NODES, dtype=jnp.int32), 'dst': jax.random.randint(ks[2], (N_EDGES,), 0, N_NODES, dtype=jnp.int32)}
        for i in range(len(DIMS) - 1):
            fin, fout = (DIMS[i], DIMS[i + 1])
            s = 1.0 / np.sqrt(fin)
            inp[f'W_self{i}'] = jax.random.uniform(ks[3 + 2 * i], (fin, fout), minval=-s, maxval=s, dtype=jnp.float32)
            inp[f'W_neigh{i}'] = jax.random.uniform(ks[4 + 2 * i], (fin, fout), minval=-s, maxval=s, dtype=jnp.float32)
            inp[f'b{i}'] = jnp.zeros((fout,), dtype=jnp.float32)
        return inp
    _L0_gnn_all = _L0_gnn_setup()
    _L0_gnn_in = {k: v for k, v in _L0_gnn_all.items() if k in ('W_self0', 'W_neigh0', 'b0', 'W_self1', 'W_neigh1', 'b1')}
    del _L0_gnn_all

    def _L1_gnn_setup():
        import jax, jax.numpy as jnp
        import numpy as np
        N, E, D, H = (10000, 2500, 128, 4)
        HC = H * D
        LN_EPS = 1e-05
        key = jax.random.key(seed)
        ks = jax.random.split(key, 16)
        s = 1.0 / np.sqrt(D)
        s2 = 1.0 / np.sqrt(HC)
        return {'x': jax.random.normal(ks[0], (N, D), jnp.float32), 'edge_index': jax.random.randint(ks[1], (2, E), 0, N, jnp.int64), 'edge_attr': jax.random.normal(ks[2], (E, D), jnp.float32), 'Wq': jax.random.normal(ks[3], (D, HC), jnp.float32) * s, 'bq': jnp.zeros((HC,), jnp.float32), 'Wk': jax.random.normal(ks[4], (D, HC), jnp.float32) * s, 'bk': jnp.zeros((HC,), jnp.float32), 'Wv': jax.random.normal(ks[5], (D, HC), jnp.float32) * s, 'bv': jnp.zeros((HC,), jnp.float32), 'We': jax.random.normal(ks[6], (D, HC), jnp.float32) * s, 'be': jnp.zeros((HC,), jnp.float32), 'Wskip': jax.random.normal(ks[7], (D, HC), jnp.float32) * s, 'bskip': jnp.zeros((HC,), jnp.float32), 'ln_g': jnp.ones((HC,), jnp.float32), 'ln_b': jnp.zeros((HC,), jnp.float32), 'Wlin': jax.random.normal(ks[8], (HC, D), jnp.float32) * s2, 'blin': jnp.zeros((D,), jnp.float32)}
    _L1_gnn_all = _L1_gnn_setup()
    _L1_gnn_in = {k: v for k, v in _L1_gnn_all.items() if k in ('Wq', 'bq', 'Wk', 'bk', 'Wv', 'bv', 'We', 'be', 'Wskip', 'bskip', 'ln_g', 'ln_b', 'Wlin', 'blin')}
    del _L1_gnn_all
    return {'x': x, 'src': src, 'dst': dst, 'edge_attr_128': edge_attr_128, 'L0_gnn_W_self0': _L0_gnn_in['W_self0'], 'L0_gnn_W_neigh0': _L0_gnn_in['W_neigh0'], 'L0_gnn_b0': _L0_gnn_in['b0'], 'L0_gnn_W_self1': _L0_gnn_in['W_self1'], 'L0_gnn_W_neigh1': _L0_gnn_in['W_neigh1'], 'L0_gnn_b1': _L0_gnn_in['b1'], 'L1_gnn_Wq': _L1_gnn_in['Wq'], 'L1_gnn_bq': _L1_gnn_in['bq'], 'L1_gnn_Wk': _L1_gnn_in['Wk'], 'L1_gnn_bk': _L1_gnn_in['bk'], 'L1_gnn_Wv': _L1_gnn_in['Wv'], 'L1_gnn_bv': _L1_gnn_in['bv'], 'L1_gnn_We': _L1_gnn_in['We'], 'L1_gnn_be': _L1_gnn_in['be'], 'L1_gnn_Wskip': _L1_gnn_in['Wskip'], 'L1_gnn_bskip': _L1_gnn_in['bskip'], 'L1_gnn_ln_g': _L1_gnn_in['ln_g'], 'L1_gnn_ln_b': _L1_gnn_in['ln_b'], 'L1_gnn_Wlin': _L1_gnn_in['Wlin'], 'L1_gnn_blin': _L1_gnn_in['blin']}

def reference(x, src, dst, edge_attr_128, L0_gnn_W_self0, L0_gnn_W_neigh0, L0_gnn_b0, L0_gnn_W_self1, L0_gnn_W_neigh1, L0_gnn_b1, L1_gnn_Wq, L1_gnn_bq, L1_gnn_Wk, L1_gnn_bk, L1_gnn_Wv, L1_gnn_bv, L1_gnn_We, L1_gnn_be, L1_gnn_Wskip, L1_gnn_bskip, L1_gnn_ln_g, L1_gnn_ln_b, L1_gnn_Wlin, L1_gnn_blin):
    import jax
    import jax.numpy as jnp

    def _L0_gnn_ref(h, src, dst, W_self0, W_neigh0, b0, W_self1, W_neigh1, b1):
        import jax, jax.numpy as jnp
        import numpy as np
        N_NODES = 50000
        N_EDGES = 9375
        DIMS = [128, 128, 128]

        def _sage_mean(h, src, dst, W_self, W_neigh, b):
            agg = jax.ops.segment_sum(h[src], dst, num_segments=N_NODES)
            deg = jax.ops.segment_sum(jnp.ones((src.shape[0],), h.dtype), dst, num_segments=N_NODES)
            mean_neigh = agg / jnp.maximum(deg, 1.0)[:, None]
            return h @ W_self + mean_neigh @ W_neigh + b
        h = _sage_mean(h, src, dst, W_self0, W_neigh0, b0)
        h = jax.nn.relu(h)
        h = _sage_mean(h, src, dst, W_self1, W_neigh1, b1)
        return h

    def _L1_gnn_ref(x, edge_index, edge_attr, Wq, bq, Wk, bk, Wv, bv, We, be, Wskip, bskip, ln_g, ln_b, Wlin, blin):
        import jax, jax.numpy as jnp
        import numpy as np
        N, E, D, H = (10000, 2500, 128, 4)
        HC = H * D
        LN_EPS = 1e-05
        n = x.shape[0]
        src, dst = (edge_index[0], edge_index[1])
        q = (x @ Wq + bq).reshape(n, H, D)
        k = (x @ Wk + bk).reshape(n, H, D)
        v = (x @ Wv + bv).reshape(n, H, D)
        e = (edge_attr @ We + be).reshape(-1, H, D)
        kj = k[src] + e
        alpha = jnp.einsum('ehd,ehd->eh', q[dst], kj) / np.sqrt(D)
        amax = jax.ops.segment_max(alpha, dst, num_segments=n)
        ex = jnp.exp(alpha - amax[dst])
        denom = jax.ops.segment_sum(ex, dst, num_segments=n)
        attn = ex / denom[dst]
        msg = (v[src] + e) * attn[:, :, None]
        agg = jax.ops.segment_sum(msg, dst, num_segments=n).reshape(n, HC)
        out = agg + (x @ Wskip + bskip)
        mu = out.mean(-1, keepdims=True)
        var = ((out - mu) ** 2).mean(-1, keepdims=True)
        normed = (out - mu) * jax.lax.rsqrt(var + LN_EPS) * ln_g + ln_b
        lin = normed @ Wlin + blin
        return jax.nn.elu(lin + x)
    edge_index = jnp.stack([src, dst])
    x = _layernorm(x + _L0_gnn_ref(x, src, dst, L0_gnn_W_self0, L0_gnn_W_neigh0, L0_gnn_b0, L0_gnn_W_self1, L0_gnn_W_neigh1, L0_gnn_b1), axis=-1)
    x = _layernorm(x + _L1_gnn_ref(x, edge_index, edge_attr_128, L1_gnn_Wq, L1_gnn_bq, L1_gnn_Wk, L1_gnn_bk, L1_gnn_Wv, L1_gnn_bv, L1_gnn_We, L1_gnn_be, L1_gnn_Wskip, L1_gnn_bskip, L1_gnn_ln_g, L1_gnn_ln_b, L1_gnn_Wlin, L1_gnn_blin), axis=-1)
    return x

_drawn_inputs = setup_inputs


def setup_inputs(seed=0):
    import zlib

    import numpy as np

    out = dict(_drawn_inputs(seed))
    spreads = {'L0_gnn_b0': (0.0, 0.1),
     'L0_gnn_b1': (0.0, 0.1),
     'L1_gnn_bq': (0.0, 0.8),
     'L1_gnn_bk': (0.0, 0.8),
     'L1_gnn_bv': (0.0, 0.655),
     'L1_gnn_be': (0.0, 0.683),
     'L1_gnn_bskip': (0.0, 0.1),
     'L1_gnn_ln_g': (1.0, 0.2),
     'L1_gnn_ln_b': (0.0, 0.1),
     'L1_gnn_blin': (0.0, 0.1)}
    factors = {'L1_gnn_Wk': 2.839}
    for name, (base, spread) in spreads.items():
        noise = np.random.default_rng([zlib.crc32(name.encode()), seed]).standard_normal(out[name].shape)
        drawn = base * np.exp(spread * noise) if base else spread * noise
        out[name] = jnp.asarray(drawn.astype(out[name].dtype))
    for name, factor in factors.items():
        out[name] = (out[name] * factor).astype(out[name].dtype)
    return out
```

```python
from contextlib import ExitStack

import concourse.bass as bass
from concourse import mybir

P = 128
F32 = mybir.dt.float32
BF16 = mybir.dt.bfloat16
I32 = mybir.dt.int32
U16 = mybir.dt.uint16
NOWHERE = 65535
ALU = mybir.AluOpType
ACT = mybir.ActivationFunctionType
AX = mybir.AxisListType
CREDIT = 4
FAR = 1000000
BIG = 1e30
EPS = 1e-5
ACT_SET = "natural_log_exp_and_others"


def gnn_kernel(nc, x, src, dst, edge_attr, Ws0, Wn0, b0, Ws1, Wn1, b1, Wq, bq, Wk, bk, Wv, bv, We, be,
               Wskip, bskip, ln_g, ln_b, Wlin, blin, out):
    N, D = x.shape
    E = src.shape[0]
    HC = Wq.shape[1]
    H = HC // D
    SCALE = float(D) ** -0.5
    R = 4
    BLK = R * P
    NBLK = -(-N // BLK)
    NT = -(-E // P)
    TAIL = E - (NT - 1) * P
    TILES = 104
    assert TILES >= NT + 3 and TILES >= NBLK + 3 and D == P and H == 4
    SUP = TILES // R
    RED = -(-N // P)
    SLOTS = (SUP - 1) * BLK

    x1_tab = nc.dram_tensor("x1_tab", [N + SLOTS, D], F32).ap()
    h1e_tab = nc.dram_tensor("h1e_tab", [SLOTS, D], F32).ap()
    unused = nc.dram_tensor("unused", [16 * BLK, D], F32).ap()
    redirect = nc.dram_tensor("redirect", [RED * P, 1], I32).ap()

    with ExitStack() as ctx:
        def sb(name, shape, dt=F32):
            return ctx.enter_context(nc.sbuf_tensor(name, shape, dt))

        def bank(name):
            return ctx.enter_context(nc.psum_tensor(name, [P, 512], F32))

        def sem(name):
            return ctx.enter_context(nc.semaphore(name))

        ident = sb("ident", [P, P])
        dst_row = sb("dst_row", [P, TILES * P], U16)
        Ws0_s, Wn0_s, Ws1_s, Wn1_s = (sb(n, [P, D]) for n in ("Ws0_s", "Wn0_s", "Ws1_s", "Wn1_s"))
        Wv_s, We_s, Wskip_s = (sb(n, [P, HC]) for n in ("Wv_s", "We_s", "Wskip_s"))
        Wg_s = sb("Wg_s", [P, H, D])
        MG_s = sb("MG_s", [P, 2 * D])
        Aqk_s = sb("Aqk_s", [P, HC])
        Aqe_s = sb("Aqe_s", [P, HC])
        small_w = sb("small_w", [P, 3 * H])
        vcol = sb("vcol", [P, 32])
        e127 = sb("e127", [P, 1])
        cl = sb("cl", [P, D])
        alpha_c = sb("alpha_c", [P, H])
        gc = sb("gc", [P, 1])
        eps = sb("eps", [P, 1])
        ones3 = sb("ones3", [3, P], BF16)
        bias3 = sb("bias3", [3, 1024], BF16)
        B0, B1, BMG, BOUT = 0, 128, 256, 512
        dst_f = sb("dst_f", [P, TILES + 1])
        idx = sb("idx", [P, 4, TILES], I32)
        SRC, DST, REP, EID = range(4)
        look = sb("look", [P, 3, TILES + 8], I32)
        hf = sb("hf", [P, 2, TILES])
        hidx = sb("hidx", [P, TILES], I32)

        big = sb("big", [P, (2 * TILES + R) * P])
        h1s = big[:, 0:(TILES + R) * P].rearrange("p (t d) -> p t d", d=P)
        ypart = big[:, TILES * P:(2 * TILES + R) * P].rearrange("p (t d) -> p t d", d=P)
        carve_at = [0]

        def carve(n):
            a = carve_at[0]
            carve_at[0] += n
            assert carve_at[0] <= (2 * TILES + R) * P
            return big[:, a:a + n]

        set_q, set_k = carve(HC), carve(HC)
        set_qT, set_kT, set_eT, set_sT = (carve(HC).rearrange("p (h d) -> p h d", h=H) for _ in range(4))
        set_wlin = carve(H * D).rearrange("p (h d) -> p h d", h=H)
        set_sc = carve(HC)
        set_b = carve(1024)
        set_r = carve(1024)
        set_t = carve(HC)
        set_u = carve(HC)
        vrow = carve(P)
        rows_f = carve(4 * P).rearrange("p (a d) -> p a d", a=4)
        rows_i = carve(3 * P).bitcast(I32).rearrange("p (a d) -> p a d", a=3)
        col_s = carve(8)
        hi3, mid3, lo3 = (carve(512).bitcast(BF16) for _ in range(3))
        red_init = carve(RED).bitcast(I32)
        b_x = [carve(BLK) for _ in range(4)]
        b_ghost = carve_at[0]
        b_y = carve(BLK)
        b_x1 = [carve(BLK) for _ in range(4)]
        b_x1c = [carve(BLK) for _ in range(2)]
        b_x1T, b_e, b_r, b_w, b_z = (carve(BLK) for _ in range(5))
        b_ghost_end = carve_at[0]
        b_xT, b_h1T = carve(BLK), carve(BLK)
        b_o = [carve(BLK) for _ in range(2)]
        b_junk = carve(BLK)
        b_st = carve(64)
        b_mv1, b_mv2 = carve(8), carve(8)
        b_l, b_rs1, b_nm1, b_var, b_rs2, b_rs3, b_nm3 = (carve(4) for _ in range(7))
        b_small_end = carve_at[0]
        carve_at[0] = 0
        d_ea = [carve(D) for _ in range(2)]
        d_x1s = [carve(D) for _ in range(2)]
        d_x1d = [carve(D) for _ in range(4)]
        d_xT = [carve(3 * D) for _ in range(2)]
        d_same = [carve(P) for _ in range(2)]
        d_last = [carve(P) for _ in range(2)]
        d_neg = [carve(P) for _ in range(2)]
        d_carry = [carve(12) for _ in range(2)]
        d_al = [carve(H) for _ in range(2)]
        d_t1, d_vex = carve(HC), carve(HC)
        d_num = [carve(HC) for _ in range(2)]
        d_rden = [carve(H) for _ in range(2)]
        d_o, d_on, d_onT = carve(HC), carve(HC), carve(HC)
        d_junk = carve(BLK)
        d_small = carve(64)
        d_x1c, d_z, d_e, d_r, d_w = (carve(D) for _ in range(5))
        d_out = [carve(D) for _ in range(4)]
        d_end = carve_at[0]

        GW = D + 1
        a_xs = [sb(f"a_xs{k}", [P, R, GW]) for k in range(2)]
        a_xd = [sb(f"a_xd{k}", [P, R, D]) for k in range(2)]
        a_same = [sb(f"a_same{k}", [P, R, P]) for k in range(2)]
        a_last = [sb(f"a_last{k}", [P, R, P]) for k in range(2)]
        a_agg = sb("a_agg", [P, R, GW])
        a_mean = sb("a_mean", [P, R, D])
        a_rdeg = sb("a_rdeg", [P, R])
        a_xsT, a_mnT, a_h1dT = (sb(n, [P, BLK]) for n in ("a_xsT", "a_mnT", "a_h1dT"))
        a_y = a_xsT
        a_xdT = [sb(f"a_xdT{k}", [P, BLK]) for k in range(2)]
        a_rows = [sb(f"a_rows{k}", [P, R, D]) for k in range(2)]
        a_st = sb("a_st", [P, 64])
        stage = sb("stage", [P, 4, 16], I32)
        got = sb("got", [P, 4, 2], I32)

        pb = [bank(f"pb{i}") for i in range(8)]

        s_ld = sem("s_ld")
        s_ident = sem("s_ident")
        s_sv = sem("s_sv")
        s_sp = sem("s_sp")
        s_sg = sem("s_sg")

        steps, phase_scope = {}, [None]

        def step(name):
            if name not in steps:
                steps[name] = phase_scope[0].enter_context(nc.semaphore(name))
            return steps[name]

        def after(eng, name, it, ago=0):
            eng.wait_ge(step(name), it + (CREDIT + 1 - ago))

        def wait_apart(eng, s, value):
            eng.wait_ge(s, value)
            eng.sem_inc(s_passed, 1)

        def after_apart(eng, name, it, ago=0):
            wait_apart(eng, step(name), it + (CREDIT + 1 - ago))

        def credit(eng, names):
            for n in names.split():
                eng.sem_inc(step(n), CREDIT)

        dma_ld = [sem(f"dma_ld{k}") for k in range(4)]
        dma_st = [sem(f"dma_st{k}") for k in range(4)]
        dma_st1 = [sem(f"dma_st1{k}") for k in range(4)]
        dma_g = [sem(f"dma_g{k}") for k in range(4)]
        dma_g2 = [sem(f"dma_g2{k}") for k in range(4)]
        s_stage = sem("s_stage")
        dma_a = [sem(f"dma_a{k}") for k in range(2)]
        dma_r = [sem(f"dma_r{k}") for k in range(2)]
        s_stage2 = sem("s_stage2")
        dma_c, dma_cr, dma_ea, dma_xs = ([sem(f"{n}{k}") for k in range(2)] for n in ("dma_c", "dma_cr", "dma_ea", "dma_xs"))
        dma_xd, dma_sc = ([sem(f"{n}{k}") for k in range(4)] for n in ("dma_xd", "dma_sc"))
        s_stage3 = sem("s_stage3")
        s_stage4 = sem("s_stage4")
        s_row = sem("s_row")
        s_passed = sem("s_passed")
        s_red = sem("s_red")
        s_look = sem("s_look")

        LOADS = []

        def setup_sync(sp):
            def ld(o, i):
                LOADS.append(1)
                sp.dma_start(o, i).then_inc(s_ld, 16)
            for o, i in ((Ws0_s, Ws0), (Wn0_s, Wn0), (Ws1_s, Ws1), (Wn1_s, Wn1), (Wv_s, Wv), (We_s, We),
                         (Wskip_s, Wskip)):
                ld(o[:], i)
            ld(set_q, Wq)
            ld(set_k, Wk)
            ld(set_wlin, Wlin.rearrange("(h p) n -> p h n", p=P))
            sp.wait_ge(s_sg, 1)
            for r, v in ((0, b0), (1, b1), (30, blin)):
                ld(vrow[r:r + 1, :], v.rearrange("(a n) -> a n", a=1))
            for r, v in ((2, bq), (6, bk), (10, bv), (14, be), (18, bskip), (22, ln_g), (26, ln_b)):
                ld(vrow[r:r + 4, :], v.rearrange("(a n) -> a n", n=P))
            full = NT - 1
            ld(rows_i[0:full, 0, :], dst[0:full * P].rearrange("(t p) -> t p", p=P))
            ld(rows_i[full:NT, 0, 0:TAIL], dst[full * P:E].rearrange("(a n) -> a n", a=1))
            ld(rows_i[0:full, 1, :], dst[1:full * P + 1].rearrange("(t p) -> t p", p=P))
            ld(rows_i[full:NT, 1, 0:TAIL - 1], dst[full * P + 1:E].rearrange("(a n) -> a n", a=1))
            ld(rows_i[0:full, 2, :], src[0:full * P].rearrange("(t p) -> t p", p=P))
            ld(rows_i[full:NT, 2, 0:TAIL], src[full * P:E].rearrange("(a n) -> a n", a=1))
            for o, v in ((set_t, bskip), (set_u, bv), (set_r[:, 512:1024], be)):
                ld(o, v.rearrange("(a n) -> a n", a=1).to_broadcast([P, HC]))
            ld(set_b[:, B0:B0 + D], b0.rearrange("(a n) -> a n", a=1).to_broadcast([P, D]))
            ld(set_b[:, B1:B1 + D], b1.rearrange("(a n) -> a n", a=1).to_broadcast([P, D]))
            ld(cl[:], blin.rearrange("(a n) -> a n", a=1).to_broadcast([P, D]))
            sp.wait_ge(s_sg, 4)
            sp.dma_start(redirect.rearrange("(p j) a -> p (j a)", p=P), red_init).then_inc(s_red, 16)

        def setup_pool(g):
            g.memset(vrow, 0.0)
            g.memset(rows_i[:, 0:2, :], NOWHERE)
            g.memset(rows_i[:, 2, :], 0)
            g.memset(dst_row[:, E:TILES * P], NOWHERE).then_inc(s_sg, 1)
            g.dma_start(dst_row[:, 0:E], dst.rearrange("(a n) -> a n", a=1).to_broadcast([P, E]),
                        max_dma_last_dim=1250).then_inc(s_row, 16)
            g.memset(ident[:], 0.0).then_inc(s_sg, 1)
            g.wait_ge(s_sg, 2)
            g.affine_select(out=ident[:], in_=ident[:], compare_op=ALU.not_equal, fill=1.0, base=0,
                            pattern=[[-1, P]], channel_multiplier=1).then_inc(s_sg, 1)
            g.iota(red_init, [[1, RED]], base=0, channel_multiplier=RED).then_inc(s_sg, 1)
            g.iota(idx[:, EID, :], [[P, TILES]], base=N, channel_multiplier=1).then_inc(s_sg, 1)
            g.memset(big[:, b_ghost:b_ghost_end], 0.0)
            g.memset(big[:, b_ghost_end:b_small_end], 0.0)
            g.memset(stage[:], FAR)
            g.memset(dst_f[:, 0:1], -2.0)
            g.memset(got[:], 0)
            g.memset(look[:, 0:2, :], 0)
            g.memset(look[:, 2, :], FAR)
            for k in range(2):
                g.memset(a_xs[k][:], 1.0)
                g.memset(a_xd[k][:], 0.0)
                g.memset(a_xdT[k][:], 0.0)
            g.memset(a_agg[:], 1.0)
            g.memset(a_mean[:], 0.0)
            g.memset(a_mnT[:], 0.0)
            g.memset(eps[:], EPS).then_inc(s_sg, 1)

        NLOADS = 7 + 3 + 3 + 7 + 6 + 3 + 3
        vi = [0]
        pi = [0]

        def vdone(ins):
            vi[0] += 1
            ins.then_inc(s_sv, 1)
            return vi[0]

        def pdone(ins):
            pi[0] += 1
            ins.then_inc(s_sp, 1)
            return pi[0]

        pm = {n: i + 1 for i, n in enumerate(
            ["vcol", "q", "k", "e", "s", "idx", "A", "Be", "G", "M", "m0", "gb", "cl", "small"])}
        vm = {n: i + 1 for i, n in enumerate(
            ["cast", "mean", "sc", "rep1", "vcol", "cen", "wg", "bke", "q", "k", "e", "s", "idx0", "idx1",
             "A", "Be", "G", "M", "m0", "gb", "cl", "small", "bout", "hi", "r1", "mid", "r2", "lo",
             "p0", "p1", "bias"])}

        def setup_pe(pe):
            def w(n):
                pe.wait_ge(s_sv, vm[n])
            pe.wait_ge(s_ld, 16 * NLOADS)
            pe.wait_ge(s_sg, 3)
            pe.transpose(pb[0][:, 0:P], vrow, ident[:]).then_inc(s_sp, 1)
            for b, m in ((1, set_q), (2, set_k), (3, We_s[:])):
                for h in range(H):
                    t = pe.transpose(pb[b][:, h * P:(h + 1) * P], m[:, h * P:(h + 1) * P], ident[:])
                t.then_inc(s_sp, 1)
            w("sc")
            for h in range(H):
                t = pe.transpose(pb[4][:, h * P:(h + 1) * P], set_sc[:, h * P:(h + 1) * P], ident[:])
            t.then_inc(s_sp, 1)
            w("rep1")
            for a in range(3):
                t = pe.transpose(pb[5][:, a * P:(a + 1) * P], rows_f[:, a, :], ident[:])
            t.then_inc(s_sp, 1)
            w("k")
            for h in range(H):
                t = pe.matmul(pb[1][:, h * P:(h + 1) * P], set_qT[:, h, :], set_kT[:, h, :])
            t.then_inc(s_sp, 1)
            w("e")
            for h in range(H):
                t = pe.matmul(pb[2][:, h * P:(h + 1) * P], set_qT[:, h, :], set_eT[:, h, :])
            t.then_inc(s_sp, 1)
            w("s")

            def sum_heads(o, lhs, rhs):
                for h in range(H):
                    t = pe.matmul(o, lhs(h), rhs(h), start=(h == 0), stop=(h == H - 1))
                return t

            sum_heads(pb[3][:, 0:P], lambda h: set_sT[:, h, :], lambda h: set_sT[:, h, :]).then_inc(s_sp, 1)
            sum_heads(pb[4][:, 0:P], lambda h: set_sT[:, h, :], lambda h: Wg_s[:, h, :]).then_inc(s_sp, 1)
            w("Be")

            def col(c):
                return vcol[:, c:c + 1]

            def wide(c):
                return col(c).to_broadcast([P, P])
            sum_heads(pb[0][:, 0:P], lambda h: wide(18 + h), lambda h: Wg_s[:, h, :]).then_inc(s_sp, 1)
            sum_heads(pb[6][:, 0:P], lambda h: wide(18 + h), lambda h: set_sT[:, h, :])
            sum_heads(pb[6][:, P:P + 1], lambda h: wide(18 + h), lambda h: col(18 + h)).then_inc(s_sp, 1)
            sum_heads(pb[7][:, 0:P], lambda h: wide(26 + h), lambda h: set_wlin[:, h, :]).then_inc(s_sp, 1)
            for h in range(H):
                pe.matmul(pb[1][:, h:h + 1], set_qT[:, h, :], col(6 + h))
                pe.matmul(pb[1][:, 4 + h:5 + h], set_kT[:, h, :], col(2 + h))
                pe.matmul(pb[1][:, 8 + h:9 + h], set_eT[:, h, :], col(2 + h))
                t = pe.matmul(pb[1][:, 12 + h:13 + h], wide(2 + h), col(6 + h))
            t.then_inc(s_sp, 1)

        def setup_dve(v):
            count = [0]

            def d(name, ins):
                ins.then_inc(s_sv, 1)
                count[0] += 1
                assert vm[name] == count[0], name

            def w(n):
                v.wait_ge(s_sv, vm[n])

            def p(n):
                v.wait_ge(s_sp, pm[n])
            v.memset(ones3[:], 1.0)
            v.wait_ge(s_ld, 16 * NLOADS)
            v.wait_ge(s_sg, 6)
            d("cast", v.tensor_copy(rows_f[:, 0:3, :], rows_i[:, 0:3, :]))
            v.tensor_reduce(col_s[:, 0:1], Wskip_s[:], AX.X, ALU.add)
            d("mean", v.tensor_reduce(col_s[:, 1:2], set_t, AX.X, ALU.add))
            w("mean")
            v.tensor_scalar(col_s[:, 2:4], col_s[:, 0:2], 1.0 / HC, None, ALU.mult)
            v.drain()
            d("sc", v.tensor_scalar(set_sc, Wskip_s[:], col_s[:, 2:3], None, ALU.subtract))
            w("cast")
            v.tensor_tensor(rows_f[:, 3, :], rows_f[:, 0, :], rows_f[:, 1, :], ALU.is_equal)
            v.drain()
            d("rep1", v.scalar_tensor_tensor(out=rows_f[:, 1, :], in0=rows_f[:, 3, :], scalar=float(FAR),
                                             in1=rows_f[:, 0, :], op0=ALU.mult, op1=ALU.add))
            p("vcol")
            d("vcol", v.tensor_copy(vcol[:], pb[0][:, 0:32]))
            w("vcol")
            v.tensor_copy(col_s[:, 4:8], vcol[:, 18:22])
            v.drain()
            d("cen", v.tensor_scalar(vcol[:, 18:22], col_s[:, 4:8], col_s[:, 3:4], None, ALU.subtract))
            for h in range(H):
                t = v.tensor_scalar(Wg_s[:, h, :], set_wlin[:, h, :], vcol[:, 22 + h:23 + h], None, ALU.mult)
            d("wg", t)
            d("bke", v.tensor_tensor(vcol[:, 6:10], vcol[:, 6:10], vcol[:, 14:18], ALU.add))
            for n, b, o in (("q", 1, set_qT), ("k", 2, set_kT), ("e", 3, set_eT), ("s", 4, set_sT)):
                p(n)
                d(n, v.tensor_copy(o, pb[b][:].rearrange("p (h d) -> p h d", h=H)))
            p("idx")
            v.tensor_scalar(dst_f[:, 1:TILES + 1], pb[5][:, 0:TILES], 0.0, None, ALU.add)
            v.tensor_copy(idx[:, REP, :], pb[5][:, P:P + TILES])
            v.tensor_copy(idx[:, SRC, :], pb[5][:, 2 * P:2 * P + TILES])
            d("idx0", v.tensor_copy(idx[:, DST, :], pb[5][:, 0:TILES]))
            d("idx1", v.tensor_scalar(e127[:], ident[:, P - 1:P], 1.0, None, ALU.mult))
            p("A")
            d("A", v.tensor_copy(Aqk_s[:], pb[1][:]))
            p("Be")
            d("Be", v.tensor_copy(Aqe_s[:], pb[2][:]))
            p("G")
            d("G", v.tensor_scalar(MG_s[:, D:2 * D], pb[3][:, 0:D], 1.0 / HC, None, ALU.mult))
            p("M")
            d("M", v.tensor_copy(MG_s[:, 0:D], pb[4][:, 0:D]))
            p("m0")
            d("m0", v.tensor_copy(set_b[:, BMG:BMG + D], pb[0][:, 0:D]))
            p("gb")
            v.tensor_scalar(gc[:], pb[6][:, P:P + 1], 1.0 / HC, None, ALU.mult)
            d("gb", v.tensor_scalar(set_b[:, BMG + D:BMG + 2 * D], pb[6][:, 0:D], 2.0 / HC, None, ALU.mult))
            p("cl")
            d("cl", v.tensor_tensor(cl[:], pb[7][:, 0:D], cl[:], ALU.add))
            p("small")
            v.tensor_scalar(alpha_c[:], pb[1][:, 12:16], SCALE, None, ALU.mult)
            d("small", v.tensor_copy(small_w[:], pb[1][:, 0:12]))
            v.tensor_tensor(set_t, set_t, set_u, ALU.add)
            v.drain()
            d("bout", v.tensor_tensor(set_b[:, BOUT:BOUT + HC], set_t, set_r[:, 512:1024], ALU.add))
            w("bout")
            d("hi", v.tensor_copy(hi3, set_b))
            w("hi")
            d("r1", v.tensor_tensor(set_r, set_b, hi3, ALU.subtract))
            w("r1")
            d("mid", v.tensor_copy(mid3, set_r))
            w("mid")
            d("r2", v.tensor_tensor(set_b, set_r, mid3, ALU.subtract))
            w("r2")
            d("lo", v.tensor_copy(lo3, set_b))
            w("lo")
            d("p0", v.tensor_scalar(hi3[0:3, :], hi3[0:3, :], ident[0:3, 0:1], None, ALU.mult))
            w("p0")
            d("p1", v.scalar_tensor_tensor(out=mid3[0:3, :], in0=mid3[0:3, :], scalar=ident[0:3, 1:2],
                                           in1=hi3[0:3, :], op0=ALU.mult, op1=ALU.add))
            w("p1")
            d("bias", v.scalar_tensor_tensor(out=bias3[:], in0=lo3[0:3, :], scalar=ident[0:3, 2:3],
                                             in1=mid3[0:3, :], op0=ALU.mult, op1=ALU.add))

        def bias_mm(pe, o, at, n):
            pe.matmul(o, ones3[:], bias3[:, at:at + n], start=True, stop=False)

        PX, PH, PY, PU, PMG = pb[0], pb[1], pb[2], pb[3], (pb[4], pb[5])
        last_base = N - BLK

        def base_of(j):
            return min(j * BLK, last_base)

        def rows_of(t, b):
            if isinstance(b, int):
                return t[b:b + BLK, :].rearrange("(p r) d -> p (r d)", r=R)
            return t[bass.ds(b, BLK), :].rearrange("(p r) d -> p (r d)", r=R)

        def b_sync(sp):
            ghosts = [0]

            def ghost():
                ghosts[0] += 1
                return unused[(ghosts[0] - 1) * BLK:ghosts[0] * BLK, :].rearrange("(p r) d -> p (r d)", r=R)

            def turn(it, u, load, x1_at, out_at, whole=True):
                if load is not None:
                    after(sp, "b_y", it, 2)
                    sp.dma_start(b_x[(u + 2) % 4], load).then_inc(dma_ld[(u + 2) % 4], 16)
                after(sp, "b_x1", it)
                if not whole:
                    sp.wait_ge(dma_st1[(u - 1) % 4], 16 * ((it - 1) // 4 + 1))
                sp.dma_start(x1_at, b_x1[u]).then_inc(dma_st1[u], 16)
                after(sp, "b_o", it)
                sp.dma_start(out_at, b_o[u % 2]).then_inc(dma_st[u], 16)

            def edge_turn(it):
                def place(t, j):
                    return rows_of(t, base_of(j)) if 0 <= j < NBLK else ghost()
                if it - 3 == NBLK - 1:
                    sp.wait_ge(dma_st[(it - 1) % 4], 16 * ((it - 1) // 4 + 1))
                turn(it, it % 4, rows_of(x, base_of(it + 2)) if it + 2 < TILES else None,
                     place(x1_tab, it - 1), place(out, it - 3), it - 1 != NBLK - 1)

            for j in range(2):
                sp.dma_start(b_x[j], rows_of(x, base_of(j))).then_inc(dma_ld[j], 16)
            for it in range(4):
                edge_turn(it)
            whole = (NBLK - 7) // 4 + 1
            with sp.Fori(1, whole) as i:
                for u in range(4):
                    turn(4 * i + u, u, rows_of(x, i * (4 * BLK) + (u + 2) * BLK),
                         rows_of(x1_tab, i * (4 * BLK) + (u - 1) * BLK),
                         rows_of(out, i * (4 * BLK) + (u - 3) * BLK))
            for it in range(4 * whole, TILES):
                edge_turn(it)
            for k in range(4):
                sp.wait_ge(dma_st[k], 16 * TILES // 4)
                sp.wait_ge(dma_st1[k], 16 * TILES // 4)
            sp.wait_ge(s_red, 16)

        def b_pe(pe):
            credit(pe, "b_pxT b_pmg b_ph b_px1T b_py")
            with pe.Fori(0, TILES // 4) as i:
                for u in range(4):
                    it = 4 * i + u
                    pe.wait_ge(dma_ld[u], 16 * i + 16)
                    after(pe, "b_xT", it, 1)
                    for r in range(R):
                        t = pe.transpose(PX[:, r * P:(r + 1) * P], b_x[u][:, r * D:(r + 1) * D], ident[:])
                    t.then_inc(step("b_pxT"), 1)
                    after(pe, "b_x1T", it, 1)
                    after(pe, "b_z", it, 1)
                    for r in range(R):
                        o = PMG[r // 2][:, (r % 2) * 256:(r % 2) * 256 + 256]
                        bias_mm(pe, o, BMG, 2 * D)
                        t = pe.matmul(o, b_x1T[:, r * P:(r + 1) * P], MG_s[:], start=False, stop=True)
                    t.then_inc(step("b_pmg"), 1)
                    after(pe, "b_xT", it)
                    after(pe, "b_h1", it, 1)
                    pe.matmul(PH[:], Ws0_s[:], b_xT, start=True, stop=True).then_inc(step("b_ph"), 1)
                    after(pe, "b_x1", it)
                    after(pe, "b_x1T", it, 1)
                    for r in range(R):
                        t = pe.transpose(PU[:, r * P:(r + 1) * P], b_x1[u][:, r * D:(r + 1) * D], ident[:])
                    t.then_inc(step("b_px1T"), 1)
                    after(pe, "b_h1", it)
                    after(pe, "b_y", it, 1)
                    for r in range(R):
                        o = PY[:, r * D:(r + 1) * D]
                        bias_mm(pe, o, B1, D)
                        t = pe.matmul(o, b_h1T[:, r * P:(r + 1) * P], Ws1_s[:], start=False, stop=True)
                    t.then_inc(step("b_py"), 1)

        def mv(t):
            return t.rearrange("p (r s) -> p r s", s=2)

        def b_act(act):
            credit(act, "b_xT b_x1T b_h1 b_x1 b_o b_e b_l1 b_r1 b_l2 b_r2 b_l3 b_r3")
            with act.Fori(0, TILES // 4) as i:
                for u in range(4):
                    it = 4 * i + u
                    after(act, "b_pxT", it)
                    after(act, "b_ph", it, 1)
                    act.activation(b_xT, PX[:], ACT.Copy).then_inc(step("b_xT"), 1)
                    after(act, "b_bn1", it, 1)
                    act.activation(b_l, mv(b_mv1)[:, :, 1], ACT.Ln, bias=eps[:, 0:1]).then_inc(step("b_l1"), 1)
                    after(act, "b_l1", it)
                    act.activation(b_rs1, b_l, ACT.Exp, scale=-0.5).then_inc(step("b_r1"), 1)
                    after(act, "b_nm1", it)
                    act.wait_ge(dma_st1[u], 16 * i)
                    after(act, "b_r", it, 1)
                    for r in range(R):
                        t = act.activation(b_x1[u][:, r * D:(r + 1) * D], b_y[:, r * D:(r + 1) * D],
                                           ACT.Identity, scale=b_rs1[:, r:r + 1], bias=b_nm1[:, r:r + 1])
                    t.then_inc(step("b_x1"), 1)
                    after(act, "b_ph", it)
                    after(act, "b_py", it, 1)
                    act.activation(b_h1T, PH[:], ACT.Relu, bias=vcol[:, 0:1]).then_inc(step("b_h1"), 1)
                    after(act, "b_px1T", it)
                    after(act, "b_pmg", it)
                    act.activation(b_x1T, PU[:], ACT.Copy).then_inc(step("b_x1T"), 1)
                    after(act, "b_bn2", it)
                    act.activation(b_l, mv(b_mv2)[:, :, 1], ACT.Ln, bias=eps[:, 0:1]).then_inc(step("b_l3"), 1)
                    after(act, "b_l3", it)
                    act.activation(b_rs3, b_l, ACT.Exp, scale=-0.5).then_inc(step("b_r3"), 1)
                    after(act, "b_nm3", it)
                    act.wait_ge(dma_st[(u - 2) % 4], 16 * i + (16 if u >= 2 else 0))
                    for r in range(R):
                        t = act.activation(b_o[u % 2][:, r * D:(r + 1) * D], b_w[:, r * D:(r + 1) * D],
                                           ACT.Identity, scale=b_rs3[:, r:r + 1], bias=b_nm3[:, r:r + 1])
                    t.then_inc(step("b_o"), 1)
                    after(act, "b_var", it)
                    act.activation(b_l, b_var, ACT.Ln, bias=eps[:, 0:1]).then_inc(step("b_l2"), 1)
                    after(act, "b_l2", it)
                    act.activation(b_rs2, b_l, ACT.Exp, scale=-0.5).then_inc(step("b_r2"), 1)
                    after(act, "b_z", it)
                    act.activation(b_e, b_z, ACT.Exp).then_inc(step("b_e"), 1)

        def b_dve(v):
            credit(v, "b_y b_z b_bn1 b_nm1 b_bn2 b_nm3 b_var b_r b_w b_vs b_s1 b_s2")
            with v.Fori(0, TILES // 4) as i:
                for u in range(4):
                    it = 4 * i + u
                    after(v, "b_e", it, 1)
                    after(v, "b_r", it, 1)
                    after(v, "b_o", it, 1)
                    v.scalar_tensor_tensor(out=b_w, in0=b_e, scalar=1.0, in1=b_r, op0=ALU.min,
                                           op1=ALU.add).then_inc(step("b_w"), 1)
                    after(v, "b_w", it)
                    for r in range(R):
                        t = v.bn_stats(b_st[:, 6 * r:6 * r + 6], b_w[:, r * D:(r + 1) * D])
                    t.then_inc(step("b_s2"), 1)
                    after_apart(v, "b_s2", it)
                    for r in range(R):
                        t = v.bn_aggr(b_mv2[:, 2 * r:2 * r + 2], b_st[:, 6 * r:6 * r + 6])
                    t.then_inc(step("b_bn2"), 1)
                    after(v, "b_r1", it)
                    v.scalar_tensor_tensor(out=b_nm1, in0=mv(b_mv1)[:, :, 0], scalar=-1.0, in1=b_rs1,
                                           op0=ALU.mult, op1=ALU.mult).then_inc(step("b_nm1"), 1)
                    after(v, "b_pmg", it)
                    after(v, "b_l2", it, 1)
                    for r in range(R):
                        t = v.tensor_tensor_reduce(b_junk[:, r * D:(r + 1) * D],
                                                   PMG[r // 2][:, (r % 2) * 256 + 128:(r % 2) * 256 + 256],
                                                   b_x1[(u - 1) % 4][:, r * D:(r + 1) * D], 1.0, gc[:, 0:1],
                                                   ALU.mult, ALU.add, b_var[:, r:r + 1])
                    t.then_inc(step("b_vs"), 1)
                    after(v, "b_vs", it)
                    v.tensor_scalar(b_var, b_var, 0.0, None, ALU.max).then_inc(step("b_var"), 1)
                    after(v, "b_r3", it)
                    after(v, "b_bn2", it)
                    v.scalar_tensor_tensor(out=b_nm3, in0=mv(b_mv2)[:, :, 0], scalar=-1.0, in1=b_rs3,
                                           op0=ALU.mult, op1=ALU.mult).then_inc(step("b_nm3"), 1)
                    after(v, "b_r2", it)
                    after(v, "b_x1c", it, 1)
                    after(v, "b_e", it, 1)
                    for r in range(R):
                        t = v.scalar_tensor_tensor(out=b_z[:, r * D:(r + 1) * D],
                                                   in0=PMG[r // 2][:, (r % 2) * 256:(r % 2) * 256 + 128],
                                                   scalar=b_rs2[:, r:r + 1],
                                                   in1=b_x1c[(u - 1) % 2][:, r * D:(r + 1) * D],
                                                   op0=ALU.mult, op1=ALU.add)
                    t.then_inc(step("b_z"), 1)
                    after(v, "b_z", it)
                    v.scalar_tensor_tensor(out=b_r, in0=b_z, scalar=0.0, in1=b_x1[(u - 1) % 4],
                                           op0=ALU.max, op1=ALU.add).then_inc(step("b_r"), 1)
                    after(v, "b_py", it)
                    after(v, "b_x1", it)
                    v.tensor_tensor(b_y, PY[:], b_x[u], ALU.add).then_inc(step("b_y"), 1)
                    after(v, "b_y", it)
                    for r in range(R):
                        t = v.bn_stats(b_st[:, 24 + 6 * r:30 + 6 * r], b_y[:, r * D:(r + 1) * D])
                    t.then_inc(step("b_s1"), 1)
                    after(v, "b_l1", it)
                    after_apart(v, "b_s1", it)
                    for r in range(R):
                        t = v.bn_aggr(b_mv1[:, 2 * r:2 * r + 2], b_st[:, 24 + 6 * r:30 + 6 * r])
                    t.then_inc(step("b_bn1"), 1)

        def b_pool(g):
            credit(g, "b_x1c")
            g.tensor_copy(look[:, 2, 4:4 + TILES], idx[:, REP, :])
            g.wait_ge(s_red, 16)

            def x1c(it, u):
                after(g, "b_x1", it)
                after(g, "b_z", it, 1)
                g.tensor_tensor(b_x1c[u % 2].rearrange("p (r d) -> p r d", r=R),
                                b_x1[u].rearrange("p (r d) -> p r d", r=R),
                                cl[:].rearrange("p (a d) -> p a d", a=1).to_broadcast([P, R, D]),
                                ALU.add).then_inc(step("b_x1c"), 1)

            def pair(t, k):
                return t[:, k, 0:2].rearrange("p (a b) -> p a b", b=1)

            with g.Fori(0, TILES // 8) as i:
                for u in range(4):
                    x1c(4 * i + u, u)
                    for a in range(2):
                        k = 2 * (u % 2) + a
                        t = 8 * i + (2 * u + a)
                        g.wait_ge(dma_g[k], 32 * i + 16 * (u // 2))
                        g.tensor_copy(pair(stage, k), idx[:, REP:EID + 1, bass.ds(t, 1)]).then_inc(s_stage, 1)
                        wait_apart(g, s_stage, t + 1)
                        g.indirect_dma_start(out=redirect, out_offset=bass.IndirectOffsetOnAxis(ap=stage[:, k, 0:1], axis=0),
                                             in_=stage[:, k, 1:2], in_offset=None, bounds_check=N - 1,
                                             oob_is_err=False).then_inc(dma_g[k], 16)
            for k in range(4):
                g.wait_ge(dma_g[k], 16 * TILES // 4)


            def lookup(rnd, k):
                t = 4 * rnd + k
                g.wait_ge(dma_g2[k], 32 * rnd)
                g.tensor_copy(look[:, 0:2, bass.ds(t, 1)], pair(got, k)).then_inc(s_look, 1)
                g.tensor_copy(pair(stage, k), idx[:, SRC:DST + 1, bass.ds(t, 1)]).then_inc(s_look, 1)
                wait_apart(g, s_look, 2 * t + 2)
                for a in range(2):
                    g.indirect_dma_start(out=got[:, k, a:a + 1], out_offset=None, in_=redirect,
                                         in_offset=bass.IndirectOffsetOnAxis(ap=stage[:, k, a:a + 1], axis=0),
                                         bounds_check=N - 1, oob_is_err=False).then_inc(dma_g2[k], 16)

            with g.Fori(TILES // 8, TILES // 4) as i:
                for u in range(4):
                    x1c(4 * i + u, u)
                    for a in range(2):
                        k = 2 * (u % 2) + a
                        rnd = 2 * (i - TILES // 8) + u // 2
                        lookup(rnd, k)
            g.wait_ge(s_row, 16)
            for k in range(4):
                g.wait_ge(dma_g2[k], 32 * (TILES // 4))
                g.tensor_copy(look[:, 0:2, TILES + k:TILES + k + 1], pair(got, k)).then_inc(s_look, 1)
            g.wait_ge(s_look, 2 * TILES + 4)
            g.tensor_scalar(hf[:, 0, :], look[:, 0, 4:4 + TILES], float(N), float(FAR), ALU.is_lt,
                            ALU.mult).then_inc(s_look, 1)
            g.tensor_scalar(hf[:, 1, :], look[:, 0, 4:4 + TILES], float(-N), None, ALU.add).then_inc(s_look, 1)
            g.wait_ge(s_look, 2 * TILES + 6)
            g.tensor_tensor(hf[:, 1, :], hf[:, 0, :], hf[:, 1, :], ALU.add).then_inc(s_look, 1)
            g.wait_ge(s_look, 2 * TILES + 7)
            g.tensor_copy(hidx[:], hf[:, 1, :]).then_inc(s_look, 1)
            g.wait_ge(s_look, 2 * TILES + 8)

        def run_matrices(v, ph, i, u, s):
            after(v, ph + "_pc", 4 * s - 5)
            for r in range(R):
                t = 4 * s + r
                row = dst_row[:, bass.ds(t * P, P)]
                v.tensor_scalar(a_same[u][:, r, :], row, dst_f[:, bass.ds(t + 1, 1)], None, ALU.is_equal)
                m = v.tensor_scalar(a_last[u][:, r, :], row, dst_f[:, bass.ds(t, 1)], e127[:, 0:1],
                                    ALU.is_equal, ALU.mult)
            m.then_inc(step(ph + "_mat"), 1)

        def chain(pe, ph, u, s, r):
            o = pb[r % 2][:, 0:GW]
            if r == 0:
                after(pe, ph + "_mat", s)
            after(pe, ph + "_agg", 4 * s + r, 2)
            pe.matmul(o, a_same[u][:, r, :], a_xs[u][:, r, :], start=True, stop=False)
            after(pe, ph + "_agg", 4 * s + r, 1)
            t = pe.matmul(o, a_last[u][:, r, :], a_agg[:, (r - 1) % 4, :], start=False, stop=True)
            t.then_inc(step(ph + "_pc"), 1)

        def chain_act(act, ph, s, r):
            after(act, ph + "_pc", 4 * s + r)
            after(act, ph + "_mean", s, 1)
            act.activation(a_agg[:, r, :], pb[r % 2][:, 0:GW], ACT.Copy).then_inc(step(ph + "_agg"), 1)

        def mean_dve(v, ph, s):
            after(v, ph + "_agg", 4 * s + 3)
            v.tensor_scalar(a_rdeg[:], a_agg[:, :, D], 1.0, None, ALU.max).then_inc(step(ph + "_dg"), 1)
            after(v, ph + "_dg", s)
            v.reciprocal(a_rdeg[:], a_rdeg[:]).then_inc(step(ph + "_rd"), 1)
            after(v, ph + "_rd", s)
            after(v, ph + "_pmT", s)
            v.tensor_tensor(a_mean[:], a_agg[:, :, 0:D],
                            a_rdeg[:].rearrange("p (r a) -> p r a", a=1).to_broadcast([P, R, D]),
                            ALU.mult).then_inc(step(ph + "_mean"), 1)

        TURNS = TILES // R

        def a_pool(g):
            def turn(s, u, i):
                after(g, "a_pc", 4 * s - 5)
                after(g, "a_xdc", s, 2)
                g.tensor_copy(stage[:, 2 * u:2 * u + 2, 0:4], idx[:, SRC:DST + 1, bass.ds(4 * s, 4)]).then_inc(s_stage2, 1)
                wait_apart(g, s_stage2, s + 1)
                for r in range(R):
                    for a, o in ((0, a_xs[u][:, r, 0:D]), (1, a_xd[u][:, r, :])):
                        g.indirect_dma_start(out=o, out_offset=None, in_=x,
                                             in_offset=bass.IndirectOffsetOnAxis(ap=stage[:, 2 * u + a, r:r + 1], axis=0),
                                             bounds_check=N - 1, oob_is_err=False).then_inc(dma_a[u], 16)
            with g.Fori(0, TURNS // 2) as i:
                for u in range(2):
                    turn(2 * i + u, u, i)

        def a_dve(v):
            v.memset(ypart[:, 0:4, :], 0.0)
            v.drain()
            credit(v, "a_mat a_dg a_rd a_mean a_mnT a_rows a_yp a_xdc")
            with v.Fori(0, TURNS // 2) as i:
                for u in range(2):
                    s = 2 * i + u
                    run_matrices(v, "a", i, u, s)
                    after(v, "a_pmT", s)
                    after(v, "a_ph1d", s, 1)
                    v.tensor_copy(a_mnT[:], pb[4][:]).then_inc(step("a_mnT"), 1)
                    after(v, "a_prow", s)
                    v.wait_ge(dma_r[u], 16 * i)
                    v.tensor_copy(a_rows[u][:], pb[4][:].rearrange("p (r d) -> p r d", r=R)).then_inc(step("a_rows"), 1)
                    after(v, "a_py", s)
                    after(v, "a_xdc", s, 1)
                    yp = ypart[:, bass.ds(4 * s, 4), :]
                    v.tensor_tensor(yp, pb[7][:].rearrange("p (r d) -> p r d", r=R), yp,
                                    ALU.add).then_inc(step("a_yp"), 1)
                    v.wait_ge(dma_a[u], 2 * R * 16 * (i + 1))
                    v.tensor_copy(ypart[:, bass.ds(4 * s + 4, 4), :], a_xd[u][:]).then_inc(step("a_xdc"), 1)
                    mean_dve(v, "a", s)

        def a_act(act):
            credit(act, "a_xsT a_xdT a_h1s a_h1d a_agg")
            with act.Fori(0, TURNS // 2) as i:
                for u in range(2):
                    s = 2 * i + u
                    chain_act(act, "a", s, 0)
                    after(act, "a_pxs", s)
                    after(act, "a_ph1s", s, 1)
                    act.activation(a_xsT[:], pb[2][:], ACT.Copy).then_inc(step("a_xsT"), 1)
                    chain_act(act, "a", s, 1)
                    after(act, "a_ph1d", s)
                    after(act, "a_py", s, 1)
                    act.activation(a_h1dT[:], pb[6][:], ACT.Relu, bias=vcol[:, 0:1]).then_inc(step("a_h1d"), 1)
                    after(act, "a_pxd", s)
                    act.activation(a_xdT[u][:], pb[3][:], ACT.Copy).then_inc(step("a_xdT"), 1)
                    chain_act(act, "a", s, 2)
                    after(act, "a_ph1s", s)
                    act.activation(h1s[:, bass.ds(4 * s, 4), :], pb[5][:].rearrange("p (r d) -> p r d", r=R),
                                   ACT.Relu).then_inc(step("a_h1s"), 1)
                    chain_act(act, "a", s, 3)

        def a_pe(pe):
            credit(pe, "a_pmT a_pxs a_ph1d a_pxd a_ph1s a_prow a_py a_pc")
            with pe.Fori(0, TURNS // 2) as i:
                for u in range(2):
                    s = 2 * i + u
                    after(pe, "a_mean", s, 1)
                    after(pe, "a_rows", s, 1)
                    for r in range(R):
                        t = pe.transpose(pb[4][:, r * P:(r + 1) * P], a_mean[:, r, :], ident[:])
                    t.then_inc(step("a_pmT"), 1)
                    pe.wait_ge(dma_a[u], 2 * R * 16 * (i + 1))
                    chain(pe, "a", u, s, 0)
                    after(pe, "a_xsT", s, 1)
                    for r in range(R):
                        t = pe.transpose(pb[2][:, r * P:(r + 1) * P], a_xs[u][:, r, 0:D], ident[:])
                    t.then_inc(step("a_pxs"), 1)
                    after(pe, "a_mnT", s)
                    after(pe, "a_xdT", s, 1)
                    after(pe, "a_h1d", s, 1)
                    pe.matmul(pb[6][:], Ws0_s[:], a_xdT[1 - u][:], start=True, stop=False)
                    pe.matmul(pb[6][:], Wn0_s[:], a_mnT[:], start=False, stop=True).then_inc(step("a_ph1d"), 1)
                    chain(pe, "a", u, s, 1)
                    for r in range(R):
                        t = pe.transpose(pb[3][:, r * P:(r + 1) * P], a_xd[u][:, r, :], ident[:])
                    t.then_inc(step("a_pxd"), 1)
                    after(pe, "a_xsT", s)
                    after(pe, "a_h1s", s, 1)
                    for r in range(R):
                        o = pb[5][:, r * D:(r + 1) * D]
                        bias_mm(pe, o, B0, D)
                        t = pe.matmul(o, a_xsT[:, r * P:(r + 1) * P], Ws0_s[:], start=False, stop=True)
                    t.then_inc(step("a_ph1s"), 1)
                    chain(pe, "a", u, s, 2)
                    after(pe, "a_h1d", s)
                    for r in range(R):
                        t = pe.transpose(pb[4][:, r * P:(r + 1) * P], a_h1dT[:, r * P:(r + 1) * P], ident[:])
                    t.then_inc(step("a_prow"), 1)
                    after(pe, "a_yp", s, 1)
                    for r in range(R):
                        o = pb[7][:, r * D:(r + 1) * D]
                        bias_mm(pe, o, B1, D)
                        t = pe.matmul(o, a_h1dT[:, r * P:(r + 1) * P], Ws1_s[:], start=False, stop=True)
                    t.then_inc(step("a_py"), 1)
                    chain(pe, "a", u, s, 3)

        def edge_rows(tab, at):
            return tab[bass.ds(at, BLK), :].rearrange("(r p) d -> p r d", p=P)

        def a_sync(sp):
            after(sp, "a_rows", 0)
            sp.dma_start(unused[12 * BLK:13 * BLK, :].rearrange("(r p) d -> p r d", p=P), a_rows[0][:]).then_inc(dma_r[0], 16)
            after(sp, "a_rows", 1)
            sp.dma_start(edge_rows(h1e_tab, 0), a_rows[1][:]).then_inc(dma_r[1], 16)
            with sp.Fori(1, TURNS // 2) as i:
                for u in range(2):
                    after(sp, "a_rows", 2 * i + u)
                    sp.dma_start(edge_rows(h1e_tab, i * (2 * BLK) + (u - 1) * BLK), a_rows[u][:]).then_inc(dma_r[u], 16)
            for u in range(2):
                sp.wait_ge(dma_r[u], 16 * (TURNS // 2))

        def c_pool(g):
            with g.Fori(0, TURNS // 2) as i:
                for u in range(2):
                    s = 2 * i + u
                    after(g, "c_fill", s)
                    g.tensor_copy(stage[:, u, 4:8], hidx[:, bass.ds(4 * s, 4)]).then_inc(s_stage3, 1)
                    wait_apart(g, s_stage3, s + 1)
                    for r in range(R):
                        g.indirect_dma_start(out=a_xs[u][:, r, 0:D], out_offset=None, in_=h1e_tab,
                                             in_offset=bass.IndirectOffsetOnAxis(ap=stage[:, u, 4 + r:5 + r], axis=0),
                                             bounds_check=SLOTS - 1, oob_is_err=False).then_inc(dma_c[u], 16)

        def c_dve(v):
            credit(v, "c_mat c_dg c_rd c_mean c_mnT c_y c_st c_bn c_nm")
            with v.Fori(0, TURNS // 2) as i:
                for u in range(2):
                    s = 2 * i + u
                    run_matrices(v, "c", i, u, s)
                    after(v, "c_pmT", s)
                    after(v, "c_py", s, 1)
                    v.tensor_copy(a_mnT[:], pb[4][:]).then_inc(step("c_mnT"), 1)
                    after(v, "c_py", s)
                    after(v, "c_x1", s, 1)
                    v.tensor_tensor(a_y[:].rearrange("p (r d) -> p r d", r=R), pb[7][:].rearrange("p (r d) -> p r d", r=R),
                                    ypart[:, bass.ds(4 * s, 4), :], ALU.add).then_inc(step("c_y"), 1)
                    after(v, "c_y", s)
                    for r in range(R):
                        t = v.bn_stats(a_st[:, 6 * r:6 * r + 6], a_y[:, r * D:(r + 1) * D])
                    t.then_inc(step("c_st"), 1)
                    after_apart(v, "c_st", s)
                    for r in range(R):
                        t = v.bn_aggr(a_st[:, 24 + 2 * r:26 + 2 * r], a_st[:, 6 * r:6 * r + 6])
                    t.then_inc(step("c_bn"), 1)
                    after(v, "c_r", s)
                    v.scalar_tensor_tensor(out=a_st[:, 40:44], in0=mv(a_st[:, 24:32])[:, :, 0], scalar=-1.0,
                                           in1=a_st[:, 36:40], op0=ALU.mult, op1=ALU.mult).then_inc(step("c_nm"), 1)
                    mean_dve(v, "c", s)

        def c_act(act):
            credit(act, "c_fill c_x1 c_l c_r c_agg")

            def fill(s, u):
                after(act, "c_pc", 4 * s - 5)
                act.activation(a_xs[u][:, :, 0:D], h1s[:, bass.ds(4 * s, 4), :], ACT.Copy).then_inc(step("c_fill"), 1)
            act.activation(a_xs[0][:, :, 0:D], h1s[:, 0:4, :], ACT.Copy).then_inc(step("c_fill"), 1)
            with act.Fori(0, TURNS // 2) as i:
                for u in range(2):
                    s = 2 * i + u
                    fill(s + 1, 1 - u)
                    for r in range(3):
                        chain_act(act, "c", s, r)
                    after(act, "c_bn", s)
                    act.activation(a_st[:, 32:36], mv(a_st[:, 24:32])[:, :, 1], ACT.Ln, bias=eps[:, 0:1]).then_inc(step("c_l"), 1)
                    after(act, "c_l", s)
                    act.activation(a_st[:, 36:40], a_st[:, 32:36], ACT.Exp, scale=-0.5).then_inc(step("c_r"), 1)
                    after(act, "c_nm", s)
                    act.wait_ge(dma_cr[u], 16 * i)
                    for r in range(R):
                        t = act.activation(a_rows[u][:, r, :], a_y[:, r * D:(r + 1) * D], ACT.Identity,
                                           scale=a_st[:, 36 + r:37 + r], bias=a_st[:, 40 + r:41 + r])
                    t.then_inc(step("c_x1"), 1)
                    chain_act(act, "c", s, 3)

        def c_pe(pe):
            credit(pe, "c_pmT c_py c_pc")
            with pe.Fori(0, TURNS // 2) as i:
                for u in range(2):
                    s = 2 * i + u
                    after(pe, "c_mean", s, 1)
                    after(pe, "c_mnT", s, 1)
                    for r in range(R):
                        t = pe.transpose(pb[4][:, r * P:(r + 1) * P], a_mean[:, r, :], ident[:])
                    t.then_inc(step("c_pmT"), 1)
                    pe.wait_ge(dma_c[u], R * 16 * (i + 1))
                    chain(pe, "c", u, s, 0)
                    after(pe, "c_mnT", s)
                    after(pe, "c_y", s, 1)
                    for r in range(R):
                        t = pe.matmul(pb[7][:, r * D:(r + 1) * D], a_mnT[:, r * P:(r + 1) * P], Wn1_s[:],
                                      start=True, stop=True)
                    t.then_inc(step("c_py"), 1)
                    for r in range(1, 4):
                        chain(pe, "c", u, s, r)

        def c_sync(sp):
            after(sp, "c_x1", 0)
            sp.dma_start(unused[13 * BLK:14 * BLK, :].rearrange("(r p) d -> p r d", p=P), a_rows[0][:]).then_inc(dma_cr[0], 16)
            after(sp, "c_x1", 1)
            sp.dma_start(edge_rows(x1_tab, N), a_rows[1][:]).then_inc(dma_cr[1], 16)
            with sp.Fori(1, TURNS // 2) as i:
                for u in range(2):
                    after(sp, "c_x1", 2 * i + u)
                    sp.dma_start(edge_rows(x1_tab, i * (2 * BLK) + (N + (u - 1) * BLK)), a_rows[u][:]).then_inc(dma_cr[u], 16)
            for u in range(2):
                sp.wait_ge(dma_cr[u], 16 * (TURNS // 2))

        TB, UB, WB, VB, NB, CB, KB, LB = pb
        LY, LR, LC, LD = 0, 128, 132, 144
        mcar, fx, den, ssum, amx, stt, mvv = (d_small[:, a:b] for a, b in
                                              ((0, 4), (4, 12), (12, 16), (16, 20), (20, 24), (24, 30), (30, 32)))
        lw, rs, nm, st2, mv2, lw2, rs2, nm2, dfx = (d_small[:, a:b] for a, b in
                                                   ((32, 33), (33, 34), (34, 35), (36, 42), (42, 44), (44, 45),
                                                    (45, 46), (46, 47), (48, 56)))
        scr = [sb(f"d_scr{k}", [P, 16]) for k in range(4)]

        def hs(t, h):
            return t[:, h * D:(h + 1) * D]

        def heads(t):
            return t.rearrange("p (h d) -> p h d", h=H)

        def d_sync(sp):
            def load(it, u, b, n=P):
                after(sp, "d_al", it, 2)
                sp.dma_start(d_ea[u % 2][0:n, :], edge_attr[bass.ds(b, n), :] if not isinstance(b, int)
                             else edge_attr[b:b + n, :]).then_inc(dma_ea[u % 2], 16)
            with sp.Fori(0, (NT - 1) // 2) as i:
                for u in range(2):
                    load(2 * i + u, u, i * (2 * P) + u * P)
            for it in range(2 * ((NT - 1) // 2), TILES):
                if it < NT - 1:
                    load(it, it, it * P)
                elif it == NT - 1:
                    load(it, it, it * P, TAIL)
                else:
                    load(it, it, E - P)

        def d_pool(g):
            def gather(it, u):
                after(g, "d_al", it, 2)
                after(g, "d_r", it, 2)
                g.tensor_copy(stage[:, u, 8:10].rearrange("p (a b) -> p a b", b=1),
                              look[:, 0:2, bass.ds(it + 4, 1)]).then_inc(s_stage4, 1)
                wait_apart(g, s_stage4, 2 * it + 1)
                for a, o, q in ((0, d_x1s[u % 2], dma_xs[u % 2]), (1, d_x1d[u], dma_xd[u])):
                    g.indirect_dma_start(out=o, out_offset=None, in_=x1_tab,
                                         in_offset=bass.IndirectOffsetOnAxis(ap=stage[:, u, 8 + a:9 + a], axis=0),
                                         bounds_check=N + SLOTS - 1, oob_is_err=False).then_inc(q, 16)

            gather(0, 0)
            with g.Fori(0, TILES // 4) as i:
                for u in range(4):
                    it = 4 * i + u
                    g.tensor_copy(stage[:, u, 10:11], look[:, 2, bass.ds(it + 1, 1)]).then_inc(s_stage4, 1)
                    gather(it + 1, (u + 1) % 4)
                    after_apart(g, "d_o2", it)
                    g.indirect_dma_start(out=out, out_offset=bass.IndirectOffsetOnAxis(ap=stage[:, u, 10:11], axis=0),
                                         in_=d_out[u], in_offset=None, bounds_check=N - 1,
                                         oob_is_err=False).then_inc(dma_sc[u], 16)
            g.wait_ge(dma_xs[0], 16 * (TILES // 2 + 1))
            g.wait_ge(dma_xd[0], 16 * (TILES // 4 + 1))
            for u in range(4):
                g.wait_ge(dma_sc[u], 16 * TILES // 4)

        def d_pe(pe):
            credit(pe, "d_pc d_pa d_pC d_pT d_pK d_pO d_pU d_pV d_pL d_pN")
            def X(b, a):
                return d_xT[b][:, a * D:(a + 1) * D]
            with pe.Fori(0, TILES // 4) as i:
                for u in range(4):
                    it = 4 * i + u
                    k, q = u % 2, (u - 1) % 2
                    after(pe, "d_z", it, 1)
                    after(pe, "d_den", it, 1)
                    pe.matmul(LB[:, LC:LC + 9], d_last[q], d_carry[k][:, 0:9], start=True, stop=True).then_inc(step("d_pc"), 1)
                    after(pe, "d_vex", it, 1)
                    after(pe, "d_al", it, 1)
                    for h in range(H):
                        t = pe.transpose(hs(VB, h), d_al[q][:, h:h + 1].to_broadcast([P, P]), ident[:])
                    t.then_inc(step("d_pa"), 1)
                    after(pe, "d_num", it, 1)
                    pe.matmul(CB[:], d_last[q], d_num[k], start=True, stop=True).then_inc(step("d_pC"), 1)
                    pe.wait_ge(dma_ea[k], 16 * (2 * i + (u // 2 + 1)))
                    pe.wait_ge(dma_xs[k], 16 * (2 * i + (u // 2 + 1)))
                    pe.wait_ge(dma_xd[u], 16 * (i + 1))
                    after(pe, "d_onT", it, 1)
                    for a, s_ in ((0, d_x1s[k]), (1, d_x1d[u]), (2, d_ea[k])):
                        t = pe.transpose(TB[:, a * P:(a + 1) * P], s_, ident[:])
                    t.then_inc(step("d_pT"), 1)
                    after(pe, "d_o", it)
                    bias_mm(pe, KB[:], BOUT, HC)
                    pe.matmul(KB[:], X(q, 1), Wskip_s[:], start=False, stop=True).then_inc(step("d_pK"), 1)
                    after(pe, "d_xT", it)
                    after(pe, "d_on", it)
                    for h in range(H):
                        t = pe.transpose(hs(TB, h), hs(d_on, h), ident[:])
                    t.then_inc(step("d_pO"), 1)
                    pe.matmul(UB[:], X(k, 1), Aqk_s[:], start=True, stop=True)
                    pe.matmul(WB[:], X(k, 1), Aqe_s[:], start=True, stop=True)
                    after(pe, "d_car", it)
                    for n, a in enumerate((1, 0, 2)):
                        t = pe.matmul(LB[:, LR:LR + H], X(k, a), small_w[:, n * H:(n + 1) * H],
                                      start=(n == 0), stop=(n == 2))
                    t.then_inc(step("d_pU"), 1)
                    after(pe, "d_max", it)
                    pe.matmul(VB[:], X(q, 0), Wv_s[:], start=True, stop=False)
                    pe.matmul(VB[:], X(q, 2), We_s[:], start=False, stop=True).then_inc(step("d_pV"), 1)
                    after(pe, "d_onT", it)
                    after(pe, "d_R", it)
                    for h in range(H):
                        pe.matmul(LB[:, LY:LY + D], hs(d_onT, h), Wg_s[:, h, :], start=(h == 0), stop=(h == H - 1))
                    after(pe, "d_ex", it)
                    pe.matmul(LB[:, LD:LD + H], d_same[q], fx[:, 0:H], start=True, stop=True).then_inc(step("d_pL"), 1)
                    after(pe, "d_vex", it)
                    pe.matmul(NB[:], d_same[q], d_vex, start=True, stop=True).then_inc(step("d_pN"), 1)

        def d_act(act):
            credit(act, "d_xT d_ln d_rs d_on d_ex d_t1 d_onT d_vex d_e d_ln2 d_rs2 d_o2")
            with act.Fori(0, TILES // 4) as i:
                for u in range(4):
                    it = 4 * i + u
                    k = u % 2
                    after(act, "d_pT", it)
                    after(act, "d_pV", it, 1)
                    after(act, "d_pU", it, 1)
                    act.activation(d_xT[k], TB[:, 0:3 * P], ACT.Copy).then_inc(step("d_xT"), 1)
                    after(act, "d_bn", it)
                    act.activation(lw, mvv[:, 1:2], ACT.Ln, bias=eps[:, 0:1]).then_inc(step("d_ln"), 1)
                    after(act, "d_ln", it)
                    act.activation(rs, lw, ACT.Exp, scale=-0.5).then_inc(step("d_rs"), 1)
                    after(act, "d_nm", it)
                    after(act, "d_pO", it, 1)
                    act.activation(d_on, d_o, ACT.Identity, scale=rs, bias=nm).then_inc(step("d_on"), 1)
                    after(act, "d_dfx", it)
                    after(act, "d_den", it, 1)
                    act.activation(fx, dfx, ACT.Exp).then_inc(step("d_ex"), 1)
                    after(act, "d_pC", it)
                    after(act, "d_num", it, 1)
                    after(act, "d_ex", it)
                    for h in range(H):
                        t = act.activation(hs(d_t1, h), hs(CB, h), ACT.Copy, scale=fx[:, 4 + h:5 + h])
                    t.then_inc(step("d_t1"), 1)
                    after(act, "d_pO", it)
                    after(act, "d_pL", it, 1)
                    act.activation(d_onT, TB[:], ACT.Copy).then_inc(step("d_onT"), 1)
                    after(act, "d_pV", it)
                    after(act, "d_pN", it, 1)
                    for h in range(H):
                        t = act.activation(hs(d_vex, h), hs(VB, h), ACT.Copy, scale=fx[:, h:h + 1])
                    t.then_inc(step("d_vex"), 1)
                    after(act, "d_bn2", it)
                    act.activation(lw2, mv2[:, 1:2], ACT.Ln, bias=eps[:, 0:1]).then_inc(step("d_ln2"), 1)
                    after(act, "d_ln2", it)
                    act.activation(rs2, lw2, ACT.Exp, scale=-0.5).then_inc(step("d_rs2"), 1)
                    after(act, "d_nm2", it)
                    act.wait_ge(dma_sc[u], 16 * i)
                    act.activation(d_out[u], d_w, ACT.Identity, scale=rs2, bias=nm2).then_inc(step("d_o2"), 1)
                    after(act, "d_z", it)
                    after(act, "d_w", it)
                    act.activation(d_e, d_z, ACT.Exp).then_inc(step("d_e"), 1)

        def d_dve(v):
            for t in (*d_num, d_o, d_e, d_r, d_w, d_onT, d_small, *d_xT, *d_last, *d_neg, *d_al, d_x1c,
                      *d_x1d[2:]):
                v.memset(t, 0.0)
            for t in (*d_carry, *d_rden, *d_same):
                v.memset(t, 1.0)
            v.memset(KB[:], 1.0)
            v.drain()
            credit(v, "d_al d_r d_z d_den d_num d_o d_car d_max d_R d_bn d_nm d_dfx d_w d_bn2 d_nm2 d_mat d_a1 d_st "
                      "d_st2 d_mc d_d0 d_x1c d_g1 d_g2")
            with v.Fori(0, TILES // 4) as i:
                for u in range(4):
                    it = 4 * i + u
                    k, q = u % 2, (u - 1) % 2
                    after(v, "d_num", it, 1)
                    after(v, "d_den", it, 1)
                    after(v, "d_on", it, 1)
                    after(v, "d_pK", it, 1)
                    for h in range(H):
                        t = v.scalar_tensor_tensor(out=hs(d_o, h), in0=hs(d_num[k], h), scalar=d_rden[k][:, h:h + 1],
                                                   in1=hs(KB, h), op0=ALU.mult, op1=ALU.add)
                    t.then_inc(step("d_o"), 1)
                    after(v, "d_o", it)
                    v.bn_stats(stt, d_o).then_inc(step("d_st"), 1)
                    after(v, "d_pc", it)
                    s = scr[u]
                    v.tensor_copy(s[:, 0:9], LB[:, LC:LC + 9]).then_inc(step("d_car"), 1)
                    after_apart(v, "d_st", it)
                    v.bn_aggr(mvv, stt).then_inc(step("d_bn"), 1)
                    after(v, "d_car", it)
                    v.tensor_scalar(s[:, 9:10], s[:, 4:5], 1.0, BIG, ALU.subtract, ALU.mult).then_inc(step("d_mc"), 1)
                    after(v, "d_mc", it)
                    v.tensor_scalar(s[:, 10:14], s[:, 0:4], s[:, 9:10], None, ALU.add).then_inc(step("d_d0"), 1)
                    after(v, "d_pa", it)
                    after_apart(v, "d_d0", it)
                    for h in range(H):
                        t = v.tensor_tensor_reduce(hs(d_junk, h), hs(VB, h), d_neg[q], 1.0, s[:, 10 + h:11 + h],
                                                   ALU.add, ALU.max, d_carry[q][:, h:h + 1])
                    t.then_inc(step("d_max"), 1)
                    after(v, "d_max", it)
                    after(v, "d_ex", it, 1)
                    v.tensor_tensor(dfx[:, 0:4], d_al[q], d_carry[q][:, 0:4], ALU.subtract)
                    v.tensor_tensor(dfx[:, 4:8], s[:, 10:14], d_carry[q][:, 0:4], ALU.subtract).then_inc(step("d_dfx"), 1)
                    after(v, "d_rs", it)
                    v.scalar_tensor_tensor(out=nm, in0=mvv[:, 0:1], scalar=-1.0, in1=rs, op0=ALU.mult,
                                           op1=ALU.mult).then_inc(step("d_nm"), 1)
                    after(v, "d_e", it, 1)
                    after(v, "d_r", it, 1)
                    after(v, "d_o2", it, 1)
                    v.scalar_tensor_tensor(out=d_w, in0=d_e, scalar=1.0, in1=d_r, op0=ALU.min,
                                           op1=ALU.add).then_inc(step("d_w"), 1)
                    after(v, "d_w", it)
                    v.bn_stats(st2, d_w).then_inc(step("d_st2"), 1)
                    row = dst_row[:, bass.ds(it * P, P)]
                    mine, prev = dst_f[:, bass.ds(it + 1, 1)], dst_f[:, bass.ds(it, 1)]
                    after(v, "d_pN", it, 1)
                    v.tensor_scalar(d_same[k], row, mine, None, ALU.is_equal)
                    v.tensor_scalar(d_neg[k], row, mine, -BIG, ALU.not_equal, ALU.mult)
                    v.tensor_scalar(d_last[k], row, prev, e127[:, 0:1], ALU.is_equal, ALU.mult).then_inc(step("d_mat"), 1)
                    after_apart(v, "d_st2", it)
                    v.bn_aggr(mv2, st2).then_inc(step("d_bn2"), 1)
                    after(v, "d_pU", it)
                    v.scalar_tensor_tensor(out=ssum, in0=LB[:, LR:LR + H], scalar=SCALE, in1=alpha_c[:],
                                           op0=ALU.mult, op1=ALU.add).then_inc(step("d_R"), 1)
                    after(v, "d_R", it)
                    for h in range(H):
                        t = v.tensor_tensor_reduce(hs(d_junk, h), hs(UB, h), d_x1s[k], SCALE, ssum[:, h:h + 1],
                                                   ALU.mult, ALU.add, amx[:, h:h + 1])
                    t.then_inc(step("d_a1"), 1)
                    after(v, "d_a1", it)
                    for h in range(H):
                        t = v.tensor_tensor_reduce(hs(d_junk, h), hs(WB, h), d_ea[k], SCALE, amx[:, h:h + 1],
                                                   ALU.mult, ALU.add, d_al[k][:, h:h + 1])
                    t.then_inc(step("d_al"), 1)
                    after(v, "d_rs2", it)
                    v.scalar_tensor_tensor(out=nm2, in0=mv2[:, 0:1], scalar=-1.0, in1=rs2, op0=ALU.mult,
                                           op1=ALU.mult).then_inc(step("d_nm2"), 1)
                    after(v, "d_pL", it)
                    x1d = d_x1d[(u - 2) % 4]
                    v.tensor_tensor(d_x1c, x1d, cl[:], ALU.add).then_inc(step("d_x1c"), 1)
                    after(v, "d_x1c", it)
                    after(v, "d_e", it, 1)
                    v.tensor_tensor(d_z, LB[:, LY:LY + D], d_x1c, ALU.add).then_inc(step("d_z"), 1)
                    after(v, "d_z", it)
                    v.scalar_tensor_tensor(out=d_r, in0=d_z, scalar=0.0, in1=x1d, op0=ALU.max,
                                           op1=ALU.add).then_inc(step("d_r"), 1)
                    v.tensor_tensor(s[:, 0:4], s[:, 5:9], fx[:, 4:8], ALU.mult).then_inc(step("d_g1"), 1)
                    after(v, "d_g1", it)
                    v.tensor_tensor(d_carry[q][:, 5:9], LB[:, LD:LD + H], s[:, 0:4], ALU.add).then_inc(step("d_g2"), 1)
                    after(v, "d_g2", it)
                    v.reciprocal(d_rden[q], d_carry[q][:, 5:9]).then_inc(step("d_den"), 1)
                    after(v, "d_pN", it)
                    after(v, "d_t1", it)
                    v.tensor_tensor(d_num[q], NB[:], d_t1, ALU.add).then_inc(step("d_num"), 1)

        def phase(sync, pool, pe, act, dve):
            with ExitStack() as scope:
                phase_scope[0] = scope
                steps.clear()
                with nc.Block() as block:
                    block.sync(sync)
                    block.gpsimd(pool)
                    block.tensor(pe)
                    block.scalar(act)
                    block.vector(dve)
                for s in steps.values():
                    nc.gpsimd.sem_clear(s)
                nc.all_engine_barrier()

        phase(setup_sync, setup_pool, setup_pe, lambda act: act.preload_act_table_set(ACT_SET), setup_dve)
        phase(b_sync, b_pool, b_pe, b_act, b_dve)
        phase(a_sync, a_pool, a_pe, a_act, a_dve)
        phase(c_sync, c_pool, c_pe, c_act, c_dve)
        phase(d_sync, d_pool, d_pe, d_act, d_dve)


_INS = ['x', 'src', 'dst', 'edge_attr_128', 'L0_gnn_W_self0', 'L0_gnn_W_neigh0', 'L0_gnn_b0', 'L0_gnn_W_self1',
        'L0_gnn_W_neigh1', 'L0_gnn_b1', 'L1_gnn_Wq', 'L1_gnn_bq', 'L1_gnn_Wk', 'L1_gnn_bk', 'L1_gnn_Wv', 'L1_gnn_bv',
        'L1_gnn_We', 'L1_gnn_be', 'L1_gnn_Wskip', 'L1_gnn_bskip', 'L1_gnn_ln_g', 'L1_gnn_ln_b', 'L1_gnn_Wlin',
        'L1_gnn_blin']
_OUTS = [((50000, 128), 'float32')]


def kernel(**inputs):
    import numpy as _np
    import concourse.bacc as _bacc
    from concourse import mybir as _mybir
    from concourse.bass_utils import run_bass_kernel_spmd as _run

    nc = _bacc.Bacc("TRN2", target_bir_lowering=False, num_devices=1)
    arrays, args = {}, []
    for name in _INS:
        a = _np.ascontiguousarray(inputs[name])
        arrays[f"in_{name}_dram"] = a
        args.append(nc.dram_tensor(f"in_{name}_dram", a.shape, _mybir.dt.from_np(a.dtype), kind="ExternalInput").ap())
    for i, (shape, dtype) in enumerate(_OUTS):
        dt = _mybir.dt.from_np(_np.dtype(dtype))
        args.append(nc.dram_tensor(f"out_{i}_dram", shape, dt, kind="ExternalOutput").ap())
    gnn_kernel(nc, *args)
    r = _run(nc, [arrays], core_ids=[0])
    return r.results[0]["out_0_dram"]
```

```python
from contextlib import ExitStack

import concourse.bass as bass
from concourse import mybir

P = 128
F32 = mybir.dt.float32
BF16 = mybir.dt.bfloat16
I32 = mybir.dt.int32
U16 = mybir.dt.uint16
NOWHERE = 65535
ALU = mybir.AluOpType
ACT = mybir.ActivationFunctionType
AX = mybir.AxisListType
CREDIT = 4
FAR = 1000000
BIG = 1e30
EPS = 1e-5
ACT_SET = "natural_log_exp_and_others"


def gnn_kernel(nc, x, src, dst, edge_attr, Ws0, Wn0, b0, Ws1, Wn1, b1, Wq, bq, Wk, bk, Wv, bv, We, be,
               Wskip, bskip, ln_g, ln_b, Wlin, blin, out):
    N, D = x.shape
    E = src.shape[0]
    HC = Wq.shape[1]
    H = HC // D
    SCALE = float(D) ** -0.5
    R = 4
    BLK = R * P
    NBLK = -(-N // BLK)
    NT = -(-E // P)
    TAIL = E - (NT - 1) * P
    TILES = 104
    assert TILES >= NT + 3 and TILES >= NBLK + 3 and D == P and H == 4
    SUP = TILES // R
    RED = -(-N // P)
    SLOTS = (SUP - 1) * BLK

    x1_tab = nc.dram_tensor("x1_tab", [N + SLOTS, D], F32).ap()
    h1e_tab = nc.dram_tensor("h1e_tab", [SLOTS, D], F32).ap()
    unused = nc.dram_tensor("unused", [16 * BLK, D], F32).ap()
    redirect = nc.dram_tensor("redirect", [RED * P, 1], I32).ap()

    with ExitStack() as ctx:
        def sb(name, shape, dt=F32):
            return ctx.enter_context(nc.sbuf_tensor(name, shape, dt))

        def bank(name):
            return ctx.enter_context(nc.psum_tensor(name, [P, 512], F32))

        def sem(name):
            return ctx.enter_context(nc.semaphore(name))

        ident = sb("ident", [P, P])
        dst_row = sb("dst_row", [P, TILES * P], U16)
        Ws0_s, Wn0_s, Ws1_s, Wn1_s = (sb(n, [P, D]) for n in ("Ws0_s", "Wn0_s", "Ws1_s", "Wn1_s"))
        Wv_s, We_s, Wskip_s = (sb(n, [P, HC]) for n in ("Wv_s", "We_s", "Wskip_s"))
        Wg_s = sb("Wg_s", [P, H, D])
        MG_s = sb("MG_s", [P, 2 * D])
        Aqk_s = sb("Aqk_s", [P, HC])
        Aqe_s = sb("Aqe_s", [P, HC])
        small_w = sb("small_w", [P, 3 * H])
        vcol = sb("vcol", [P, 32])
        e127 = sb("e127", [P, 1])
        cl = sb("cl", [P, D])
        alpha_c = sb("alpha_c", [P, H])
        gc = sb("gc", [P, 1])
        eps = sb("eps", [P, 1])
        ones3 = sb("ones3", [3, P], BF16)
        bias3 = sb("bias3", [3, 1024], BF16)
        B0, B1, BMG, BOUT = 0, 128, 256, 512
        dst_f = sb("dst_f", [P, TILES + 1])
        idx = sb("idx", [P, 4, TILES], I32)
        SRC, DST, REP, EID = range(4)
        look = sb("look", [P, 3, TILES + 8], I32)
        hf = sb("hf", [P, 2, TILES])
        hidx = sb("hidx", [P, TILES], I32)

        big = sb("big", [P, (2 * TILES + R) * P])
        h1s = big[:, 0:(TILES + R) * P].rearrange("p (t d) -> p t d", d=P)
        ypart = big[:, TILES * P:(2 * TILES + R) * P].rearrange("p (t d) -> p t d", d=P)
        carve_at = [0]

        def carve(n):
            a = carve_at[0]
            carve_at[0] += n
            assert carve_at[0] <= (2 * TILES + R) * P
            return big[:, a:a + n]

        set_q, set_k = carve(HC), carve(HC)
        set_qT, set_kT, set_eT, set_sT = (carve(HC).rearrange("p (h d) -> p h d", h=H) for _ in range(4))
        set_wlin = carve(H * D).rearrange("p (h d) -> p h d", h=H)
        set_sc = carve(HC)
        set_b = carve(1024)
        set_r = carve(1024)
        set_t = carve(HC)
        set_u = carve(HC)
        vrow = carve(P)
        rows_f = carve(4 * P).rearrange("p (a d) -> p a d", a=4)
        rows_i = carve(3 * P).bitcast(I32).rearrange("p (a d) -> p a d", a=3)
        col_s = carve(8)
        hi3, mid3, lo3 = (carve(512).bitcast(BF16) for _ in range(3))
        red_init = carve(RED).bitcast(I32)
        b_ghost = carve_at[0]
        b_x = [carve(BLK) for _ in range(4)]
        b_y = [carve(BLK) for _ in range(2)]
        b_x1 = [carve(BLK) for _ in range(4)]
        b_x1c = [carve(BLK) for _ in range(2)]
        b_w = [carve(BLK) for _ in range(2)]
        b_x1T, b_e, b_r, b_z = (carve(BLK) for _ in range(4))
        b_ghost_end = carve_at[0]
        b_xT, b_h1T = carve(BLK), carve(BLK)
        b_o = [carve(BLK) for _ in range(2)]
        b_junk = carve(BLK)
        b_st = carve(64)
        b_mv1, b_mv2 = carve(8), carve(8)
        b_l1, b_l2, b_l3, b_rs1, b_nm1, b_var, b_rs2, b_rs3, b_nm3 = (carve(4) for _ in range(9))
        b_small_end = carve_at[0]
        carve_at[0] = 0
        d_ea = [carve(D) for _ in range(2)]
        d_x1s = [carve(D) for _ in range(2)]
        d_x1d = [carve(D) for _ in range(4)]
        d_xT = [carve(3 * D) for _ in range(2)]
        d_same = [carve(P) for _ in range(2)]
        d_last = [carve(P) for _ in range(2)]
        d_neg = [carve(P) for _ in range(2)]
        d_carry = [carve(12) for _ in range(2)]
        d_al = [carve(H) for _ in range(2)]
        d_t1, d_vex = carve(HC), carve(HC)
        d_num = [carve(HC) for _ in range(2)]
        d_rden = [carve(H) for _ in range(2)]
        d_o, d_on, d_onT = carve(HC), carve(HC), carve(HC)
        d_junk = carve(BLK)
        d_small = carve(64)
        d_x1c, d_x1k = ([carve(D) for _ in range(4)] for _ in range(2))
        d_z, d_e, d_r, d_w = (carve(D) for _ in range(4))
        d_out = [carve(D) for _ in range(4)]
        d_end = carve_at[0]

        GW = D + 1
        a_xs = [sb(f"a_xs{k}", [P, R, GW]) for k in range(2)]
        a_xd = [sb(f"a_xd{k}", [P, R, D]) for k in range(2)]
        a_same = [sb(f"a_same{k}", [P, R, P]) for k in range(2)]
        a_last = [sb(f"a_last{k}", [P, R, P]) for k in range(2)]
        a_agg = sb("a_agg", [P, R, GW])
        a_mean = sb("a_mean", [P, R, D])
        a_rdeg = sb("a_rdeg", [P, R])
        a_xsT, a_mnT, a_h1dT = (sb(n, [P, BLK]) for n in ("a_xsT", "a_mnT", "a_h1dT"))
        a_y = a_xsT
        a_xdT = [sb(f"a_xdT{k}", [P, BLK]) for k in range(2)]
        a_rows = [sb(f"a_rows{k}", [P, R, D]) for k in range(2)]
        a_st = sb("a_st", [P, 64])
        stage = sb("stage", [P, 4, 16], I32)
        got = sb("got", [P, 4, 2], I32)

        pb = [bank(f"pb{i}") for i in range(8)]

        s_ld = sem("s_ld")
        s_ident = sem("s_ident")
        s_sv = sem("s_sv")
        s_sp = sem("s_sp")
        s_sg = sem("s_sg")

        steps, phase_scope = {}, [None]

        def step(name):
            if name not in steps:
                steps[name] = phase_scope[0].enter_context(nc.semaphore(name))
            return steps[name]

        def after(eng, name, it, ago=0):
            eng.wait_ge(step(name), it + (CREDIT + 1 - ago))

        def wait_apart(eng, s, value):
            eng.wait_ge(s, value)
            eng.sem_inc(s_passed, 1)

        def after_apart(eng, name, it, ago=0):
            wait_apart(eng, step(name), it + (CREDIT + 1 - ago))

        def made(eng, lags, name, it, lag):
            after(eng, name, it, lag - lags[name])

        def freed(eng, lags, name, it, lag, buffers):
            after(eng, name, it, lag + buffers - lags[name])

        def landed(eng, s, n):
            eng.wait_ge(s, n * 16 + 16)

        def credit(eng, names):
            for n in names.split():
                eng.sem_inc(step(n), CREDIT)

        dma_ld = [sem(f"dma_ld{k}") for k in range(4)]
        dma_st = [sem(f"dma_st{k}") for k in range(4)]
        dma_st1 = [sem(f"dma_st1{k}") for k in range(4)]
        dma_p = [sem(f"dma_p{k}") for k in range(4)]
        LOOKUPS_FROM, ROWS_FROM = TILES // 4, 3 * TILES // 4
        s_stage = sem("s_stage")
        dma_a = [sem(f"dma_a{k}") for k in range(2)]
        dma_r = [sem(f"dma_r{k}") for k in range(2)]
        s_stage2 = sem("s_stage2")
        dma_c, dma_cr, dma_ea, dma_xs = ([sem(f"{n}{k}") for k in range(2)] for n in ("dma_c", "dma_cr", "dma_ea", "dma_xs"))
        dma_xd = [sem(f"dma_xd{k}") for k in range(4)]
        s_stage3 = sem("s_stage3")
        s_stage4 = sem("s_stage4")
        s_row = sem("s_row")
        s_passed = sem("s_passed")
        s_red = sem("s_red")
        s_look = sem("s_look")

        LOADS = []

        def setup_sync(sp):
            for q in (dma_st, dma_st1, dma_r, dma_cr):
                for s in q:
                    sp.sem_inc(s, 16)

            def ld(o, i):
                LOADS.append(1)
                sp.dma_start(o, i).then_inc(s_ld, 16)
            for o, i in ((Ws0_s, Ws0), (Wn0_s, Wn0), (Ws1_s, Ws1), (Wn1_s, Wn1), (Wv_s, Wv), (We_s, We),
                         (Wskip_s, Wskip)):
                ld(o[:], i)
            ld(set_q, Wq)
            ld(set_k, Wk)
            ld(set_wlin, Wlin.rearrange("(h p) n -> p h n", p=P))
            sp.wait_ge(s_sg, 1)
            for r, v in ((0, b0), (1, b1), (30, blin)):
                ld(vrow[r:r + 1, :], v.rearrange("(a n) -> a n", a=1))
            for r, v in ((2, bq), (6, bk), (10, bv), (14, be), (18, bskip), (22, ln_g), (26, ln_b)):
                ld(vrow[r:r + 4, :], v.rearrange("(a n) -> a n", n=P))
            full = NT - 1
            ld(rows_i[0:full, 0, :], dst[0:full * P].rearrange("(t p) -> t p", p=P))
            ld(rows_i[full:NT, 0, 0:TAIL], dst[full * P:E].rearrange("(a n) -> a n", a=1))
            ld(rows_i[0:full, 1, :], dst[1:full * P + 1].rearrange("(t p) -> t p", p=P))
            ld(rows_i[full:NT, 1, 0:TAIL - 1], dst[full * P + 1:E].rearrange("(a n) -> a n", a=1))
            ld(rows_i[0:full, 2, :], src[0:full * P].rearrange("(t p) -> t p", p=P))
            ld(rows_i[full:NT, 2, 0:TAIL], src[full * P:E].rearrange("(a n) -> a n", a=1))
            for o, v in ((set_t, bskip), (set_u, bv), (set_r[:, 512:1024], be)):
                ld(o, v.rearrange("(a n) -> a n", a=1).to_broadcast([P, HC]))
            ld(set_b[:, B0:B0 + D], b0.rearrange("(a n) -> a n", a=1).to_broadcast([P, D]))
            ld(set_b[:, B1:B1 + D], b1.rearrange("(a n) -> a n", a=1).to_broadcast([P, D]))
            ld(cl[:], blin.rearrange("(a n) -> a n", a=1).to_broadcast([P, D]))
            sp.wait_ge(s_sg, 4)
            sp.dma_start(redirect.rearrange("(p j) a -> p (j a)", p=P), red_init).then_inc(s_red, 16)

        def setup_pool(g):
            g.memset(vrow, 0.0)
            g.memset(rows_i[:, 0:2, :], NOWHERE)
            g.memset(rows_i[:, 2, :], 0)
            g.memset(dst_row[:, E:TILES * P], NOWHERE).then_inc(s_sg, 1)
            g.dma_start(dst_row[:, 0:E], dst.rearrange("(a n) -> a n", a=1).to_broadcast([P, E]),
                        max_dma_last_dim=1250).then_inc(s_row, 16)
            g.memset(ident[:], 0.0).then_inc(s_sg, 1)
            g.wait_ge(s_sg, 2)
            g.affine_select(out=ident[:], in_=ident[:], compare_op=ALU.not_equal, fill=1.0, base=0,
                            pattern=[[-1, P]], channel_multiplier=1).then_inc(s_sg, 1)
            g.wait_ge(s_sg, 3)
            for k in range(4):
                g.dma_start(unused[14 * BLK + k:14 * BLK + k + 1, 0:P], ident[k:k + 1, :]).then_inc(dma_p[k], 16)
            g.iota(red_init, [[1, RED]], base=0, channel_multiplier=RED).then_inc(s_sg, 1)
            g.iota(idx[:, EID, :], [[P, TILES]], base=N, channel_multiplier=1).then_inc(s_sg, 1)
            g.memset(big[:, b_ghost:b_ghost_end], 0.0)
            g.memset(big[:, b_ghost_end:b_small_end], 0.0)
            g.memset(stage[:], FAR)
            g.memset(dst_f[:, 0:1], -2.0)
            g.memset(got[:], 0)
            g.memset(look[:, 0:2, :], 0)
            g.memset(look[:, 2, :], FAR)
            for k in range(2):
                g.memset(a_xs[k][:], 1.0)
                g.memset(a_xd[k][:], 0.0)
                g.memset(a_xdT[k][:], 0.0)
            g.memset(a_agg[:], 1.0)
            g.memset(a_mean[:], 0.0)
            g.memset(a_mnT[:], 0.0)
            g.memset(eps[:], EPS).then_inc(s_sg, 1)

        NLOADS = 7 + 3 + 3 + 7 + 6 + 3 + 3
        vi = [0]
        pi = [0]

        def vdone(ins):
            vi[0] += 1
            ins.then_inc(s_sv, 1)
            return vi[0]

        def pdone(ins):
            pi[0] += 1
            ins.then_inc(s_sp, 1)
            return pi[0]

        pm = {n: i + 1 for i, n in enumerate(
            ["vcol", "q", "k", "e", "s", "idx", "A", "Be", "G", "M", "m0", "gb", "cl", "small"])}
        vm = {n: i + 1 for i, n in enumerate(
            ["cast", "mean", "sc", "rep1", "vcol", "cen", "wg", "bke", "q", "k", "e", "s", "idx0", "idx1",
             "A", "Be", "G", "M", "m0", "gb", "cl", "small", "bout", "hi", "r1", "mid", "r2", "lo",
             "p0", "p1", "bias"])}

        def setup_pe(pe):
            def w(n):
                pe.wait_ge(s_sv, vm[n])
            pe.wait_ge(s_ld, 16 * NLOADS)
            pe.wait_ge(s_sg, 3)
            pe.transpose(pb[0][:, 0:P], vrow, ident[:]).then_inc(s_sp, 1)
            for b, m in ((1, set_q), (2, set_k), (3, We_s[:])):
                for h in range(H):
                    t = pe.transpose(pb[b][:, h * P:(h + 1) * P], m[:, h * P:(h + 1) * P], ident[:])
                t.then_inc(s_sp, 1)
            w("sc")
            for h in range(H):
                t = pe.transpose(pb[4][:, h * P:(h + 1) * P], set_sc[:, h * P:(h + 1) * P], ident[:])
            t.then_inc(s_sp, 1)
            w("rep1")
            for a in range(3):
                t = pe.transpose(pb[5][:, a * P:(a + 1) * P], rows_f[:, a, :], ident[:])
            t.then_inc(s_sp, 1)
            w("k")
            for h in range(H):
                t = pe.matmul(pb[1][:, h * P:(h + 1) * P], set_qT[:, h, :], set_kT[:, h, :])
            t.then_inc(s_sp, 1)
            w("e")
            for h in range(H):
                t = pe.matmul(pb[2][:, h * P:(h + 1) * P], set_qT[:, h, :], set_eT[:, h, :])
            t.then_inc(s_sp, 1)
            w("s")

            def sum_heads(o, lhs, rhs):
                for h in range(H):
                    t = pe.matmul(o, lhs(h), rhs(h), start=(h == 0), stop=(h == H - 1))
                return t

            sum_heads(pb[3][:, 0:P], lambda h: set_sT[:, h, :], lambda h: set_sT[:, h, :]).then_inc(s_sp, 1)
            sum_heads(pb[4][:, 0:P], lambda h: set_sT[:, h, :], lambda h: Wg_s[:, h, :]).then_inc(s_sp, 1)
            w("Be")

            def col(c):
                return vcol[:, c:c + 1]

            def wide(c):
                return col(c).to_broadcast([P, P])
            sum_heads(pb[0][:, 0:P], lambda h: wide(18 + h), lambda h: Wg_s[:, h, :]).then_inc(s_sp, 1)
            sum_heads(pb[6][:, 0:P], lambda h: wide(18 + h), lambda h: set_sT[:, h, :])
            sum_heads(pb[6][:, P:P + 1], lambda h: wide(18 + h), lambda h: col(18 + h)).then_inc(s_sp, 1)
            sum_heads(pb[7][:, 0:P], lambda h: wide(26 + h), lambda h: set_wlin[:, h, :]).then_inc(s_sp, 1)
            for h in range(H):
                pe.matmul(pb[1][:, h:h + 1], set_qT[:, h, :], col(6 + h))
                pe.matmul(pb[1][:, 4 + h:5 + h], set_kT[:, h, :], col(2 + h))
                pe.matmul(pb[1][:, 8 + h:9 + h], set_eT[:, h, :], col(2 + h))
                t = pe.matmul(pb[1][:, 12 + h:13 + h], wide(2 + h), col(6 + h))
            t.then_inc(s_sp, 1)

        def setup_dve(v):
            count = [0]

            def d(name, ins):
                ins.then_inc(s_sv, 1)
                count[0] += 1
                assert vm[name] == count[0], name

            def w(n):
                v.wait_ge(s_sv, vm[n])

            def p(n):
                v.wait_ge(s_sp, pm[n])
            v.memset(ones3[:], 1.0)
            v.wait_ge(s_ld, 16 * NLOADS)
            v.wait_ge(s_sg, 6)
            d("cast", v.tensor_copy(rows_f[:, 0:3, :], rows_i[:, 0:3, :]))
            v.tensor_reduce(col_s[:, 0:1], Wskip_s[:], AX.X, ALU.add)
            d("mean", v.tensor_reduce(col_s[:, 1:2], set_t, AX.X, ALU.add))
            w("mean")
            v.tensor_scalar(col_s[:, 2:4], col_s[:, 0:2], 1.0 / HC, None, ALU.mult)
            v.drain()
            d("sc", v.tensor_scalar(set_sc, Wskip_s[:], col_s[:, 2:3], None, ALU.subtract))
            w("cast")
            v.tensor_tensor(rows_f[:, 3, :], rows_f[:, 0, :], rows_f[:, 1, :], ALU.is_equal)
            v.drain()
            d("rep1", v.scalar_tensor_tensor(out=rows_f[:, 1, :], in0=rows_f[:, 3, :], scalar=float(FAR),
                                             in1=rows_f[:, 0, :], op0=ALU.mult, op1=ALU.add))
            p("vcol")
            d("vcol", v.tensor_copy(vcol[:], pb[0][:, 0:32]))
            w("vcol")
            v.tensor_copy(col_s[:, 4:8], vcol[:, 18:22])
            v.drain()
            d("cen", v.tensor_scalar(vcol[:, 18:22], col_s[:, 4:8], col_s[:, 3:4], None, ALU.subtract))
            for h in range(H):
                t = v.tensor_scalar(Wg_s[:, h, :], set_wlin[:, h, :], vcol[:, 22 + h:23 + h], None, ALU.mult)
            d("wg", t)
            d("bke", v.tensor_tensor(vcol[:, 6:10], vcol[:, 6:10], vcol[:, 14:18], ALU.add))
            for n, b, o in (("q", 1, set_qT), ("k", 2, set_kT), ("e", 3, set_eT), ("s", 4, set_sT)):
                p(n)
                d(n, v.tensor_copy(o, pb[b][:].rearrange("p (h d) -> p h d", h=H)))
            p("idx")
            v.tensor_scalar(dst_f[:, 1:TILES + 1], pb[5][:, 0:TILES], 0.0, None, ALU.add)
            v.tensor_copy(idx[:, REP, :], pb[5][:, P:P + TILES])
            v.tensor_copy(idx[:, SRC, :], pb[5][:, 2 * P:2 * P + TILES])
            d("idx0", v.tensor_copy(idx[:, DST, :], pb[5][:, 0:TILES]))
            d("idx1", v.tensor_scalar(e127[:], ident[:, P - 1:P], 1.0, None, ALU.mult))
            p("A")
            d("A", v.tensor_copy(Aqk_s[:], pb[1][:]))
            p("Be")
            d("Be", v.tensor_copy(Aqe_s[:], pb[2][:]))
            p("G")
            d("G", v.tensor_scalar(MG_s[:, D:2 * D], pb[3][:, 0:D], 1.0 / HC, None, ALU.mult))
            p("M")
            d("M", v.tensor_copy(MG_s[:, 0:D], pb[4][:, 0:D]))
            p("m0")
            d("m0", v.tensor_copy(set_b[:, BMG:BMG + D], pb[0][:, 0:D]))
            p("gb")
            v.tensor_scalar(gc[:], pb[6][:, P:P + 1], 1.0 / HC, None, ALU.mult)
            d("gb", v.tensor_scalar(set_b[:, BMG + D:BMG + 2 * D], pb[6][:, 0:D], 2.0 / HC, None, ALU.mult))
            p("cl")
            d("cl", v.tensor_tensor(cl[:], pb[7][:, 0:D], cl[:], ALU.add))
            p("small")
            v.tensor_scalar(alpha_c[:], pb[1][:, 12:16], SCALE, None, ALU.mult)
            d("small", v.tensor_copy(small_w[:], pb[1][:, 0:12]))
            v.tensor_tensor(set_t, set_t, set_u, ALU.add)
            v.drain()
            d("bout", v.tensor_tensor(set_b[:, BOUT:BOUT + HC], set_t, set_r[:, 512:1024], ALU.add))
            w("bout")
            d("hi", v.tensor_copy(hi3, set_b))
            w("hi")
            d("r1", v.tensor_tensor(set_r, set_b, hi3, ALU.subtract))
            w("r1")
            d("mid", v.tensor_copy(mid3, set_r))
            w("mid")
            d("r2", v.tensor_tensor(set_b, set_r, mid3, ALU.subtract))
            w("r2")
            d("lo", v.tensor_copy(lo3, set_b))
            w("lo")
            d("p0", v.tensor_scalar(hi3[0:3, :], hi3[0:3, :], ident[0:3, 0:1], None, ALU.mult))
            w("p0")
            d("p1", v.scalar_tensor_tensor(out=mid3[0:3, :], in0=mid3[0:3, :], scalar=ident[0:3, 1:2],
                                           in1=hi3[0:3, :], op0=ALU.mult, op1=ALU.add))
            w("p1")
            d("bias", v.scalar_tensor_tensor(out=bias3[:], in0=lo3[0:3, :], scalar=ident[0:3, 2:3],
                                             in1=mid3[0:3, :], op0=ALU.mult, op1=ALU.add))
            for b in pb:
                v.memset(b[:], 0.0)

        def bias_mm(pe, o, at, n):
            pe.matmul(o, ones3[:], bias3[:, at:at + n], start=True, stop=False)

        PX, PH, PY, PU, PMG = pb[0], pb[1], pb[2], pb[3], ((pb[4], pb[5]), (pb[6], pb[7]))
        last_base = N - BLK

        def base_of(j):
            return min(j * BLK, last_base)

        def rows_of(t, b):
            if isinstance(b, int):
                return t[b:b + BLK, :].rearrange("(p r) d -> p (r d)", r=R)
            return t[bass.ds(b, BLK), :].rearrange("(p r) d -> p (r d)", r=R)

        B_LAG = dict(b_pxT=0, b_xT=0, b_ph=0, b_h1=1, b_py=1, b_y=1, b_s1=1, b_bn1=1, b_l1=2, b_r1=2, b_nm1=2,
                     b_x1=2, b_x1c=2, b_px1T=3, b_x1T=3, b_pmg=3, b_vs=3, b_var=4, b_l2=4, b_r2=4, b_z=4, b_e=4,
                     b_r=5, b_w=5, b_s2=5, b_bn2=5, b_l3=5, b_r3=5, b_nm3=6, b_o=6)
        AHEAD = 2

        def b_sync(sp):
            ghosts = [0]
            out_lag, x1_lag = B_LAG["b_o"], B_LAG["b_x1"]

            def ghost():
                ghosts[0] += 1
                return unused[(ghosts[0] - 1) * BLK:ghosts[0] * BLK, :].rearrange("(p r) d -> p (r d)", r=R)

            def turn(it, u, load, x1_at, out_at, before_x1=None, before_out=None):
                if load is not None:
                    freed(sp, B_LAG, "b_y", it, -AHEAD, 4)
                    sp.dma_start(b_x[(u + AHEAD) % 4], load).then_inc(dma_ld[(u + AHEAD) % 4], 16)
                made(sp, B_LAG, "b_o", it, out_lag)
                if before_out:
                    landed(sp, *before_out)
                sp.dma_start(out_at, b_o[u % 2]).then_inc(dma_st[u], 16)
                made(sp, B_LAG, "b_x1", it, x1_lag)
                if before_x1:
                    landed(sp, *before_x1)
                sp.dma_start(x1_at, b_x1[(u - x1_lag) % 4]).then_inc(dma_st1[u], 16)

            def edge_turn(it):
                def place(t, j):
                    return rows_of(t, base_of(j)) if 0 <= j < NBLK else ghost()
                n = ((it - 1) % 4, (it - 1) // 4 + 1)
                turn(it, it % 4, rows_of(x, base_of(it + AHEAD)) if it + AHEAD < TILES else None,
                     place(x1_tab, it - x1_lag), place(out, it - out_lag),
                     (dma_st1[n[0]], n[1]) if it - x1_lag == NBLK - 1 else None,
                     (dma_st[n[0]], n[1]) if it - out_lag == NBLK - 1 else None)

            for j in range(AHEAD):
                sp.dma_start(b_x[j], rows_of(x, base_of(j))).then_inc(dma_ld[j], 16)
            first = -(-out_lag // 4)
            whole = (NBLK - 1 - AHEAD) // 4
            for it in range(4 * first):
                edge_turn(it)
            with sp.Fori(first, whole) as i:
                for u in range(4):
                    turn(4 * i + u, u, rows_of(x, i * (4 * BLK) + (u + AHEAD) * BLK),
                         rows_of(x1_tab, i * (4 * BLK) + (u - x1_lag) * BLK),
                         rows_of(out, i * (4 * BLK) + (u - out_lag) * BLK))
            for it in range(4 * whole, TILES):
                edge_turn(it)
            for k in range(4):
                landed(sp, dma_st[k], TILES // 4)
                landed(sp, dma_st1[k], TILES // 4)
            sp.wait_ge(s_red, 16)

        def b_pe(pe):
            credit(pe, "b_pxT b_pmg b_ph b_px1T b_py")
            with pe.Fori(0, TILES // 4) as i:
                for u in range(4):
                    it = 4 * i + u
                    pe.wait_ge(dma_ld[u], 16 * i + 16)
                    freed(pe, B_LAG, "b_xT", it, 0, 1)
                    for r in range(R):
                        t = pe.transpose(PX[:, r * P:(r + 1) * P], b_x[u][:, r * D:(r + 1) * D], ident[:])
                    t.then_inc(step("b_pxT"), 1)
                    made(pe, B_LAG, "b_x1", it, 3)
                    freed(pe, B_LAG, "b_x1T", it, 3, 1)
                    for r in range(R):
                        t = pe.transpose(PU[:, r * P:(r + 1) * P], b_x1[(u - 3) % 4][:, r * D:(r + 1) * D], ident[:])
                    t.then_inc(step("b_px1T"), 1)
                    made(pe, B_LAG, "b_h1", it, 1)
                    freed(pe, B_LAG, "b_y", it, 1, 1)
                    for r in range(R):
                        o = PY[:, r * D:(r + 1) * D]
                        bias_mm(pe, o, B1, D)
                        t = pe.matmul(o, b_h1T[:, r * P:(r + 1) * P], Ws1_s[:], start=False, stop=True)
                    t.then_inc(step("b_py"), 1)
                    made(pe, B_LAG, "b_x1T", it, 3)
                    freed(pe, B_LAG, "b_z", it, 3, 2)
                    for r in range(R):
                        o = PMG[(u - 3) % 2][r // 2][:, (r % 2) * 256:(r % 2) * 256 + 256]
                        bias_mm(pe, o, BMG, 2 * D)
                        t = pe.matmul(o, b_x1T[:, r * P:(r + 1) * P], MG_s[:], start=False, stop=True)
                    t.then_inc(step("b_pmg"), 1)
                    made(pe, B_LAG, "b_xT", it, 0)
                    freed(pe, B_LAG, "b_h1", it, 0, 1)
                    pe.matmul(PH[:], Ws0_s[:], b_xT, start=True, stop=True).then_inc(step("b_ph"), 1)

        def mv(t):
            return t.rearrange("p (r s) -> p r s", s=2)

        def b_act(act):
            credit(act, "b_xT b_x1T b_h1 b_x1 b_o b_e b_l1 b_r1 b_l2 b_r2 b_l3 b_r3")
            with act.Fori(0, TILES // 4) as i:
                for u in range(4):
                    it = 4 * i + u
                    made(act, B_LAG, "b_bn1", it, 2)
                    act.activation(b_l1, mv(b_mv1)[:, :, 1], ACT.Ln, bias=eps[:, 0:1]).then_inc(step("b_l1"), 1)
                    made(act, B_LAG, "b_l1", it, 2)
                    act.activation(b_rs1, b_l1, ACT.Exp, scale=-0.5).then_inc(step("b_r1"), 1)
                    made(act, B_LAG, "b_pxT", it, 0)
                    freed(act, B_LAG, "b_ph", it, 0, 1)
                    act.activation(b_xT, PX[:], ACT.Copy).then_inc(step("b_xT"), 1)
                    made(act, B_LAG, "b_ph", it, 1)
                    freed(act, B_LAG, "b_py", it, 1, 1)
                    act.activation(b_h1T, PH[:], ACT.Relu, bias=vcol[:, 0:1]).then_inc(step("b_h1"), 1)
                    made(act, B_LAG, "b_px1T", it, 3)
                    freed(act, B_LAG, "b_pmg", it, 3, 1)
                    act.activation(b_x1T, PU[:], ACT.Copy).then_inc(step("b_x1T"), 1)
                    made(act, B_LAG, "b_var", it, 4)
                    act.activation(b_l2, b_var, ACT.Ln, bias=eps[:, 0:1]).then_inc(step("b_l2"), 1)
                    made(act, B_LAG, "b_l2", it, 4)
                    freed(act, B_LAG, "b_z", it, 4, 1)
                    act.activation(b_rs2, b_l2, ACT.Exp, scale=-0.5).then_inc(step("b_r2"), 1)
                    made(act, B_LAG, "b_nm3", it, 6)
                    landed(act, dma_st[(u - 2) % 4], i + (1 if u >= 2 else 0))
                    for r in range(R):
                        t = act.activation(b_o[u % 2][:, r * D:(r + 1) * D], b_w[u % 2][:, r * D:(r + 1) * D],
                                           ACT.Identity, scale=b_rs3[:, r:r + 1], bias=b_nm3[:, r:r + 1])
                    t.then_inc(step("b_o"), 1)
                    made(act, B_LAG, "b_nm1", it, 2)
                    landed(act, dma_st1[u], i)
                    freed(act, B_LAG, "b_r", it, 2, 4)
                    for r in range(R):
                        t = act.activation(b_x1[(u - 2) % 4][:, r * D:(r + 1) * D], b_y[u % 2][:, r * D:(r + 1) * D],
                                           ACT.Identity, scale=b_rs1[:, r:r + 1], bias=b_nm1[:, r:r + 1])
                    t.then_inc(step("b_x1"), 1)
                    made(act, B_LAG, "b_z", it, 4)
                    freed(act, B_LAG, "b_w", it, 4, 1)
                    act.activation(b_e, b_z, ACT.Exp).then_inc(step("b_e"), 1)
                    made(act, B_LAG, "b_bn2", it, 5)
                    act.activation(b_l3, mv(b_mv2)[:, :, 1], ACT.Ln, bias=eps[:, 0:1]).then_inc(step("b_l3"), 1)
                    made(act, B_LAG, "b_l3", it, 5)
                    act.activation(b_rs3, b_l3, ACT.Exp, scale=-0.5).then_inc(step("b_r3"), 1)

        def b_dve(v):
            credit(v, "b_y b_z b_bn1 b_nm1 b_bn2 b_nm3 b_var b_r b_w b_vs b_s1 b_s2")
            with v.Fori(0, TILES // 4) as i:
                for u in range(4):
                    it = 4 * i + u
                    made(v, B_LAG, "b_z", it, 5)
                    v.scalar_tensor_tensor(out=b_r, in0=b_z, scalar=0.0, in1=b_x1[(u - 5) % 4], op0=ALU.max,
                                           op1=ALU.add).then_inc(step("b_r"), 1)
                    made(v, B_LAG, "b_r3", it, 6)
                    freed(v, B_LAG, "b_o", it, 6, 1)
                    v.scalar_tensor_tensor(out=b_nm3, in0=mv(b_mv2)[:, :, 0], scalar=-1.0, in1=b_rs3,
                                           op0=ALU.mult, op1=ALU.mult).then_inc(step("b_nm3"), 1)
                    made(v, B_LAG, "b_vs", it, 4)
                    v.tensor_scalar(b_var, b_var, 0.0, None, ALU.max).then_inc(step("b_var"), 1)
                    made(v, B_LAG, "b_e", it, 5)
                    made(v, B_LAG, "b_r", it, 5)
                    freed(v, B_LAG, "b_o", it, 5, 2)
                    v.scalar_tensor_tensor(out=b_w[(u - 5) % 2], in0=b_e, scalar=1.0, in1=b_r, op0=ALU.min,
                                           op1=ALU.add).then_inc(step("b_w"), 1)
                    made(v, B_LAG, "b_w", it, 5)
                    for r in range(R):
                        t = v.bn_stats(b_st[:, 6 * r:6 * r + 6], b_w[(u - 5) % 2][:, r * D:(r + 1) * D])
                    t.then_inc(step("b_s2"), 1)
                    made(v, B_LAG, "b_r2", it, 4)
                    made(v, B_LAG, "b_x1c", it, 4)
                    freed(v, B_LAG, "b_e", it, 4, 1)
                    for r in range(R):
                        t = v.scalar_tensor_tensor(out=b_z[:, r * D:(r + 1) * D],
                                                   in0=PMG[u % 2][r // 2][:, (r % 2) * 256:(r % 2) * 256 + 128],
                                                   scalar=b_rs2[:, r:r + 1],
                                                   in1=b_x1c[u % 2][:, r * D:(r + 1) * D],
                                                   op0=ALU.mult, op1=ALU.add)
                    t.then_inc(step("b_z"), 1)
                    made(v, B_LAG, "b_r1", it, 2)
                    freed(v, B_LAG, "b_x1", it, 2, 1)
                    v.scalar_tensor_tensor(out=b_nm1, in0=mv(b_mv1)[:, :, 0], scalar=-1.0, in1=b_rs1,
                                           op0=ALU.mult, op1=ALU.mult).then_inc(step("b_nm1"), 1)
                    made(v, B_LAG, "b_py", it, 1)
                    freed(v, B_LAG, "b_x1", it, 1, 2)
                    v.tensor_tensor(b_y[(u - 1) % 2], PY[:], b_x[(u - 1) % 4], ALU.add).then_inc(step("b_y"), 1)
                    made(v, B_LAG, "b_y", it, 1)
                    for r in range(R):
                        t = v.bn_stats(b_st[:, 24 + 6 * r:30 + 6 * r], b_y[(u - 1) % 2][:, r * D:(r + 1) * D])
                    t.then_inc(step("b_s1"), 1)
                    wait_apart(v, step("b_s2"), it + CREDIT + 1)
                    for r in range(R):
                        t = v.bn_aggr(b_mv2[:, 2 * r:2 * r + 2], b_st[:, 6 * r:6 * r + 6])
                    t.then_inc(step("b_bn2"), 1)
                    wait_apart(v, step("b_s1"), it + CREDIT + 1)
                    for r in range(R):
                        t = v.bn_aggr(b_mv1[:, 2 * r:2 * r + 2], b_st[:, 24 + 6 * r:30 + 6 * r])
                    t.then_inc(step("b_bn1"), 1)
                    made(v, B_LAG, "b_pmg", it, 3)
                    for r in range(R):
                        t = v.tensor_tensor_reduce(b_junk[:, r * D:(r + 1) * D],
                                                   PMG[(u - 3) % 2][r // 2][:, (r % 2) * 256 + 128:(r % 2) * 256 + 256],
                                                   b_x1[(u - 3) % 4][:, r * D:(r + 1) * D], 1.0, gc[:, 0:1],
                                                   ALU.mult, ALU.add, b_var[:, r:r + 1])
                    t.then_inc(step("b_vs"), 1)

        def b_pool(g):
            credit(g, "b_x1c")
            g.tensor_copy(look[:, 2, 4:4 + TILES], idx[:, REP, :])
            g.wait_ge(s_red, 16)

            def x1c(it, u):
                made(g, B_LAG, "b_x1", it, 2)
                freed(g, B_LAG, "b_z", it, 2, 2)
                g.tensor_tensor(b_x1c[u % 2].rearrange("p (r d) -> p r d", r=R),
                                b_x1[(u - 2) % 4].rearrange("p (r d) -> p r d", r=R),
                                cl[:].rearrange("p (a d) -> p a d", a=1).to_broadcast([P, R, D]),
                                ALU.add).then_inc(step("b_x1c"), 1)

            def pair(t, k):
                return t[:, k, 0:2].rearrange("p (a b) -> p a b", b=1)

            with g.Fori(0, TILES // 8) as i:
                for u in range(4):
                    x1c(4 * i + u, u)
                    for a in range(2):
                        k = 2 * (u % 2) + a
                        t = 8 * i + (2 * u + a)
                        landed(g, dma_p[k], 2 * i + u // 2)
                        g.tensor_copy(pair(stage, k), idx[:, REP:EID + 1, bass.ds(t, 1)]).then_inc(s_stage, 1)
                        wait_apart(g, s_stage, t + 1)
                        g.indirect_dma_start(out=redirect, out_offset=bass.IndirectOffsetOnAxis(ap=stage[:, k, 0:1], axis=0),
                                             in_=stage[:, k, 1:2], in_offset=None, bounds_check=N - 1,
                                             oob_is_err=False).then_inc(dma_p[k], 16)
            for k in range(4):
                landed(g, dma_p[k], TILES // 4)


            def lookup(rnd, k):
                t = 4 * rnd + k
                landed(g, dma_p[k], 2 * rnd + LOOKUPS_FROM)
                g.tensor_copy(look[:, 0:2, bass.ds(t, 1)], pair(got, k)).then_inc(s_look, 1)
                g.tensor_copy(pair(stage, k), idx[:, SRC:DST + 1, bass.ds(t, 1)]).then_inc(s_look, 1)
                wait_apart(g, s_look, 2 * t + 2)
                for a in range(2):
                    g.indirect_dma_start(out=got[:, k, a:a + 1], out_offset=None, in_=redirect,
                                         in_offset=bass.IndirectOffsetOnAxis(ap=stage[:, k, a:a + 1], axis=0),
                                         bounds_check=N - 1, oob_is_err=False).then_inc(dma_p[k], 16)

            with g.Fori(TILES // 8, TILES // 4) as i:
                for u in range(4):
                    x1c(4 * i + u, u)
                    for a in range(2):
                        k = 2 * (u % 2) + a
                        rnd = 2 * (i - TILES // 8) + u // 2
                        lookup(rnd, k)
            g.wait_ge(s_row, 16)
            for k in range(4):
                landed(g, dma_p[k], ROWS_FROM)
                g.tensor_copy(look[:, 0:2, TILES + k:TILES + k + 1], pair(got, k)).then_inc(s_look, 1)
            g.wait_ge(s_look, 2 * TILES + 4)
            g.tensor_scalar(hf[:, 0, :], look[:, 0, 4:4 + TILES], float(N), float(FAR), ALU.is_lt,
                            ALU.mult).then_inc(s_look, 1)
            g.tensor_scalar(hf[:, 1, :], look[:, 0, 4:4 + TILES], float(-N), None, ALU.add).then_inc(s_look, 1)
            g.wait_ge(s_look, 2 * TILES + 6)
            g.tensor_tensor(hf[:, 1, :], hf[:, 0, :], hf[:, 1, :], ALU.add).then_inc(s_look, 1)
            g.wait_ge(s_look, 2 * TILES + 7)
            g.tensor_copy(hidx[:], hf[:, 1, :]).then_inc(s_look, 1)
            g.wait_ge(s_look, 2 * TILES + 8)

        def run_matrices(v, ph, i, u, s):
            after(v, ph + "_pc", 4 * s - 5)
            for r in range(R):
                t = 4 * s + r
                row = dst_row[:, bass.ds(t * P, P)]
                v.tensor_scalar(a_same[u][:, r, :], row, dst_f[:, bass.ds(t + 1, 1)], None, ALU.is_equal)
                m = v.tensor_scalar(a_last[u][:, r, :], row, dst_f[:, bass.ds(t, 1)], e127[:, 0:1],
                                    ALU.is_equal, ALU.mult)
            m.then_inc(step(ph + "_mat"), 1)

        def chain(pe, ph, u, s, r):
            o = pb[r % 2][:, 0:GW]
            if r == 0:
                after(pe, ph + "_mat", s)
            after(pe, ph + "_agg", 4 * s + r, 2)
            pe.matmul(o, a_same[u][:, r, :], a_xs[u][:, r, :], start=True, stop=False)
            after(pe, ph + "_agg", 4 * s + r, 1)
            t = pe.matmul(o, a_last[u][:, r, :], a_agg[:, (r - 1) % 4, :], start=False, stop=True)
            t.then_inc(step(ph + "_pc"), 1)

        def chain_act(act, ph, s, r):
            after(act, ph + "_pc", 4 * s + r)
            after(act, ph + "_mean", s, 1)
            act.activation(a_agg[:, r, :], pb[r % 2][:, 0:GW], ACT.Copy).then_inc(step(ph + "_agg"), 1)

        def mean_dve(v, ph, s):
            after(v, ph + "_agg", 4 * s + 3)
            v.tensor_scalar(a_rdeg[:], a_agg[:, :, D], 1.0, None, ALU.max).then_inc(step(ph + "_dg"), 1)
            after(v, ph + "_dg", s)
            v.reciprocal(a_rdeg[:], a_rdeg[:]).then_inc(step(ph + "_rd"), 1)
            after(v, ph + "_rd", s)
            after(v, ph + "_pmT", s)
            v.tensor_tensor(a_mean[:], a_agg[:, :, 0:D],
                            a_rdeg[:].rearrange("p (r a) -> p r a", a=1).to_broadcast([P, R, D]),
                            ALU.mult).then_inc(step(ph + "_mean"), 1)

        TURNS = TILES // R

        def a_pool(g):
            def turn(s, u, i):
                after(g, "a_pc", 4 * s - 5)
                after(g, "a_xdc", s, 2)
                g.tensor_copy(stage[:, 2 * u:2 * u + 2, 0:4], idx[:, SRC:DST + 1, bass.ds(4 * s, 4)]).then_inc(s_stage2, 1)
                wait_apart(g, s_stage2, s + 1)
                for r in range(R):
                    for a, o in ((0, a_xs[u][:, r, 0:D]), (1, a_xd[u][:, r, :])):
                        g.indirect_dma_start(out=o, out_offset=None, in_=x,
                                             in_offset=bass.IndirectOffsetOnAxis(ap=stage[:, 2 * u + a, r:r + 1], axis=0),
                                             bounds_check=N - 1, oob_is_err=False).then_inc(dma_a[u], 16)
            with g.Fori(0, TURNS // 2) as i:
                for u in range(2):
                    turn(2 * i + u, u, i)

        def a_dve(v):
            v.memset(ypart[:, 0:4, :], 0.0)
            v.drain()
            credit(v, "a_mat a_dg a_rd a_mean a_mnT a_rows a_yp a_xdc")
            with v.Fori(0, TURNS // 2) as i:
                for u in range(2):
                    s = 2 * i + u
                    run_matrices(v, "a", i, u, s)
                    after(v, "a_pmT", s)
                    after(v, "a_ph1d", s, 1)
                    v.tensor_copy(a_mnT[:], pb[4][:]).then_inc(step("a_mnT"), 1)
                    after(v, "a_prow", s)
                    landed(v, dma_r[u], i)
                    v.tensor_copy(a_rows[u][:], pb[4][:].rearrange("p (r d) -> p r d", r=R)).then_inc(step("a_rows"), 1)
                    after(v, "a_py", s)
                    after(v, "a_xdc", s, 1)
                    yp = ypart[:, bass.ds(4 * s, 4), :]
                    v.tensor_tensor(yp, pb[7][:].rearrange("p (r d) -> p r d", r=R), yp,
                                    ALU.add).then_inc(step("a_yp"), 1)
                    v.wait_ge(dma_a[u], 2 * R * 16 * (i + 1))
                    v.tensor_copy(ypart[:, bass.ds(4 * s + 4, 4), :], a_xd[u][:]).then_inc(step("a_xdc"), 1)
                    mean_dve(v, "a", s)

        def a_act(act):
            credit(act, "a_xsT a_xdT a_h1s a_h1d a_agg")
            with act.Fori(0, TURNS // 2) as i:
                for u in range(2):
                    s = 2 * i + u
                    chain_act(act, "a", s, 0)
                    after(act, "a_pxs", s)
                    after(act, "a_ph1s", s, 1)
                    act.activation(a_xsT[:], pb[2][:], ACT.Copy).then_inc(step("a_xsT"), 1)
                    chain_act(act, "a", s, 1)
                    after(act, "a_ph1d", s)
                    after(act, "a_py", s, 1)
                    act.activation(a_h1dT[:], pb[6][:], ACT.Relu, bias=vcol[:, 0:1]).then_inc(step("a_h1d"), 1)
                    after(act, "a_pxd", s)
                    act.activation(a_xdT[u][:], pb[3][:], ACT.Copy).then_inc(step("a_xdT"), 1)
                    chain_act(act, "a", s, 2)
                    after(act, "a_ph1s", s)
                    act.activation(h1s[:, bass.ds(4 * s, 4), :], pb[5][:].rearrange("p (r d) -> p r d", r=R),
                                   ACT.Relu).then_inc(step("a_h1s"), 1)
                    chain_act(act, "a", s, 3)

        def a_pe(pe):
            credit(pe, "a_pmT a_pxs a_ph1d a_pxd a_ph1s a_prow a_py a_pc")
            with pe.Fori(0, TURNS // 2) as i:
                for u in range(2):
                    s = 2 * i + u
                    after(pe, "a_mean", s, 1)
                    after(pe, "a_rows", s, 1)
                    for r in range(R):
                        t = pe.transpose(pb[4][:, r * P:(r + 1) * P], a_mean[:, r, :], ident[:])
                    t.then_inc(step("a_pmT"), 1)
                    pe.wait_ge(dma_a[u], 2 * R * 16 * (i + 1))
                    chain(pe, "a", u, s, 0)
                    after(pe, "a_xsT", s, 1)
                    for r in range(R):
                        t = pe.transpose(pb[2][:, r * P:(r + 1) * P], a_xs[u][:, r, 0:D], ident[:])
                    t.then_inc(step("a_pxs"), 1)
                    after(pe, "a_mnT", s)
                    after(pe, "a_xdT", s, 1)
                    after(pe, "a_h1d", s, 1)
                    pe.matmul(pb[6][:], Ws0_s[:], a_xdT[1 - u][:], start=True, stop=False)
                    pe.matmul(pb[6][:], Wn0_s[:], a_mnT[:], start=False, stop=True).then_inc(step("a_ph1d"), 1)
                    chain(pe, "a", u, s, 1)
                    for r in range(R):
                        t = pe.transpose(pb[3][:, r * P:(r + 1) * P], a_xd[u][:, r, :], ident[:])
                    t.then_inc(step("a_pxd"), 1)
                    after(pe, "a_xsT", s)
                    after(pe, "a_h1s", s, 1)
                    for r in range(R):
                        o = pb[5][:, r * D:(r + 1) * D]
                        bias_mm(pe, o, B0, D)
                        t = pe.matmul(o, a_xsT[:, r * P:(r + 1) * P], Ws0_s[:], start=False, stop=True)
                    t.then_inc(step("a_ph1s"), 1)
                    chain(pe, "a", u, s, 2)
                    after(pe, "a_h1d", s)
                    for r in range(R):
                        t = pe.transpose(pb[4][:, r * P:(r + 1) * P], a_h1dT[:, r * P:(r + 1) * P], ident[:])
                    t.then_inc(step("a_prow"), 1)
                    after(pe, "a_yp", s, 1)
                    for r in range(R):
                        o = pb[7][:, r * D:(r + 1) * D]
                        bias_mm(pe, o, B1, D)
                        t = pe.matmul(o, a_h1dT[:, r * P:(r + 1) * P], Ws1_s[:], start=False, stop=True)
                    t.then_inc(step("a_py"), 1)
                    chain(pe, "a", u, s, 3)

        def edge_rows(tab, at):
            return tab[bass.ds(at, BLK), :].rearrange("(r p) d -> p r d", p=P)

        def a_sync(sp):
            after(sp, "a_rows", 0)
            sp.dma_start(unused[12 * BLK:13 * BLK, :].rearrange("(r p) d -> p r d", p=P), a_rows[0][:]).then_inc(dma_r[0], 16)
            after(sp, "a_rows", 1)
            sp.dma_start(edge_rows(h1e_tab, 0), a_rows[1][:]).then_inc(dma_r[1], 16)
            with sp.Fori(1, TURNS // 2) as i:
                for u in range(2):
                    after(sp, "a_rows", 2 * i + u)
                    sp.dma_start(edge_rows(h1e_tab, i * (2 * BLK) + (u - 1) * BLK), a_rows[u][:]).then_inc(dma_r[u], 16)
            for u in range(2):
                landed(sp, dma_r[u], TURNS // 2)

        def c_pool(g):
            with g.Fori(0, TURNS // 2) as i:
                for u in range(2):
                    s = 2 * i + u
                    after(g, "c_fill", s)
                    g.tensor_copy(stage[:, u, 4:8], hidx[:, bass.ds(4 * s, 4)]).then_inc(s_stage3, 1)
                    wait_apart(g, s_stage3, s + 1)
                    for r in range(R):
                        g.indirect_dma_start(out=a_xs[u][:, r, 0:D], out_offset=None, in_=h1e_tab,
                                             in_offset=bass.IndirectOffsetOnAxis(ap=stage[:, u, 4 + r:5 + r], axis=0),
                                             bounds_check=SLOTS - 1, oob_is_err=False).then_inc(dma_c[u], 16)

        def c_dve(v):
            credit(v, "c_mat c_dg c_rd c_mean c_mnT c_y c_st c_bn c_nm")
            with v.Fori(0, TURNS // 2) as i:
                for u in range(2):
                    s = 2 * i + u
                    run_matrices(v, "c", i, u, s)
                    after(v, "c_pmT", s)
                    after(v, "c_py", s, 1)
                    v.tensor_copy(a_mnT[:], pb[4][:]).then_inc(step("c_mnT"), 1)
                    after(v, "c_py", s)
                    after(v, "c_x1", s, 1)
                    v.tensor_tensor(a_y[:].rearrange("p (r d) -> p r d", r=R), pb[7][:].rearrange("p (r d) -> p r d", r=R),
                                    ypart[:, bass.ds(4 * s, 4), :], ALU.add).then_inc(step("c_y"), 1)
                    after(v, "c_y", s)
                    for r in range(R):
                        t = v.bn_stats(a_st[:, 6 * r:6 * r + 6], a_y[:, r * D:(r + 1) * D])
                    t.then_inc(step("c_st"), 1)
                    after_apart(v, "c_st", s)
                    for r in range(R):
                        t = v.bn_aggr(a_st[:, 24 + 2 * r:26 + 2 * r], a_st[:, 6 * r:6 * r + 6])
                    t.then_inc(step("c_bn"), 1)
                    after(v, "c_r", s)
                    v.scalar_tensor_tensor(out=a_st[:, 40:44], in0=mv(a_st[:, 24:32])[:, :, 0], scalar=-1.0,
                                           in1=a_st[:, 36:40], op0=ALU.mult, op1=ALU.mult).then_inc(step("c_nm"), 1)
                    mean_dve(v, "c", s)

        def c_act(act):
            credit(act, "c_fill c_x1 c_l c_r c_agg")

            def fill(s, u):
                after(act, "c_pc", 4 * s - 5)
                act.activation(a_xs[u][:, :, 0:D], h1s[:, bass.ds(4 * s, 4), :], ACT.Copy).then_inc(step("c_fill"), 1)
            act.activation(a_xs[0][:, :, 0:D], h1s[:, 0:4, :], ACT.Copy).then_inc(step("c_fill"), 1)
            with act.Fori(0, TURNS // 2) as i:
                for u in range(2):
                    s = 2 * i + u
                    fill(s + 1, 1 - u)
                    for r in range(3):
                        chain_act(act, "c", s, r)
                    after(act, "c_bn", s)
                    act.activation(a_st[:, 32:36], mv(a_st[:, 24:32])[:, :, 1], ACT.Ln, bias=eps[:, 0:1]).then_inc(step("c_l"), 1)
                    after(act, "c_l", s)
                    act.activation(a_st[:, 36:40], a_st[:, 32:36], ACT.Exp, scale=-0.5).then_inc(step("c_r"), 1)
                    after(act, "c_nm", s)
                    landed(act, dma_cr[u], i)
                    for r in range(R):
                        t = act.activation(a_rows[u][:, r, :], a_y[:, r * D:(r + 1) * D], ACT.Identity,
                                           scale=a_st[:, 36 + r:37 + r], bias=a_st[:, 40 + r:41 + r])
                    t.then_inc(step("c_x1"), 1)
                    chain_act(act, "c", s, 3)

        def c_pe(pe):
            credit(pe, "c_pmT c_py c_pc")
            with pe.Fori(0, TURNS // 2) as i:
                for u in range(2):
                    s = 2 * i + u
                    after(pe, "c_mean", s, 1)
                    after(pe, "c_mnT", s, 1)
                    for r in range(R):
                        t = pe.transpose(pb[4][:, r * P:(r + 1) * P], a_mean[:, r, :], ident[:])
                    t.then_inc(step("c_pmT"), 1)
                    pe.wait_ge(dma_c[u], R * 16 * (i + 1))
                    chain(pe, "c", u, s, 0)
                    after(pe, "c_mnT", s)
                    after(pe, "c_y", s, 1)
                    for r in range(R):
                        t = pe.matmul(pb[7][:, r * D:(r + 1) * D], a_mnT[:, r * P:(r + 1) * P], Wn1_s[:],
                                      start=True, stop=True)
                    t.then_inc(step("c_py"), 1)
                    for r in range(1, 4):
                        chain(pe, "c", u, s, r)

        def c_sync(sp):
            after(sp, "c_x1", 0)
            sp.dma_start(unused[13 * BLK:14 * BLK, :].rearrange("(r p) d -> p r d", p=P), a_rows[0][:]).then_inc(dma_cr[0], 16)
            after(sp, "c_x1", 1)
            sp.dma_start(edge_rows(x1_tab, N), a_rows[1][:]).then_inc(dma_cr[1], 16)
            with sp.Fori(1, TURNS // 2) as i:
                for u in range(2):
                    after(sp, "c_x1", 2 * i + u)
                    sp.dma_start(edge_rows(x1_tab, i * (2 * BLK) + (N + (u - 1) * BLK)), a_rows[u][:]).then_inc(dma_cr[u], 16)
            for u in range(2):
                landed(sp, dma_cr[u], TURNS // 2)

        TB, UB, WB, VB, NB, CB, KB, LB = pb
        LY, LR = 0, 128
        DEN = NB[:, 0:H]
        CAR = CB[:, 0:9]
        D_LAG = dict(d_pT=0, d_xT=0, d_pU=0, d_R=0, d_a1=0, d_al=0, d_mat=0, d_pc=0, d_car=0, d_mc=0, d_d0=0, d_pa=0,
                     d_pC=0, d_max=1, d_dfx=1, d_ex=1, d_g1=1, d_g2=1, d_den=1, d_pK=1, d_pV=1, d_pL=1, d_pN=1,
                     d_vex=1, d_t1=1, d_num=1, d_o=1, d_x1k=1, d_x1c=1, d_st=2, d_bn=2, d_ln=2, d_rs=2, d_nm=2,
                     d_on=2, d_pO=2, d_onT=2, d_pY=3, d_z=3, d_e=4, d_r=4, d_w=4, d_st2=4, d_bn2=4, d_ln2=4,
                     d_rs2=4, d_nm2=4, d_o2=4)
        fx, den, ssum, amx, stt, mvv = (d_small[:, a:b] for a, b in
                                              ((4, 12), (12, 16), (16, 20), (20, 24), (24, 30), (30, 32)))
        lw, rs, nm, st2, mv2, lw2, rs2, nm2, dfx = (d_small[:, a:b] for a, b in
                                                   ((32, 33), (33, 34), (34, 35), (36, 42), (42, 44), (44, 45),
                                                    (45, 46), (46, 47), (48, 56)))
        scr = [sb(f"d_scr{k}", [P, 16]) for k in range(4)]

        def hs(t, h):
            return t[:, h * D:(h + 1) * D]

        def heads(t):
            return t.rearrange("p (h d) -> p h d", h=H)

        def d_sync(sp):
            def load(it, u, b, n=P):
                freed(sp, D_LAG, "d_al", it, 0, 2)
                sp.dma_start(d_ea[u % 2][0:n, :], edge_attr[bass.ds(b, n), :] if not isinstance(b, int)
                             else edge_attr[b:b + n, :]).then_inc(dma_ea[u % 2], 16)
            with sp.Fori(0, (NT - 1) // 2) as i:
                for u in range(2):
                    load(2 * i + u, u, i * (2 * P) + u * P)
            for it in range(2 * ((NT - 1) // 2), TILES):
                if it < NT - 1:
                    load(it, it, it * P)
                elif it == NT - 1:
                    load(it, it, it * P, TAIL)
                else:
                    load(it, it, E - P)

        def d_pool(g):
            credit(g, "d_x1c d_x1k")

            def gather(it, u):
                t, w = it + 1, (u + 1) % 4
                freed(g, D_LAG, "d_a1", it, -1, 2)
                freed(g, D_LAG, "d_x1k", it, -1, 4)
                g.tensor_copy(stage[:, w, 8:10].rearrange("p (a b) -> p a b", b=1),
                              look[:, 0:2, bass.ds(t + 4, 1)]).then_inc(s_stage4, 1)
                wait_apart(g, s_stage4, 2 * t + 1)
                for a, o, q in ((0, d_x1s[w % 2], dma_xs[w % 2]), (1, d_x1d[w], dma_xd[w])):
                    g.indirect_dma_start(out=o, out_offset=None, in_=x1_tab,
                                         in_offset=bass.IndirectOffsetOnAxis(ap=stage[:, w, 8 + a:9 + a], axis=0),
                                         bounds_check=N + SLOTS - 1, oob_is_err=False).then_inc(q, 16)

            gather(-1, -1)
            with g.Fori(0, TILES // 4) as i:
                for u in range(4):
                    it = 4 * i + u
                    g.tensor_copy(stage[:, u, 10:11], look[:, 2, bass.ds(it, 1)]).then_inc(s_stage4, 1)
                    gather(it, u)
                    made(g, D_LAG, "d_pT", it, 1)
                    wait_apart(g, step("d_r"), it - (1 + 4 - D_LAG["d_r"]) + CREDIT + 1)
                    g.tensor_copy(d_x1k[(u - 1) % 4], d_x1d[(u - 1) % 4]).then_inc(step("d_x1k"), 1)
                    g.tensor_tensor(d_x1c[(u - 1) % 4], d_x1d[(u - 1) % 4], cl[:], ALU.add).then_inc(step("d_x1c"), 1)
                    after_apart(g, "d_o2", it)
                    g.indirect_dma_start(out=out, out_offset=bass.IndirectOffsetOnAxis(ap=stage[:, u, 10:11], axis=0),
                                         in_=d_out[u], in_offset=None, bounds_check=N - 1,
                                         oob_is_err=False).then_inc(dma_p[u], 16)
            g.wait_ge(dma_xs[0], 16 * (TILES // 2 + 1))
            g.wait_ge(dma_xd[0], 16 * (TILES // 4 + 1))
            for u in range(4):
                landed(g, dma_p[u], ROWS_FROM + TILES // 4)

        def d_pe(pe):
            credit(pe, "d_pc d_pa d_pC d_pT d_pK d_pO d_pU d_pV d_pL d_pN d_pY")
            def X(b, a):
                return d_xT[b][:, a * D:(a + 1) * D]
            with pe.Fori(0, TILES // 4) as i:
                for u in range(4):
                    it = 4 * i + u
                    k, q = u % 2, (u - 1) % 2
                    pe.wait_ge(dma_ea[k], 16 * (2 * i + (u // 2 + 1)))
                    pe.wait_ge(dma_xs[k], 16 * (2 * i + (u // 2 + 1)))
                    pe.wait_ge(dma_xd[u], 16 * (i + 1))
                    after(pe, "d_onT", it, 1)
                    for a, s_ in ((0, d_x1s[k]), (1, d_x1d[u]), (2, d_ea[k])):
                        t = pe.transpose(TB[:, a * P:(a + 1) * P], s_, ident[:])
                    t.then_inc(step("d_pT"), 1)
                    freed(pe, D_LAG, "d_o", it, 1, 1)
                    bias_mm(pe, KB[:], BOUT, HC)
                    pe.matmul(KB[:], X(q, 1), Wskip_s[:], start=False, stop=True).then_inc(step("d_pK"), 1)
                    made(pe, D_LAG, "d_xT", it, 0)
                    freed(pe, D_LAG, "d_al", it, 0, 1)
                    pe.matmul(UB[:], X(k, 1), Aqk_s[:], start=True, stop=True)
                    pe.matmul(WB[:], X(k, 1), Aqe_s[:], start=True, stop=True)
                    after(pe, "d_z", it, 1)
                    for n, a in enumerate((1, 0, 2)):
                        t = pe.matmul(LB[:, LR:LR + H], X(k, a), small_w[:, n * H:(n + 1) * H],
                                      start=(n == 0), stop=(n == 2))
                    t.then_inc(step("d_pU"), 1)
                    after(pe, "d_max", it)
                    pe.matmul(VB[:], X(q, 0), Wv_s[:], start=True, stop=False)
                    pe.matmul(VB[:], X(q, 2), We_s[:], start=False, stop=True).then_inc(step("d_pV"), 1)
                    made(pe, D_LAG, "d_ex", it, 1)
                    freed(pe, D_LAG, "d_num", it, 1, 1)
                    pe.matmul(DEN, d_same[q], fx[:, 0:H], start=True, stop=True).then_inc(step("d_pL"), 1)
                    made(pe, D_LAG, "d_onT", it, 3)
                    after(pe, "d_R", it)
                    for h in range(H):
                        t = pe.matmul(LB[:, LY:LY + D], hs(d_onT, h), Wg_s[:, h, :], start=(h == 0), stop=(h == H - 1))
                    t.then_inc(step("d_pY"), 1)
                    made(pe, D_LAG, "d_mat", it, 0)
                    made(pe, D_LAG, "d_den", it, 1)
                    after(pe, "d_t1", it)
                    pe.matmul(CAR, d_last[k], d_carry[q][:, 0:9], start=True, stop=True).then_inc(step("d_pc"), 1)
                    made(pe, D_LAG, "d_vex", it, 1)
                    pe.matmul(NB[:], d_same[q], d_vex, start=True, stop=True).then_inc(step("d_pN"), 1)
                    made(pe, D_LAG, "d_on", it, 2)
                    for h in range(H):
                        t = pe.transpose(hs(TB, h), hs(d_on, h), ident[:])
                    t.then_inc(step("d_pO"), 1)
                    made(pe, D_LAG, "d_al", it, 0)
                    for h in range(H):
                        t = pe.transpose(hs(VB, h), d_al[k][:, h:h + 1].to_broadcast([P, P]), ident[:])
                    t.then_inc(step("d_pa"), 1)
                    made(pe, D_LAG, "d_num", it, 1)
                    after(pe, "d_car", it)
                    pe.matmul(CB[:], d_last[k], d_num[q], start=True, stop=True).then_inc(step("d_pC"), 1)

        def d_act(act):
            credit(act, "d_xT d_ln d_rs d_on d_ex d_t1 d_onT d_vex d_e d_ln2 d_rs2 d_o2")
            with act.Fori(0, TILES // 4) as i:
                for u in range(4):
                    it = 4 * i + u
                    k = u % 2
                    made(act, D_LAG, "d_z", it, 4)
                    freed(act, D_LAG, "d_w", it, 4, 1)
                    act.activation(d_e, d_z, ACT.Exp).then_inc(step("d_e"), 1)
                    made(act, D_LAG, "d_pT", it, 0)
                    freed(act, D_LAG, "d_pV", it, 0, 2)
                    act.activation(d_xT[k], TB[:, 0:3 * P], ACT.Copy).then_inc(step("d_xT"), 1)
                    made(act, D_LAG, "d_dfx", it, 1)
                    freed(act, D_LAG, "d_den", it, 1, 1)
                    act.activation(fx, dfx, ACT.Exp).then_inc(step("d_ex"), 1)
                    made(act, D_LAG, "d_pC", it, 1)
                    freed(act, D_LAG, "d_num", it, 1, 1)
                    made(act, D_LAG, "d_ex", it, 1)
                    for h in range(H):
                        t = act.activation(hs(d_t1, h), hs(CB, h), ACT.Copy, scale=fx[:, 4 + h:5 + h])
                    t.then_inc(step("d_t1"), 1)
                    made(act, D_LAG, "d_bn", it, 2)
                    act.activation(lw, mvv[:, 1:2], ACT.Ln, bias=eps[:, 0:1]).then_inc(step("d_ln"), 1)
                    made(act, D_LAG, "d_ln", it, 2)
                    act.activation(rs, lw, ACT.Exp, scale=-0.5).then_inc(step("d_rs"), 1)
                    made(act, D_LAG, "d_bn2", it, 4)
                    act.activation(lw2, mv2[:, 1:2], ACT.Ln, bias=eps[:, 0:1]).then_inc(step("d_ln2"), 1)
                    made(act, D_LAG, "d_ln2", it, 4)
                    act.activation(rs2, lw2, ACT.Exp, scale=-0.5).then_inc(step("d_rs2"), 1)
                    made(act, D_LAG, "d_pV", it, 1)
                    freed(act, D_LAG, "d_pN", it, 1, 1)
                    for h in range(H):
                        t = act.activation(hs(d_vex, h), hs(VB, h), ACT.Copy, scale=fx[:, h:h + 1])
                    t.then_inc(step("d_vex"), 1)
                    made(act, D_LAG, "d_nm", it, 2)
                    freed(act, D_LAG, "d_pO", it, 2, 1)
                    act.activation(d_on, d_o, ACT.Identity, scale=rs, bias=nm).then_inc(step("d_on"), 1)
                    made(act, D_LAG, "d_nm2", it, 4)
                    landed(act, dma_p[u], i + ROWS_FROM)
                    act.activation(d_out[u], d_w, ACT.Identity, scale=rs2, bias=nm2).then_inc(step("d_o2"), 1)
                    made(act, D_LAG, "d_pO", it, 2)
                    freed(act, D_LAG, "d_pY", it, 2, 1)
                    act.activation(d_onT, TB[:], ACT.Copy).then_inc(step("d_onT"), 1)

        def d_dve(v):
            for t in (*d_num, d_o, d_e, d_z, d_r, d_w, d_onT, d_small, *d_xT, *d_last, *d_neg, *d_al, *d_x1c, *d_x1k,
                      *d_x1d[2:], *scr, VB, CB):
                v.memset(t[:], 0.0)
            for t in (*d_carry, *d_rden, *d_same):
                v.memset(t, 1.0)
            v.drain()
            credit(v, "d_al d_r d_z d_den d_num d_o d_car d_max d_R d_bn d_nm d_dfx d_w d_bn2 d_nm2 d_mat d_a1 d_st "
                      "d_st2 d_mc d_d0 d_g1 d_g2")
            with v.Fori(0, TILES // 4) as i:
                for u in range(4):
                    it = 4 * i + u
                    k, q = u % 2, (u - 1) % 2
                    now, old = scr[u], scr[(u - 1) % 4]
                    made(v, D_LAG, "d_pa", it, 1)
                    wait_apart(v, step("d_d0"), it + CREDIT)
                    for h in range(H):
                        t = v.tensor_tensor_reduce(hs(d_junk, h), hs(VB, h), d_neg[q], 1.0, old[:, 10 + h:11 + h],
                                                   ALU.add, ALU.max, d_carry[q][:, h:h + 1])
                    t.then_inc(step("d_max"), 1)
                    made(v, D_LAG, "d_z", it, 4)
                    made(v, D_LAG, "d_x1k", it, 4)
                    v.scalar_tensor_tensor(out=d_r, in0=d_z, scalar=0.0, in1=d_x1k[u], op0=ALU.max,
                                           op1=ALU.add).then_inc(step("d_r"), 1)
                    made(v, D_LAG, "d_max", it, 1)
                    freed(v, D_LAG, "d_ex", it, 1, 1)
                    v.tensor_tensor(dfx[:, 0:4], d_al[q], d_carry[q][:, 0:4], ALU.subtract)
                    v.tensor_tensor(dfx[:, 4:8], old[:, 10:14], d_carry[q][:, 0:4], ALU.subtract).then_inc(step("d_dfx"), 1)
                    made(v, D_LAG, "d_o", it, 2)
                    v.bn_stats(stt, d_o).then_inc(step("d_st"), 1)
                    made(v, D_LAG, "d_e", it, 4)
                    made(v, D_LAG, "d_r", it, 4)
                    freed(v, D_LAG, "d_o2", it, 4, 1)
                    v.scalar_tensor_tensor(out=d_w, in0=d_e, scalar=1.0, in1=d_r, op0=ALU.min,
                                           op1=ALU.add).then_inc(step("d_w"), 1)
                    row = dst_row[:, bass.ds(it * P, P)]
                    mine, prev = dst_f[:, bass.ds(it + 1, 1)], dst_f[:, bass.ds(it, 1)]
                    after(v, "d_pN", it, 1)
                    v.tensor_scalar(d_same[k], row, mine, None, ALU.is_equal)
                    v.tensor_scalar(d_neg[k], row, mine, -BIG, ALU.not_equal, ALU.mult)
                    v.tensor_scalar(d_last[k], row, prev, e127[:, 0:1], ALU.is_equal, ALU.mult).then_inc(step("d_mat"), 1)
                    made(v, D_LAG, "d_w", it, 4)
                    v.bn_stats(st2, d_w).then_inc(step("d_st2"), 1)
                    wait_apart(v, step("d_st2"), it + CREDIT + 1)
                    v.bn_aggr(mv2, st2).then_inc(step("d_bn2"), 1)
                    made(v, D_LAG, "d_pU", it, 0)
                    v.scalar_tensor_tensor(out=ssum, in0=LB[:, LR:LR + H], scalar=SCALE, in1=alpha_c[:],
                                           op0=ALU.mult, op1=ALU.add).then_inc(step("d_R"), 1)
                    wait_apart(v, step("d_st"), it + CREDIT + 1)
                    v.bn_aggr(mvv, stt).then_inc(step("d_bn"), 1)
                    made(v, D_LAG, "d_R", it, 0)
                    for h in range(H):
                        t = v.tensor_tensor_reduce(hs(d_junk, h), hs(UB, h), d_x1s[k], SCALE, ssum[:, h:h + 1],
                                                   ALU.mult, ALU.add, amx[:, h:h + 1])
                    t.then_inc(step("d_a1"), 1)
                    made(v, D_LAG, "d_ex", it, 1)
                    v.tensor_tensor(old[:, 0:4], old[:, 5:9], fx[:, 4:8], ALU.mult).then_inc(step("d_g1"), 1)
                    made(v, D_LAG, "d_rs", it, 2)
                    freed(v, D_LAG, "d_on", it, 2, 1)
                    v.scalar_tensor_tensor(out=nm, in0=mvv[:, 0:1], scalar=-1.0, in1=rs, op0=ALU.mult,
                                           op1=ALU.mult).then_inc(step("d_nm"), 1)
                    made(v, D_LAG, "d_rs2", it, 4)
                    freed(v, D_LAG, "d_o2", it, 4, 1)
                    v.scalar_tensor_tensor(out=nm2, in0=mv2[:, 0:1], scalar=-1.0, in1=rs2, op0=ALU.mult,
                                           op1=ALU.mult).then_inc(step("d_nm2"), 1)
                    made(v, D_LAG, "d_pL", it, 1)
                    made(v, D_LAG, "d_g1", it, 1)
                    v.tensor_tensor(d_carry[q][:, 5:9], DEN, old[:, 0:4], ALU.add).then_inc(step("d_g2"), 1)
                    made(v, D_LAG, "d_g2", it, 1)
                    v.reciprocal(d_rden[q], d_carry[q][:, 5:9]).then_inc(step("d_den"), 1)
                    made(v, D_LAG, "d_pY", it, 3)
                    made(v, D_LAG, "d_x1c", it, 3)
                    freed(v, D_LAG, "d_e", it, 3, 1)
                    v.tensor_tensor(d_z, LB[:, LY:LY + D], d_x1c[(u - 3) % 4], ALU.add).then_inc(step("d_z"), 1)
                    made(v, D_LAG, "d_pc", it, 0)
                    v.tensor_copy(now[:, 0:9], CAR).then_inc(step("d_car"), 1)
                    made(v, D_LAG, "d_a1", it, 0)
                    for h in range(H):
                        t = v.tensor_tensor_reduce(hs(d_junk, h), hs(WB, h), d_ea[k], SCALE, amx[:, h:h + 1],
                                                   ALU.mult, ALU.add, d_al[k][:, h:h + 1])
                    t.then_inc(step("d_al"), 1)
                    made(v, D_LAG, "d_pN", it, 1)
                    made(v, D_LAG, "d_t1", it, 1)
                    v.tensor_tensor(d_num[q], NB[:], d_t1, ALU.add).then_inc(step("d_num"), 1)
                    made(v, D_LAG, "d_car", it, 0)
                    v.tensor_scalar(now[:, 9:10], now[:, 4:5], 1.0, BIG, ALU.subtract, ALU.mult).then_inc(step("d_mc"), 1)
                    made(v, D_LAG, "d_mc", it, 0)
                    v.tensor_scalar(now[:, 10:14], now[:, 0:4], now[:, 9:10], None, ALU.add).then_inc(step("d_d0"), 1)
                    made(v, D_LAG, "d_pK", it, 1)
                    made(v, D_LAG, "d_num", it, 1)
                    freed(v, D_LAG, "d_on", it, 1, 1)
                    for h in range(H):
                        t = v.scalar_tensor_tensor(out=hs(d_o, h), in0=hs(d_num[q], h), scalar=d_rden[q][:, h:h + 1],
                                                   in1=hs(KB, h), op0=ALU.mult, op1=ALU.add)
                    t.then_inc(step("d_o"), 1)

        def phase(sync, pool, pe, act, dve):
            with ExitStack() as scope:
                phase_scope[0] = scope
                steps.clear()
                with nc.Block() as block:
                    block.sync(sync)
                    block.gpsimd(pool)
                    block.tensor(pe)
                    block.scalar(act)
                    block.vector(dve)
                for s in steps.values():
                    nc.gpsimd.sem_clear(s)
                nc.all_engine_barrier()

        phase(setup_sync, setup_pool, setup_pe, lambda act: act.preload_act_table_set(ACT_SET), setup_dve)
        phase(b_sync, b_pool, b_pe, b_act, b_dve)
        phase(a_sync, a_pool, a_pe, a_act, a_dve)
        phase(c_sync, c_pool, c_pe, c_act, c_dve)
        phase(d_sync, d_pool, d_pe, d_act, d_dve)


_INS = ['x', 'src', 'dst', 'edge_attr_128', 'L0_gnn_W_self0', 'L0_gnn_W_neigh0', 'L0_gnn_b0', 'L0_gnn_W_self1',
        'L0_gnn_W_neigh1', 'L0_gnn_b1', 'L1_gnn_Wq', 'L1_gnn_bq', 'L1_gnn_Wk', 'L1_gnn_bk', 'L1_gnn_Wv', 'L1_gnn_bv',
        'L1_gnn_We', 'L1_gnn_be', 'L1_gnn_Wskip', 'L1_gnn_bskip', 'L1_gnn_ln_g', 'L1_gnn_ln_b', 'L1_gnn_Wlin',
        'L1_gnn_blin']
_OUTS = [((50000, 128), 'float32')]


def kernel(**inputs):
    import numpy as _np
    import concourse.bacc as _bacc
    from concourse import mybir as _mybir
    from concourse.bass_utils import run_bass_kernel_spmd as _run

    nc = _bacc.Bacc("TRN2", target_bir_lowering=False, num_devices=1)
    arrays, args = {}, []
    for name in _INS:
        a = _np.ascontiguousarray(inputs[name])
        arrays[f"in_{name}_dram"] = a
        args.append(nc.dram_tensor(f"in_{name}_dram", a.shape, _mybir.dt.from_np(a.dtype), kind="ExternalInput").ap())
    for i, (shape, dtype) in enumerate(_OUTS):
        dt = _mybir.dt.from_np(_np.dtype(dtype))
        args.append(nc.dram_tensor(f"out_{i}_dram", shape, dt, kind="ExternalOutput").ap())
    gnn_kernel(nc, *args)
    r = _run(nc, [arrays], core_ids=[0])
    return r.results[0]["out_0_dram"]
```

```python
from contextlib import ExitStack

import concourse.bass as bass
from concourse import mybir

P = 128
F32 = mybir.dt.float32
BF16 = mybir.dt.bfloat16
I32 = mybir.dt.int32
U16 = mybir.dt.uint16
NOWHERE = 65535
ALU = mybir.AluOpType
ACT = mybir.ActivationFunctionType
AX = mybir.AxisListType
CREDIT = 16
FAR = 1000000
BIG = 1e30
EPS = 1e-5
ACT_SET = "natural_log_exp_and_others"


def gnn_kernel(nc, x, src, dst, edge_attr, Ws0, Wn0, b0, Ws1, Wn1, b1, Wq, bq, Wk, bk, Wv, bv, We, be,
               Wskip, bskip, ln_g, ln_b, Wlin, blin, out):
    N, D = x.shape
    E = src.shape[0]
    HC = Wq.shape[1]
    H = HC // D
    SCALE = float(D) ** -0.5
    R = 4
    BLK = R * P
    NBLK = -(-N // BLK)
    NT = -(-E // P)
    TAIL = E - (NT - 1) * P
    TILES = 104
    assert TILES >= NT + 3 and TILES >= NBLK + 3 and D == P and H == 4
    SUP = TILES // R
    RED = -(-N // P)
    SLOTS = (SUP - 1) * BLK

    x1_tab = nc.dram_tensor("x1_tab", [N + SLOTS, D], F32).ap()
    h1e_tab = nc.dram_tensor("h1e_tab", [SLOTS, D], F32).ap()
    unused = nc.dram_tensor("unused", [17 * BLK, D], F32).ap()
    redirect = nc.dram_tensor("redirect", [RED * P, 1], I32).ap()

    with ExitStack() as ctx:
        def sb(name, shape, dt=F32):
            return ctx.enter_context(nc.sbuf_tensor(name, shape, dt))

        def bank(name):
            return ctx.enter_context(nc.psum_tensor(name, [P, 512], F32))

        def sem(name):
            return ctx.enter_context(nc.semaphore(name))

        ident = sb("ident", [P, P])
        dst_row = sb("dst_row", [P, TILES * P], U16)
        Ws0_s, Wn0_s, Ws1_s, Wn1_s = (sb(n, [P, D]) for n in ("Ws0_s", "Wn0_s", "Ws1_s", "Wn1_s"))
        Wv_s, We_s, Wskip_s = (sb(n, [P, HC]) for n in ("Wv_s", "We_s", "Wskip_s"))
        Wg_s = sb("Wg_s", [P, H, D])
        MG_s = sb("MG_s", [P, 2 * D])
        Aqk_s = sb("Aqk_s", [P, HC])
        Aqe_s = sb("Aqe_s", [P, HC])
        small_w = sb("small_w", [P, 3 * H])
        vcol = sb("vcol", [P, 32])
        e127 = sb("e127", [P, 1])
        cl = sb("cl", [P, D])
        alpha_c = sb("alpha_c", [P, H])
        gc = sb("gc", [P, 1])
        eps = sb("eps", [P, 1])
        ones3 = sb("ones3", [3, P], BF16)
        bias3 = sb("bias3", [3, 1024], BF16)
        B0, B1, BMG, BOUT = 0, 128, 256, 512
        dst_f = sb("dst_f", [P, TILES + 1])
        idx = sb("idx", [P, 4, TILES], I32)
        SRC, DST, REP, EID = range(4)
        look = sb("look", [P, 3, TILES + 8], I32)
        hf = sb("hf", [P, 2, TILES])
        hidx = sb("hidx", [P, TILES], I32)

        big = sb("big", [P, (2 * TILES + 3 * R) * P])
        h1s = big[:, 0:(TILES + R) * P].rearrange("p (t d) -> p t d", d=P)
        ypart = big[:, (TILES + R) * P:(2 * TILES + 3 * R) * P].rearrange("p (t d) -> p t d", d=P)
        carve_at = [0]

        def carve(n):
            a = carve_at[0]
            carve_at[0] += n
            assert carve_at[0] <= (2 * TILES + 3 * R) * P
            return big[:, a:a + n]

        set_q, set_k = carve(HC), carve(HC)
        set_qT, set_kT, set_eT, set_sT = (carve(HC).rearrange("p (h d) -> p h d", h=H) for _ in range(4))
        set_wlin = carve(H * D).rearrange("p (h d) -> p h d", h=H)
        set_sc = carve(HC)
        set_b = carve(1024)
        set_r = carve(1024)
        set_t = carve(HC)
        set_u = carve(HC)
        vrow = carve(P)
        rows_f = carve(4 * P).rearrange("p (a d) -> p a d", a=4)
        rows_i = carve(3 * P).bitcast(I32).rearrange("p (a d) -> p a d", a=3)
        col_s = carve(8)
        hi3, mid3, lo3 = (carve(512).bitcast(BF16) for _ in range(3))
        red_init = carve(RED).bitcast(I32)
        b_ghost = carve_at[0]
        b_x = [carve(BLK) for _ in range(4)]
        b_y = [carve(BLK) for _ in range(2)]
        b_x1 = [carve(BLK) for _ in range(4)]
        b_x1c = [carve(BLK) for _ in range(2)]
        b_w = [carve(BLK) for _ in range(2)]
        b_x1T, b_e, b_r, b_z = (carve(BLK) for _ in range(4))
        b_ghost_end = carve_at[0]
        b_xT, b_h1T = carve(BLK), carve(BLK)
        b_o = [carve(BLK) for _ in range(2)]
        b_junk = carve(BLK)
        b_st = carve(64)
        b_mv1, b_mv2 = carve(8), carve(8)
        b_l1, b_l2, b_l3, b_rs1, b_nm1, b_var, b_rs2, b_rs3, b_nm3 = (carve(4) for _ in range(9))
        b_small_end = carve_at[0]
        carve_at[0] = 0
        d_ea = [carve(D) for _ in range(2)]
        d_x1s = [carve(D) for _ in range(2)]
        d_x1d = [carve(D) for _ in range(4)]
        d_xT = [carve(3 * D) for _ in range(2)]
        d_same = [carve(P) for _ in range(2)]
        d_last = [carve(P) for _ in range(2)]
        d_neg = [carve(P) for _ in range(2)]
        d_carry = [carve(12) for _ in range(2)]
        d_al = [carve(H) for _ in range(2)]
        d_t1, d_vex = carve(HC), carve(HC)
        d_num = [carve(HC) for _ in range(2)]
        d_rden = [carve(H) for _ in range(2)]
        d_o, d_on, d_onT = carve(HC), carve(HC), carve(HC)
        d_junk = carve(BLK)
        d_small = carve(64)
        d_x1c, d_x1k = ([carve(D) for _ in range(4)] for _ in range(2))
        d_z, d_e, d_r, d_w = (carve(D) for _ in range(4))
        d_out = [carve(D) for _ in range(4)]
        d_end = carve_at[0]

        GW = D + 1
        a_xs = [sb(f"a_xs{k}", [P, R, GW]) for k in range(4)]
        a_xd = [sb(f"a_xd{k}", [P, R, D]) for k in range(4)]
        a_same = [sb(f"a_same{k}", [P, R, P]) for k in range(2)]
        a_last = [sb(f"a_last{k}", [P, R, P]) for k in range(2)]
        a_agg = sb("a_agg", [P, 2 * R, GW])
        a_mean = sb("a_mean", [P, R, D])
        a_rdeg = sb("a_rdeg", [P, R])
        a_xsT, a_mnT, a_h1dT = (sb(n, [P, BLK]) for n in ("a_xsT", "a_mnT", "a_h1dT"))
        a_y = a_xsT
        a_xdT = [sb(f"a_xdT{k}", [P, BLK]) for k in range(2)]
        a_rows = [sb(f"a_rows{k}", [P, R, D]) for k in range(2)]
        a_st = sb("a_st", [P, 64])
        stage = sb("stage", [P, 4, 16], I32)
        got = sb("got", [P, 4, 2], I32)

        pb = [bank(f"pb{i}") for i in range(8)]

        s_ld = sem("s_ld")
        s_ident = sem("s_ident")
        s_sv = sem("s_sv")
        s_sp = sem("s_sp")
        s_sg = sem("s_sg")

        steps, phase_scope = {}, [None]

        def step(name):
            if name not in steps:
                steps[name] = phase_scope[0].enter_context(nc.semaphore(name))
            return steps[name]

        def turn_end(it, ago=0):
            return it + (CREDIT + 1 - ago)

        def made(lags, name, it, lag):
            return turn_end(it, lag - lags[name])

        def freed(lags, name, it, lag, buffers):
            return turn_end(it, lag + buffers - lags[name])

        def landed(n):
            return n * 16 + 16

        def wait_apart(eng, s, value):
            eng.wait_ge(s, value)
            eng.sem_inc(s_passed, 1)

        def credit(eng, names):
            for n in names.split():
                eng.sem_inc(step(n), CREDIT)

        dma_ld = [sem(f"dma_ld{k}") for k in range(4)]
        dma_st = [sem(f"dma_st{k}") for k in range(4)]
        dma_st1 = [sem(f"dma_st1{k}") for k in range(4)]
        dma_p = [sem(f"dma_p{k}") for k in range(4)]
        LOOKUPS_FROM, ROWS_FROM = TILES // 4, 3 * TILES // 4
        s_stage = sem("s_stage")
        dma_a = [sem(f"dma_a{k}") for k in range(4)]
        dma_r = [sem(f"dma_r{k}") for k in range(2)]
        s_stage2 = sem("s_stage2")
        dma_c = [sem(f"dma_c{k}") for k in range(4)]
        dma_cr, dma_ea, dma_xs = ([sem(f"{n}{k}") for k in range(2)] for n in ("dma_cr", "dma_ea", "dma_xs"))
        dma_xd = [sem(f"dma_xd{k}") for k in range(4)]
        s_stage3 = sem("s_stage3")
        s_stage4 = sem("s_stage4")
        s_row = sem("s_row")
        s_passed = sem("s_passed")
        s_red = sem("s_red")
        s_look = sem("s_look")

        LOADS = []

        def setup_sync(sp):
            for q in (dma_st, dma_st1, dma_r, dma_cr):
                for s in q:
                    sp.sem_inc(s, 16)

            def ld(o, i):
                LOADS.append(1)
                sp.dma_start(o, i).then_inc(s_ld, 16)
            for o, i in ((Ws0_s, Ws0), (Wn0_s, Wn0), (Ws1_s, Ws1), (Wn1_s, Wn1), (Wv_s, Wv), (We_s, We),
                         (Wskip_s, Wskip)):
                ld(o[:], i)
            ld(set_q, Wq)
            ld(set_k, Wk)
            ld(set_wlin, Wlin.rearrange("(h p) n -> p h n", p=P))
            sp.wait_ge(s_sg, 1)
            for r, v in ((0, b0), (1, b1), (30, blin)):
                ld(vrow[r:r + 1, :], v.rearrange("(a n) -> a n", a=1))
            for r, v in ((2, bq), (6, bk), (10, bv), (14, be), (18, bskip), (22, ln_g), (26, ln_b)):
                ld(vrow[r:r + 4, :], v.rearrange("(a n) -> a n", n=P))
            full = NT - 1
            ld(rows_i[0:full, 0, :], dst[0:full * P].rearrange("(t p) -> t p", p=P))
            ld(rows_i[full:NT, 0, 0:TAIL], dst[full * P:E].rearrange("(a n) -> a n", a=1))
            ld(rows_i[0:full, 1, :], dst[1:full * P + 1].rearrange("(t p) -> t p", p=P))
            ld(rows_i[full:NT, 1, 0:TAIL - 1], dst[full * P + 1:E].rearrange("(a n) -> a n", a=1))
            ld(rows_i[0:full, 2, :], src[0:full * P].rearrange("(t p) -> t p", p=P))
            ld(rows_i[full:NT, 2, 0:TAIL], src[full * P:E].rearrange("(a n) -> a n", a=1))
            for o, v in ((set_t, bskip), (set_u, bv), (set_r[:, 512:1024], be)):
                ld(o, v.rearrange("(a n) -> a n", a=1).to_broadcast([P, HC]))
            ld(set_b[:, B0:B0 + D], b0.rearrange("(a n) -> a n", a=1).to_broadcast([P, D]))
            ld(set_b[:, B1:B1 + D], b1.rearrange("(a n) -> a n", a=1).to_broadcast([P, D]))
            ld(cl[:], blin.rearrange("(a n) -> a n", a=1).to_broadcast([P, D]))
            sp.wait_ge(s_sg, 4)
            sp.dma_start(redirect.rearrange("(p j) a -> p (j a)", p=P), red_init).then_inc(s_red, 16)

        def gather_ends(g, s, u):
            half, at = 2 * (u % 2), 4 + R * (u // 2)
            g.tensor_copy(stage[:, half:half + 2, at:at + R],
                          idx[:, SRC:DST + 1, bass.ds(4 * s, R)]).then_inc(s_stage2, 1)
            g.wait_ge(s_stage2, s + 1)
            g.sem_inc(s_passed, 1)
            for r in range(R):
                for a, o in ((0, a_xs[u][:, r, 0:D]), (1, a_xd[u][:, r, :])):
                    where = stage[:, half + a, at + r:at + r + 1]
                    g.indirect_dma_start(out=o, out_offset=None, in_=x,
                                         in_offset=bass.IndirectOffsetOnAxis(ap=where, axis=0),
                                         bounds_check=N - 1, oob_is_err=False).then_inc(dma_a[u], 16)

        def setup_pool(g):
            g.memset(vrow, 0.0)
            g.memset(rows_i[:, 0:2, :], NOWHERE)
            g.memset(rows_i[:, 2, :], 0)
            g.memset(dst_row[:, E:TILES * P], NOWHERE).then_inc(s_sg, 1)
            g.memset(ident[:], 0.0).then_inc(s_sg, 1)
            g.wait_ge(s_sg, 2)
            g.affine_select(out=ident[:], in_=ident[:], compare_op=ALU.not_equal, fill=1.0, base=0,
                            pattern=[[-1, P]], channel_multiplier=1).then_inc(s_sg, 1)
            g.wait_ge(s_sg, 3)
            for k in range(4):
                g.dma_start(unused[14 * BLK + k:14 * BLK + k + 1, 0:P], ident[k:k + 1, :]).then_inc(dma_p[k], 16)
            g.iota(red_init, [[1, RED]], base=0, channel_multiplier=RED).then_inc(s_sg, 1)
            g.iota(idx[:, EID, :], [[P, TILES]], base=N, channel_multiplier=1).then_inc(s_sg, 1)
            g.memset(stage[:], FAR)
            g.memset(dst_f[:, 0:1], -2.0)
            g.memset(got[:], 0)
            g.memset(look[:, 0:2, :], 0)
            g.memset(look[:, 2, :], FAR)
            for k in range(4):
                g.memset(a_xs[k][:], 1.0)
                g.memset(a_xd[k][:], 0.0)
            for k in range(2):
                g.memset(a_xdT[k][:], 0.0)
            g.memset(a_agg[:], 1.0)
            g.memset(a_mean[:], 0.0)
            g.memset(a_mnT[:], 0.0)
            g.memset(big[:, b_ghost:b_small_end], 0.0)
            g.memset(eps[:], EPS).then_inc(s_sg, 1)
            g.wait_ge(s_sg, 6)
            g.wait_ge(s_sv, vm["idx0"])
            for s in range(2):
                gather_ends(g, s, s)

        NLOADS = 7 + 3 + 3 + 7 + 6 + 3 + 3
        vi = [0]
        pi = [0]

        def vdone(ins):
            vi[0] += 1
            ins.then_inc(s_sv, 1)
            return vi[0]

        def pdone(ins):
            pi[0] += 1
            ins.then_inc(s_sp, 1)
            return pi[0]

        pm = {n: i + 1 for i, n in enumerate(
            ["vcol", "q", "k", "e", "s", "idx", "A", "Be", "G", "M", "m0", "gb", "cl", "small"])}
        vm = {n: i + 1 for i, n in enumerate(
            ["cast", "mean", "sc", "rep1", "vcol", "cen", "wg", "bke", "q", "k", "e", "s", "idx0", "idx1",
             "A", "Be", "G", "M", "m0", "gb", "cl", "small", "bout", "hi", "r1", "mid", "r2", "lo",
             "p0", "p1", "bias"])}

        def setup_pe(pe):
            def w(n):
                pe.wait_ge(s_sv, vm[n])
            pe.wait_ge(s_ld, 16 * NLOADS)
            pe.wait_ge(s_sg, 3)
            pe.transpose(pb[0][:, 0:P], vrow, ident[:]).then_inc(s_sp, 1)
            for b, m in ((1, set_q), (2, set_k), (3, We_s[:])):
                for h in range(H):
                    t = pe.transpose(pb[b][:, h * P:(h + 1) * P], m[:, h * P:(h + 1) * P], ident[:])
                t.then_inc(s_sp, 1)
            w("sc")
            for h in range(H):
                t = pe.transpose(pb[4][:, h * P:(h + 1) * P], set_sc[:, h * P:(h + 1) * P], ident[:])
            t.then_inc(s_sp, 1)
            w("rep1")
            for a in range(3):
                t = pe.transpose(pb[5][:, a * P:(a + 1) * P], rows_f[:, a, :], ident[:])
            t.then_inc(s_sp, 1)
            w("k")
            for h in range(H):
                t = pe.matmul(pb[1][:, h * P:(h + 1) * P], set_qT[:, h, :], set_kT[:, h, :])
            t.then_inc(s_sp, 1)
            w("e")
            for h in range(H):
                t = pe.matmul(pb[2][:, h * P:(h + 1) * P], set_qT[:, h, :], set_eT[:, h, :])
            t.then_inc(s_sp, 1)
            w("s")

            def sum_heads(o, lhs, rhs):
                for h in range(H):
                    t = pe.matmul(o, lhs(h), rhs(h), start=(h == 0), stop=(h == H - 1))
                return t

            sum_heads(pb[3][:, 0:P], lambda h: set_sT[:, h, :], lambda h: set_sT[:, h, :]).then_inc(s_sp, 1)
            sum_heads(pb[4][:, 0:P], lambda h: set_sT[:, h, :], lambda h: Wg_s[:, h, :]).then_inc(s_sp, 1)
            w("Be")

            def col(c):
                return vcol[:, c:c + 1]

            def wide(c):
                return col(c).to_broadcast([P, P])
            sum_heads(pb[0][:, 0:P], lambda h: wide(18 + h), lambda h: Wg_s[:, h, :]).then_inc(s_sp, 1)
            sum_heads(pb[6][:, 0:P], lambda h: wide(18 + h), lambda h: set_sT[:, h, :])
            sum_heads(pb[6][:, P:P + 1], lambda h: wide(18 + h), lambda h: col(18 + h)).then_inc(s_sp, 1)
            sum_heads(pb[7][:, 0:P], lambda h: wide(26 + h), lambda h: set_wlin[:, h, :]).then_inc(s_sp, 1)
            for h in range(H):
                pe.matmul(pb[1][:, h:h + 1], set_qT[:, h, :], col(6 + h))
                pe.matmul(pb[1][:, 4 + h:5 + h], set_kT[:, h, :], col(2 + h))
                pe.matmul(pb[1][:, 8 + h:9 + h], set_eT[:, h, :], col(2 + h))
                t = pe.matmul(pb[1][:, 12 + h:13 + h], wide(2 + h), col(6 + h))
            t.then_inc(s_sp, 1)

        def setup_dve(v):
            count = [0]

            def d(name, ins):
                ins.then_inc(s_sv, 1)
                count[0] += 1
                assert vm[name] == count[0], name

            def w(n):
                v.wait_ge(s_sv, vm[n])

            def p(n):
                v.wait_ge(s_sp, pm[n])
            v.memset(ones3[:], 1.0)
            v.wait_ge(s_ld, 16 * NLOADS)
            v.wait_ge(s_sg, 3)
            d("cast", v.tensor_copy(rows_f[:, 0:3, :], rows_i[:, 0:3, :]))
            v.tensor_reduce(col_s[:, 0:1], Wskip_s[:], AX.X, ALU.add)
            d("mean", v.tensor_reduce(col_s[:, 1:2], set_t, AX.X, ALU.add))
            w("mean")
            v.tensor_scalar(col_s[:, 2:4], col_s[:, 0:2], 1.0 / HC, None, ALU.mult)
            v.drain()
            d("sc", v.tensor_scalar(set_sc, Wskip_s[:], col_s[:, 2:3], None, ALU.subtract))
            w("cast")
            v.tensor_tensor(rows_f[:, 3, :], rows_f[:, 0, :], rows_f[:, 1, :], ALU.is_equal)
            v.drain()
            d("rep1", v.scalar_tensor_tensor(out=rows_f[:, 1, :], in0=rows_f[:, 3, :], scalar=float(FAR),
                                             in1=rows_f[:, 0, :], op0=ALU.mult, op1=ALU.add))
            p("vcol")
            d("vcol", v.tensor_copy(vcol[:], pb[0][:, 0:32]))
            w("vcol")
            v.tensor_copy(col_s[:, 4:8], vcol[:, 18:22])
            v.drain()
            d("cen", v.tensor_scalar(vcol[:, 18:22], col_s[:, 4:8], col_s[:, 3:4], None, ALU.subtract))
            for h in range(H):
                t = v.tensor_scalar(Wg_s[:, h, :], set_wlin[:, h, :], vcol[:, 22 + h:23 + h], None, ALU.mult)
            d("wg", t)
            d("bke", v.tensor_tensor(vcol[:, 6:10], vcol[:, 6:10], vcol[:, 14:18], ALU.add))
            for n, b, o in (("q", 1, set_qT), ("k", 2, set_kT), ("e", 3, set_eT), ("s", 4, set_sT)):
                p(n)
                d(n, v.tensor_copy(o, pb[b][:].rearrange("p (h d) -> p h d", h=H)))
            p("idx")
            v.tensor_scalar(dst_f[:, 1:TILES + 1], pb[5][:, 0:TILES], 0.0, None, ALU.add)
            v.tensor_copy(idx[:, REP, :], pb[5][:, P:P + TILES])
            v.tensor_copy(idx[:, SRC, :], pb[5][:, 2 * P:2 * P + TILES])
            d("idx0", v.tensor_copy(idx[:, DST, :], pb[5][:, 0:TILES]))
            d("idx1", v.tensor_scalar(e127[:], ident[:, P - 1:P], 1.0, None, ALU.mult))
            p("A")
            d("A", v.tensor_copy(Aqk_s[:], pb[1][:]))
            p("Be")
            d("Be", v.tensor_copy(Aqe_s[:], pb[2][:]))
            p("G")
            d("G", v.tensor_scalar(MG_s[:, D:2 * D], pb[3][:, 0:D], 1.0 / HC, None, ALU.mult))
            p("M")
            d("M", v.tensor_copy(MG_s[:, 0:D], pb[4][:, 0:D]))
            p("m0")
            d("m0", v.tensor_copy(set_b[:, BMG:BMG + D], pb[0][:, 0:D]))
            p("gb")
            v.tensor_scalar(gc[:], pb[6][:, P:P + 1], 1.0 / HC, None, ALU.mult)
            d("gb", v.tensor_scalar(set_b[:, BMG + D:BMG + 2 * D], pb[6][:, 0:D], 2.0 / HC, None, ALU.mult))
            p("cl")
            d("cl", v.tensor_tensor(cl[:], pb[7][:, 0:D], cl[:], ALU.add))
            p("small")
            v.tensor_scalar(alpha_c[:], pb[1][:, 12:16], SCALE, None, ALU.mult)
            d("small", v.tensor_copy(small_w[:], pb[1][:, 0:12]))
            v.tensor_tensor(set_t, set_t, set_u, ALU.add)
            v.drain()
            d("bout", v.tensor_tensor(set_b[:, BOUT:BOUT + HC], set_t, set_r[:, 512:1024], ALU.add))
            w("bout")
            d("hi", v.tensor_copy(hi3, set_b))
            w("hi")
            d("r1", v.tensor_tensor(set_r, set_b, hi3, ALU.subtract))
            w("r1")
            d("mid", v.tensor_copy(mid3, set_r))
            w("mid")
            d("r2", v.tensor_tensor(set_b, set_r, mid3, ALU.subtract))
            w("r2")
            d("lo", v.tensor_copy(lo3, set_b))
            w("lo")
            d("p0", v.tensor_scalar(hi3[0:3, :], hi3[0:3, :], ident[0:3, 0:1], None, ALU.mult))
            w("p0")
            d("p1", v.scalar_tensor_tensor(out=mid3[0:3, :], in0=mid3[0:3, :], scalar=ident[0:3, 1:2],
                                           in1=hi3[0:3, :], op0=ALU.mult, op1=ALU.add))
            w("p1")
            d("bias", v.scalar_tensor_tensor(out=bias3[:], in0=lo3[0:3, :], scalar=ident[0:3, 2:3],
                                             in1=mid3[0:3, :], op0=ALU.mult, op1=ALU.add))
            for b in pb[4:]:
                v.memset(b[:], 0.0)

        def bias_mm(pe, o, at, n):
            pe.matmul(o, ones3[:], bias3[:, at:at + n], start=True, stop=False)

        PX, PH, PY, PU, PMG = pb[0], pb[1], pb[2], pb[3], ((pb[4], pb[5]), (pb[6], pb[7]))
        last_base = N - BLK

        def base_of(j):
            return min(j * BLK, last_base)

        def rows_of(t, b):
            if isinstance(b, int):
                return t[b:b + BLK, :].rearrange("(p r) d -> p (r d)", r=R)
            return t[bass.ds(b, BLK), :].rearrange("(p r) d -> p (r d)", r=R)

        B_LAG = dict(b_pxT=0, b_xT=0, b_ph=0, b_h1=1, b_py=1, b_y=1, b_s1=1, b_bn1=1, b_l1=2, b_r1=2, b_nm1=2,
                     b_x1=2, b_x1c=2, b_px1T=3, b_x1T=3, b_pmg=3, b_vs=3, b_var=4, b_l2=4, b_r2=4, b_z=4, b_e=4,
                     b_r=5, b_w=5, b_s2=5, b_bn2=5, b_l3=5, b_r3=5, b_nm3=6, b_o=6)
        AHEAD = 2

        def b_sync(sp):
            ghosts = [0]
            out_lag, x1_lag = B_LAG["b_o"], B_LAG["b_x1"]

            def ghost():
                ghosts[0] += 1
                return unused[(ghosts[0] - 1) * BLK:ghosts[0] * BLK, :].rearrange("(p r) d -> p (r d)", r=R)

            def turn(it, u, load, x1_at, out_at, before_x1=None, before_out=None):
                if load is not None:
                    sp.wait_ge(step("b_y"), freed(B_LAG, "b_y", it, -AHEAD, 4))
                    sp.dma_start(b_x[(u + AHEAD) % 4], load).then_inc(dma_ld[(u + AHEAD) % 4], 16)
                sp.wait_ge(step("b_o"), made(B_LAG, "b_o", it, out_lag))
                if before_out:
                    sp.wait_ge(before_out[0], landed(before_out[1]))
                sp.dma_start(out_at, b_o[u % 2]).then_inc(dma_st[u], 16)
                sp.wait_ge(step("b_x1"), made(B_LAG, "b_x1", it, x1_lag))
                if before_x1:
                    sp.wait_ge(before_x1[0], landed(before_x1[1]))
                sp.dma_start(x1_at, b_x1[(u - x1_lag) % 4]).then_inc(dma_st1[u], 16)

            def edge_turn(it):
                def place(t, j):
                    return rows_of(t, base_of(j)) if 0 <= j < NBLK else ghost()
                n = ((it - 1) % 4, (it - 1) // 4 + 1)
                turn(it, it % 4, rows_of(x, base_of(it + AHEAD)) if it + AHEAD < TILES else None,
                     place(x1_tab, it - x1_lag), place(out, it - out_lag),
                     (dma_st1[n[0]], n[1]) if it - x1_lag == NBLK - 1 else None,
                     (dma_st[n[0]], n[1]) if it - out_lag == NBLK - 1 else None)

            for j in range(AHEAD):
                sp.dma_start(b_x[j], rows_of(x, base_of(j))).then_inc(dma_ld[j], 16)
            first = -(-out_lag // 4)
            whole = (NBLK - 1 - AHEAD) // 4
            for it in range(4 * first):
                edge_turn(it)
            with sp.Fori(first, whole) as i:
                for u in range(4):
                    turn(4 * i + u, u, rows_of(x, i * (4 * BLK) + (u + AHEAD) * BLK),
                         rows_of(x1_tab, i * (4 * BLK) + (u - x1_lag) * BLK),
                         rows_of(out, i * (4 * BLK) + (u - out_lag) * BLK))
            for it in range(4 * whole, TILES):
                edge_turn(it)
            for k in range(4):
                sp.wait_ge(dma_st[k], landed(TILES // 4))
                sp.wait_ge(dma_st1[k], landed(TILES // 4))
            sp.wait_ge(s_red, 16)

        def b_pe(pe):
            credit(pe, "b_pxT b_pmg b_ph b_px1T b_py")
            with pe.Fori(0, TILES // 4) as i:
                for u in range(4):
                    it = 4 * i + u
                    pe.wait_ge(dma_ld[u], 16 * i + 16)
                    pe.wait_ge(step("b_xT"), freed(B_LAG, "b_xT", it, 0, 1))
                    for r in range(R):
                        t = pe.transpose(PX[:, r * P:(r + 1) * P], b_x[u][:, r * D:(r + 1) * D], ident[:])
                    t.then_inc(step("b_pxT"), 1)
                    pe.wait_ge(step("b_x1"), made(B_LAG, "b_x1", it, 3))
                    pe.wait_ge(step("b_x1T"), freed(B_LAG, "b_x1T", it, 3, 1))
                    for r in range(R):
                        t = pe.transpose(PU[:, r * P:(r + 1) * P], b_x1[(u - 3) % 4][:, r * D:(r + 1) * D], ident[:])
                    t.then_inc(step("b_px1T"), 1)
                    pe.wait_ge(step("b_h1"), made(B_LAG, "b_h1", it, 1))
                    pe.wait_ge(step("b_y"), freed(B_LAG, "b_y", it, 1, 1))
                    for r in range(R):
                        o = PY[:, r * D:(r + 1) * D]
                        bias_mm(pe, o, B1, D)
                        t = pe.matmul(o, b_h1T[:, r * P:(r + 1) * P], Ws1_s[:], start=False, stop=True)
                    t.then_inc(step("b_py"), 1)
                    pe.wait_ge(step("b_x1T"), made(B_LAG, "b_x1T", it, 3))
                    pe.wait_ge(step("b_z"), freed(B_LAG, "b_z", it, 3, 2))
                    for r in range(R):
                        o = PMG[(u - 3) % 2][r // 2][:, (r % 2) * 256:(r % 2) * 256 + 256]
                        bias_mm(pe, o, BMG, 2 * D)
                        t = pe.matmul(o, b_x1T[:, r * P:(r + 1) * P], MG_s[:], start=False, stop=True)
                    t.then_inc(step("b_pmg"), 1)
                    pe.wait_ge(step("b_xT"), made(B_LAG, "b_xT", it, 0))
                    pe.wait_ge(step("b_h1"), freed(B_LAG, "b_h1", it, 0, 1))
                    pe.matmul(PH[:], Ws0_s[:], b_xT, start=True, stop=True).then_inc(step("b_ph"), 1)

        def mv(t):
            return t.rearrange("p (r s) -> p r s", s=2)

        def b_act(act):
            credit(act, "b_xT b_x1T b_h1 b_x1 b_o b_e b_l1 b_r1 b_l2 b_r2 b_l3 b_r3")
            with act.Fori(0, TILES // 4) as i:
                for u in range(4):
                    it = 4 * i + u
                    act.wait_ge(step("b_bn1"), made(B_LAG, "b_bn1", it, 2))
                    act.activation(b_l1, mv(b_mv1)[:, :, 1], ACT.Ln, bias=eps[:, 0:1]).then_inc(step("b_l1"), 1)
                    act.wait_ge(step("b_l1"), made(B_LAG, "b_l1", it, 2))
                    act.activation(b_rs1, b_l1, ACT.Exp, scale=-0.5).then_inc(step("b_r1"), 1)
                    act.wait_ge(step("b_pxT"), made(B_LAG, "b_pxT", it, 0))
                    act.wait_ge(step("b_ph"), freed(B_LAG, "b_ph", it, 0, 1))
                    act.activation(b_xT, PX[:], ACT.Copy).then_inc(step("b_xT"), 1)
                    act.wait_ge(step("b_ph"), made(B_LAG, "b_ph", it, 1))
                    act.wait_ge(step("b_py"), freed(B_LAG, "b_py", it, 1, 1))
                    act.activation(b_h1T, PH[:], ACT.Relu, bias=vcol[:, 0:1]).then_inc(step("b_h1"), 1)
                    act.wait_ge(step("b_px1T"), made(B_LAG, "b_px1T", it, 3))
                    act.wait_ge(step("b_pmg"), freed(B_LAG, "b_pmg", it, 3, 1))
                    act.activation(b_x1T, PU[:], ACT.Copy).then_inc(step("b_x1T"), 1)
                    act.wait_ge(step("b_var"), made(B_LAG, "b_var", it, 4))
                    act.activation(b_l2, b_var, ACT.Ln, bias=eps[:, 0:1]).then_inc(step("b_l2"), 1)
                    act.wait_ge(step("b_l2"), made(B_LAG, "b_l2", it, 4))
                    act.wait_ge(step("b_z"), freed(B_LAG, "b_z", it, 4, 1))
                    act.activation(b_rs2, b_l2, ACT.Exp, scale=-0.5).then_inc(step("b_r2"), 1)
                    act.wait_ge(step("b_nm3"), made(B_LAG, "b_nm3", it, 6))
                    act.wait_ge(dma_st[(u - 2) % 4], landed(i + (1 if u >= 2 else 0)))
                    for r in range(R):
                        t = act.activation(b_o[u % 2][:, r * D:(r + 1) * D], b_w[u % 2][:, r * D:(r + 1) * D],
                                           ACT.Identity, scale=b_rs3[:, r:r + 1], bias=b_nm3[:, r:r + 1])
                    t.then_inc(step("b_o"), 1)
                    act.wait_ge(step("b_nm1"), made(B_LAG, "b_nm1", it, 2))
                    act.wait_ge(dma_st1[u], landed(i))
                    act.wait_ge(step("b_r"), freed(B_LAG, "b_r", it, 2, 4))
                    for r in range(R):
                        t = act.activation(b_x1[(u - 2) % 4][:, r * D:(r + 1) * D], b_y[u % 2][:, r * D:(r + 1) * D],
                                           ACT.Identity, scale=b_rs1[:, r:r + 1], bias=b_nm1[:, r:r + 1])
                    t.then_inc(step("b_x1"), 1)
                    act.wait_ge(step("b_z"), made(B_LAG, "b_z", it, 4))
                    act.wait_ge(step("b_w"), freed(B_LAG, "b_w", it, 4, 1))
                    act.activation(b_e, b_z, ACT.Exp).then_inc(step("b_e"), 1)
                    act.wait_ge(step("b_bn2"), made(B_LAG, "b_bn2", it, 5))
                    act.activation(b_l3, mv(b_mv2)[:, :, 1], ACT.Ln, bias=eps[:, 0:1]).then_inc(step("b_l3"), 1)
                    act.wait_ge(step("b_l3"), made(B_LAG, "b_l3", it, 5))
                    act.activation(b_rs3, b_l3, ACT.Exp, scale=-0.5).then_inc(step("b_r3"), 1)

        def b_dve(v):
            credit(v, "b_y b_z b_bn1 b_nm1 b_bn2 b_nm3 b_var b_r b_w b_vs b_s1 b_s2")
            with v.Fori(0, TILES // 4) as i:
                for u in range(4):
                    it = 4 * i + u
                    v.wait_ge(step("b_z"), made(B_LAG, "b_z", it, 5))
                    v.scalar_tensor_tensor(out=b_r, in0=b_z, scalar=0.0, in1=b_x1[(u - 5) % 4], op0=ALU.max,
                                           op1=ALU.add).then_inc(step("b_r"), 1)
                    v.wait_ge(step("b_r3"), made(B_LAG, "b_r3", it, 6))
                    v.wait_ge(step("b_o"), freed(B_LAG, "b_o", it, 6, 1))
                    v.scalar_tensor_tensor(out=b_nm3, in0=mv(b_mv2)[:, :, 0], scalar=-1.0, in1=b_rs3,
                                           op0=ALU.mult, op1=ALU.mult).then_inc(step("b_nm3"), 1)
                    v.wait_ge(step("b_vs"), made(B_LAG, "b_vs", it, 4))
                    v.tensor_scalar(b_var, b_var, 0.0, None, ALU.max).then_inc(step("b_var"), 1)
                    v.wait_ge(step("b_e"), made(B_LAG, "b_e", it, 5))
                    v.wait_ge(step("b_r"), made(B_LAG, "b_r", it, 5))
                    v.wait_ge(step("b_o"), freed(B_LAG, "b_o", it, 5, 2))
                    v.scalar_tensor_tensor(out=b_w[(u - 5) % 2], in0=b_e, scalar=1.0, in1=b_r, op0=ALU.min,
                                           op1=ALU.add).then_inc(step("b_w"), 1)
                    v.wait_ge(step("b_w"), made(B_LAG, "b_w", it, 5))
                    for r in range(R):
                        t = v.bn_stats(b_st[:, 6 * r:6 * r + 6], b_w[(u - 5) % 2][:, r * D:(r + 1) * D])
                    t.then_inc(step("b_s2"), 1)
                    v.wait_ge(step("b_r2"), made(B_LAG, "b_r2", it, 4))
                    v.wait_ge(step("b_x1c"), made(B_LAG, "b_x1c", it, 4))
                    v.wait_ge(step("b_e"), freed(B_LAG, "b_e", it, 4, 1))
                    for r in range(R):
                        t = v.scalar_tensor_tensor(out=b_z[:, r * D:(r + 1) * D],
                                                   in0=PMG[u % 2][r // 2][:, (r % 2) * 256:(r % 2) * 256 + 128],
                                                   scalar=b_rs2[:, r:r + 1],
                                                   in1=b_x1c[u % 2][:, r * D:(r + 1) * D],
                                                   op0=ALU.mult, op1=ALU.add)
                    t.then_inc(step("b_z"), 1)
                    v.wait_ge(step("b_r1"), made(B_LAG, "b_r1", it, 2))
                    v.wait_ge(step("b_x1"), freed(B_LAG, "b_x1", it, 2, 1))
                    v.scalar_tensor_tensor(out=b_nm1, in0=mv(b_mv1)[:, :, 0], scalar=-1.0, in1=b_rs1,
                                           op0=ALU.mult, op1=ALU.mult).then_inc(step("b_nm1"), 1)
                    v.wait_ge(step("b_py"), made(B_LAG, "b_py", it, 1))
                    v.wait_ge(step("b_x1"), freed(B_LAG, "b_x1", it, 1, 2))
                    v.tensor_tensor(b_y[(u - 1) % 2], PY[:], b_x[(u - 1) % 4], ALU.add).then_inc(step("b_y"), 1)
                    v.wait_ge(step("b_y"), made(B_LAG, "b_y", it, 1))
                    for r in range(R):
                        t = v.bn_stats(b_st[:, 24 + 6 * r:30 + 6 * r], b_y[(u - 1) % 2][:, r * D:(r + 1) * D])
                    t.then_inc(step("b_s1"), 1)
                    wait_apart(v, step("b_s2"), it + CREDIT + 1)
                    for r in range(R):
                        t = v.bn_aggr(b_mv2[:, 2 * r:2 * r + 2], b_st[:, 6 * r:6 * r + 6])
                    t.then_inc(step("b_bn2"), 1)
                    wait_apart(v, step("b_s1"), it + CREDIT + 1)
                    for r in range(R):
                        t = v.bn_aggr(b_mv1[:, 2 * r:2 * r + 2], b_st[:, 24 + 6 * r:30 + 6 * r])
                    t.then_inc(step("b_bn1"), 1)
                    v.wait_ge(step("b_pmg"), made(B_LAG, "b_pmg", it, 3))
                    for r in range(R):
                        t = v.tensor_tensor_reduce(b_junk[:, r * D:(r + 1) * D],
                                                   PMG[(u - 3) % 2][r // 2][:, (r % 2) * 256 + 128:(r % 2) * 256 + 256],
                                                   b_x1[(u - 3) % 4][:, r * D:(r + 1) * D], 1.0, gc[:, 0:1],
                                                   ALU.mult, ALU.add, b_var[:, r:r + 1])
                    t.then_inc(step("b_vs"), 1)

        def b_pool(g):
            credit(g, "b_x1c")
            for s in range(2, 4):
                gather_ends(g, s, s)
            g.tensor_copy(look[:, 2, 4:4 + TILES], idx[:, REP, :])
            g.wait_ge(s_red, 16)

            def x1c(it, u):
                g.wait_ge(step("b_x1"), made(B_LAG, "b_x1", it, 2))
                g.wait_ge(step("b_z"), freed(B_LAG, "b_z", it, 2, 2))
                g.tensor_tensor(b_x1c[u % 2].rearrange("p (r d) -> p r d", r=R),
                                b_x1[(u - 2) % 4].rearrange("p (r d) -> p r d", r=R),
                                cl[:].rearrange("p (a d) -> p a d", a=1).to_broadcast([P, R, D]),
                                ALU.add).then_inc(step("b_x1c"), 1)

            def pair(t, k):
                return t[:, k, 0:2].rearrange("p (a b) -> p a b", b=1)

            part = E // (TILES // 8)
            spread = part * (TILES // 8)
            if spread < E:
                g.dma_start(dst_row[:, spread:E], dst[spread:E].rearrange("(a n) -> a n", a=1).to_broadcast([P, E - spread])
                            ).then_inc(s_row, 16)
            with g.Fori(0, TILES // 8) as i:
                g.dma_start(dst_row[:, bass.ds(i * part, part)], dst[bass.ds(i * part, part)].rearrange("(a n) -> a n", a=1)
                            .to_broadcast([P, part])).then_inc(s_row, 16)
                for u in range(4):
                    x1c(4 * i + u, u)
                    for a in range(2):
                        k = 2 * (u % 2) + a
                        t = 8 * i + (2 * u + a)
                        g.wait_ge(dma_p[k], landed(2 * i + u // 2))
                        g.tensor_copy(pair(stage, k), idx[:, REP:EID + 1, bass.ds(t, 1)]).then_inc(s_stage, 1)
                        wait_apart(g, s_stage, t + 1)
                        g.indirect_dma_start(out=redirect, out_offset=bass.IndirectOffsetOnAxis(ap=stage[:, k, 0:1], axis=0),
                                             in_=stage[:, k, 1:2], in_offset=None, bounds_check=N - 1,
                                             oob_is_err=False).then_inc(dma_p[k], 16)
            for k in range(4):
                g.wait_ge(dma_p[k], landed(TILES // 4))


            def lookup(rnd, k):
                t = 4 * rnd + k
                g.wait_ge(dma_p[k], landed(2 * rnd + LOOKUPS_FROM))
                g.tensor_copy(look[:, 0:2, bass.ds(t, 1)], pair(got, k)).then_inc(s_look, 1)
                g.tensor_copy(pair(stage, k), idx[:, SRC:DST + 1, bass.ds(t, 1)]).then_inc(s_look, 1)
                wait_apart(g, s_look, 2 * t + 2)
                for a in range(2):
                    g.indirect_dma_start(out=got[:, k, a:a + 1], out_offset=None, in_=redirect,
                                         in_offset=bass.IndirectOffsetOnAxis(ap=stage[:, k, a:a + 1], axis=0),
                                         bounds_check=N - 1, oob_is_err=False).then_inc(dma_p[k], 16)

            with g.Fori(TILES // 8, TILES // 4) as i:
                for u in range(4):
                    x1c(4 * i + u, u)
                    for a in range(2):
                        k = 2 * (u % 2) + a
                        rnd = 2 * (i - TILES // 8) + u // 2
                        lookup(rnd, k)
            g.wait_ge(s_row, 16 * (TILES // 8 + (1 if spread < E else 0)))
            for k in range(4):
                g.wait_ge(dma_p[k], landed(ROWS_FROM))
                g.tensor_copy(look[:, 0:2, TILES + k:TILES + k + 1], pair(got, k)).then_inc(s_look, 1)
            g.wait_ge(s_look, 2 * TILES + 4)
            g.tensor_scalar(hf[:, 0, :], look[:, 0, 4:4 + TILES], float(N), float(FAR), ALU.is_lt,
                            ALU.mult).then_inc(s_look, 1)
            g.tensor_scalar(hf[:, 1, :], look[:, 0, 4:4 + TILES], float(-N), None, ALU.add).then_inc(s_look, 1)
            g.wait_ge(s_look, 2 * TILES + 6)
            g.tensor_tensor(hf[:, 1, :], hf[:, 0, :], hf[:, 1, :], ALU.add).then_inc(s_look, 1)
            g.wait_ge(s_look, 2 * TILES + 7)
            g.tensor_copy(hidx[:], hf[:, 1, :]).then_inc(s_look, 1)
            g.wait_ge(s_look, 2 * TILES + 8)

        TURNS = TILES // R

        def rounds(eng, turn, tail=None):
            with eng.Fori(0, TURNS // 4) as i:
                for u in range(4):
                    turn(4 * i + u, u, i)
            for s in range(4 * (TURNS // 4), TURNS):
                turn(s, s % 4, s // 4)
            if tail:
                tail(TURNS, TURNS % 4, TURNS // 4)

        def run_matrices(v, ph, s, u):
            v.wait_ge(step(ph + "_pc"), turn_end(4 * s - 5))
            for r in range(R):
                t = 4 * s + r
                row = dst_row[:, bass.ds(t * P, P)]
                v.tensor_scalar(a_same[u % 2][:, r, :], row, dst_f[:, bass.ds(t + 1, 1)], None, ALU.is_equal)
                m = v.tensor_scalar(a_last[u % 2][:, r, :], row, dst_f[:, bass.ds(t, 1)], e127[:, 0:1],
                                    ALU.is_equal, ALU.mult)
            m.then_inc(step(ph + "_mat"), 1)

        def next_matrices(v, ph, s, u):
            if not isinstance(s, int) or s + 1 < TURNS:
                run_matrices(v, ph, s + 1, u + 1)

        def chain(pe, ph, u, s, r):
            o = pb[r % 2][:, 0:GW]
            if r == 0:
                pe.wait_ge(step(ph + "_mat"), turn_end(s))
            pe.wait_ge(step(ph + "_agg"), turn_end(4 * s + r, 2))
            pe.matmul(o, a_same[u % 2][:, r, :], a_xs[u][:, r, :], start=True, stop=False)
            pe.wait_ge(step(ph + "_agg"), turn_end(4 * s + r, 1))
            pe.matmul(o, a_last[u % 2][:, r, :], a_agg[:, (4 * u + r - 1) % (2 * R), :], start=False,
                      stop=True).then_inc(step(ph + "_pc"), 1)

        def chain_act(act, ph, u, s, r):
            act.wait_ge(step(ph + "_pc"), turn_end(4 * s + r))
            act.wait_ge(step(ph + "_mean"), turn_end(s, 1))
            act.activation(a_agg[:, (4 * u + r) % (2 * R), :], pb[r % 2][:, 0:GW],
                           ACT.Copy).then_inc(step(ph + "_agg"), 1)

        def mean_dve(v, ph, u, s):
            at = R * ((u - 1) % 2)
            v.wait_ge(step(ph + "_agg"), turn_end(4 * s - 1))
            v.tensor_scalar(a_rdeg[:], a_agg[:, at:at + R, D], 1.0, None, ALU.max).then_inc(step(ph + "_dg"), 1)
            v.wait_ge(step(ph + "_dg"), turn_end(s))
            v.reciprocal(a_rdeg[:], a_rdeg[:]).then_inc(step(ph + "_rd"), 1)
            v.wait_ge(step(ph + "_rd"), turn_end(s))
            v.wait_ge(step(ph + "_pmT"), turn_end(s, 1))
            v.tensor_tensor(a_mean[:], a_agg[:, at:at + R, 0:D],
                            a_rdeg[:].rearrange("p (r a) -> p r a", a=1).to_broadcast([P, R, D]),
                            ALU.mult).then_inc(step(ph + "_mean"), 1)

        def a_pool(g):
            def turn(s, u):
                g.wait_ge(step("a_pc"), turn_end(4 * s - 13))
                g.wait_ge(step("a_xdc"), turn_end(s, 4))
                gather_ends(g, s, u)
            with g.Fori(1, TURNS // 4) as i:
                for u in range(4):
                    turn(4 * i + u, u)
            for s in range(4 * (TURNS // 4), TURNS):
                turn(s, s % 4)

        def a_dve(v):
            v.memset(ypart[:, 0:2 * R, :], 0.0)
            v.drain()
            credit(v, "a_mat a_dg a_rd a_mean a_mnT a_rows a_yp a_xdc")
            run_matrices(v, "a", 0, 0)

            def ends(s, u, i):
                v.wait_ge(step("a_py"), turn_end(s))
                v.wait_ge(step("a_xdc"), turn_end(s, 2))
                yp = ypart[:, bass.ds(4 * s, 4), :]
                v.tensor_tensor(yp, pb[7][:].rearrange("p (r d) -> p r d", r=R), yp,
                                ALU.add).then_inc(step("a_yp"), 1)
                v.wait_ge(step("a_prow"), turn_end(s))
                v.wait_ge(dma_r[u % 2], landed(2 * i + u // 2))
                v.tensor_copy(a_rows[u % 2][:], pb[4][:].rearrange("p (r d) -> p r d", r=R)).then_inc(step("a_rows"), 1)

            def turn(s, u, i):
                mean_dve(v, "a", u, s)
                next_matrices(v, "a", s, u)
                ends(s, u, i)
                v.wait_ge(dma_a[u], 2 * R * 16 * (i + 1))
                v.tensor_copy(ypart[:, bass.ds(4 * s + 2 * R, 4), :], a_xd[u][:]).then_inc(step("a_xdc"), 1)
                v.wait_ge(step("a_pmT"), turn_end(s))
                v.wait_ge(step("a_ph1d"), turn_end(s, 1))
                v.tensor_copy(a_mnT[:], pb[4][:]).then_inc(step("a_mnT"), 1)
            rounds(v, turn, ends)

        def a_act(act):
            credit(act, "a_xsT a_xdT a_h1s a_h1d a_agg")

            def h1_dst(s):
                act.wait_ge(step("a_ph1d"), turn_end(s, 1))
                act.wait_ge(step("a_prow"), turn_end(s, 1))
                act.activation(a_h1dT[:], pb[6][:], ACT.Relu, bias=vcol[:, 0:1]).then_inc(step("a_h1d"), 1)

            def h1_src(s):
                act.wait_ge(step("a_ph1s"), turn_end(s, 1))
                act.activation(h1s[:, bass.ds(4 * s, 4), :], pb[5][:].rearrange("p (r d) -> p r d", r=R),
                               ACT.Relu).then_inc(step("a_h1s"), 1)

            def turn(s, u, i):
                chain_act(act, "a", u, s, 0)
                h1_dst(s)
                chain_act(act, "a", u, s, 1)
                act.wait_ge(step("a_pxs"), turn_end(s))
                act.wait_ge(step("a_ph1s"), turn_end(s, 1))
                act.activation(a_xsT[:], pb[2][:], ACT.Copy).then_inc(step("a_xsT"), 1)
                chain_act(act, "a", u, s, 2)
                h1_src(s)
                chain_act(act, "a", u, s, 3)
                act.wait_ge(step("a_pxd"), turn_end(s))
                act.wait_ge(step("a_ph1d"), turn_end(s, 1))
                act.activation(a_xdT[u % 2][:], pb[3][:], ACT.Copy).then_inc(step("a_xdT"), 1)

            def tail(s, u, i):
                h1_dst(s)
                h1_src(s)
            rounds(act, turn, tail)

        def a_pe(pe):
            credit(pe, "a_pmT a_pxs a_ph1d a_pxd a_ph1s a_prow a_py a_pc")

            def h1_ws1(s):
                pe.wait_ge(step("a_h1d"), turn_end(s))
                pe.wait_ge(step("a_yp"), turn_end(s, 1))
                for r in range(R):
                    o = pb[7][:, r * D:(r + 1) * D]
                    bias_mm(pe, o, B1, D)
                    t = pe.matmul(o, a_h1dT[:, r * P:(r + 1) * P], Ws1_s[:], start=False, stop=True)
                t.then_inc(step("a_py"), 1)

            def h1_rows(s):
                pe.wait_ge(step("a_mnT"), turn_end(s, 1))
                for r in range(R):
                    t = pe.transpose(pb[4][:, r * P:(r + 1) * P], a_h1dT[:, r * P:(r + 1) * P], ident[:])
                t.then_inc(step("a_prow"), 1)

            def turn(s, u, i):
                pe.wait_ge(dma_a[u], 2 * R * 16 * (i + 1))
                chain(pe, "a", u, s, 0)
                pe.wait_ge(step("a_xsT"), turn_end(s, 1))
                for r in range(R):
                    t = pe.transpose(pb[2][:, r * P:(r + 1) * P], a_xs[u][:, r, 0:D], ident[:])
                t.then_inc(step("a_pxs"), 1)
                chain(pe, "a", u, s, 1)
                h1_ws1(s)
                chain(pe, "a", u, s, 2)
                h1_rows(s)
                pe.wait_ge(step("a_xdT"), turn_end(s, 1))
                for r in range(R):
                    t = pe.transpose(pb[3][:, r * P:(r + 1) * P], a_xd[u][:, r, :], ident[:])
                t.then_inc(step("a_pxd"), 1)
                chain(pe, "a", u, s, 3)
                pe.wait_ge(step("a_mean"), turn_end(s))
                pe.wait_ge(step("a_rows"), turn_end(s))
                for r in range(R):
                    t = pe.transpose(pb[4][:, r * P:(r + 1) * P], a_mean[:, r, :], ident[:])
                t.then_inc(step("a_pmT"), 1)
                pe.wait_ge(step("a_xsT"), turn_end(s))
                pe.wait_ge(step("a_h1s"), turn_end(s))
                for r in range(R):
                    o = pb[5][:, r * D:(r + 1) * D]
                    bias_mm(pe, o, B0, D)
                    t = pe.matmul(o, a_xsT[:, r * P:(r + 1) * P], Ws0_s[:], start=False, stop=True)
                t.then_inc(step("a_ph1s"), 1)
                pe.wait_ge(step("a_mnT"), turn_end(s))
                pe.wait_ge(step("a_xdT"), turn_end(s, 1))
                pe.wait_ge(step("a_h1d"), turn_end(s))
                pe.matmul(pb[6][:], Ws0_s[:], a_xdT[(u - 1) % 2][:], start=True, stop=False)
                pe.matmul(pb[6][:], Wn0_s[:], a_mnT[:], start=False, stop=True).then_inc(step("a_ph1d"), 1)

            def tail(s, u, i):
                h1_ws1(s)
                h1_rows(s)
            rounds(pe, turn, tail)

        def edge_rows(tab, at):
            rows = tab[at:at + BLK, :] if isinstance(at, int) else tab[bass.ds(at, BLK), :]
            return rows.rearrange("(r p) d -> p r d", p=P)

        def store_rows(sp, name, queues, tab, base, ghost):
            def put(s, u, to):
                sp.wait_ge(step(name), turn_end(s))
                sp.dma_start(to, a_rows[u][:]).then_inc(queues[u], 16)
            for s in range(2):
                put(s, s, edge_rows(unused, (ghost + s) * BLK))
            with sp.Fori(1, TURNS // 2) as i:
                for u in range(2):
                    put(2 * i + u, u, edge_rows(tab, i * (2 * BLK) + (base + (u - 2) * BLK)))
            put(TURNS, 0, edge_rows(tab, base + (TURNS - 2) * BLK))
            for u in range(2):
                sp.wait_ge(queues[u], landed(TURNS // 2 + 1 - u))

        def a_sync(sp):
            store_rows(sp, "a_rows", dma_r, h1e_tab, 0, 12)

        def c_pool(g):
            def turn(s, u, i):
                g.wait_ge(step("c_fill"), turn_end(s))
                g.tensor_copy(stage[:, u, 12:16], hidx[:, bass.ds(4 * s, 4)]).then_inc(s_stage3, 1)
                wait_apart(g, s_stage3, s + 1)
                for r in range(R):
                    g.indirect_dma_start(out=a_xs[u][:, r, 0:D], out_offset=None, in_=h1e_tab,
                                         in_offset=bass.IndirectOffsetOnAxis(ap=stage[:, u, 12 + r:13 + r], axis=0),
                                         bounds_check=SLOTS - 1, oob_is_err=False).then_inc(dma_c[u], 16)
            rounds(g, turn)

        def c_dve(v):
            credit(v, "c_mat c_dg c_rd c_mean c_mnT c_y c_st c_bn c_nm")
            run_matrices(v, "c", 0, 0)

            def y_stats(s):
                v.wait_ge(step("c_py"), turn_end(s, 1))
                v.wait_ge(step("c_x1"), turn_end(s, 1))
                v.tensor_tensor(a_y[:].rearrange("p (r d) -> p r d", r=R), pb[7][:].rearrange("p (r d) -> p r d", r=R),
                                ypart[:, bass.ds(4 * s, 4), :], ALU.add).then_inc(step("c_y"), 1)
                v.wait_ge(step("c_y"), turn_end(s))
                for r in range(R):
                    t = v.bn_stats(a_st[:, 6 * r:6 * r + 6], a_y[:, r * D:(r + 1) * D])
                t.then_inc(step("c_st"), 1)

            def moments(s):
                wait_apart(v, step("c_st"), turn_end(s))
                for r in range(R):
                    t = v.bn_aggr(a_st[:, 24 + 2 * r:26 + 2 * r], a_st[:, 6 * r:6 * r + 6])
                t.then_inc(step("c_bn"), 1)

            def minus_mean(s):
                v.wait_ge(step("c_r"), turn_end(s))
                v.scalar_tensor_tensor(out=a_st[:, 40:44], in0=mv(a_st[:, 24:32])[:, :, 0], scalar=-1.0,
                                       in1=a_st[:, 36:40], op0=ALU.mult, op1=ALU.mult).then_inc(step("c_nm"), 1)

            def turn(s, u, i):
                mean_dve(v, "c", u, s)
                y_stats(s)
                next_matrices(v, "c", s, u)
                moments(s)
                v.wait_ge(step("c_pmT"), turn_end(s))
                v.wait_ge(step("c_py"), turn_end(s, 1))
                v.tensor_copy(a_mnT[:], pb[4][:]).then_inc(step("c_mnT"), 1)
                minus_mean(s)

            def tail(s, u, i):
                y_stats(s)
                moments(s)
                minus_mean(s)
            rounds(v, turn, tail)

        def c_act(act):
            credit(act, "c_fill c_x1 c_l c_r c_agg")
            for s in range(2):
                act.activation(a_xs[s][:, :, 0:D], h1s[:, 4 * s + R:4 * s + 2 * R, :], ACT.Copy).then_inc(step("c_fill"), 1)

            def norm(s, u, i):
                act.wait_ge(step("c_bn"), turn_end(s))
                act.activation(a_st[:, 32:36], mv(a_st[:, 24:32])[:, :, 1], ACT.Ln, bias=eps[:, 0:1]).then_inc(step("c_l"), 1)
                act.wait_ge(step("c_l"), turn_end(s))
                act.activation(a_st[:, 36:40], a_st[:, 32:36], ACT.Exp, scale=-0.5).then_inc(step("c_r"), 1)
                act.wait_ge(step("c_nm"), turn_end(s))
                act.wait_ge(dma_cr[u % 2], landed(2 * i + u // 2))
                for r in range(R):
                    t = act.activation(a_rows[u % 2][:, r, :], a_y[:, r * D:(r + 1) * D], ACT.Identity,
                                       scale=a_st[:, 36 + r:37 + r], bias=a_st[:, 40 + r:41 + r])
                t.then_inc(step("c_x1"), 1)

            def turn(s, u, i):
                chain_act(act, "c", u, s, 0)
                if not isinstance(s, int):
                    act.wait_ge(step("c_pc"), turn_end(4 * s - 5))
                    act.activation(a_xs[(u + 2) % 4][:, :, 0:D], h1s[:, bass.ds(4 * s + 3 * R, 4), :],
                                   ACT.Copy).then_inc(step("c_fill"), 1)
                for r in range(1, R):
                    chain_act(act, "c", u, s, r)
                norm(s, u, i)
            rounds(act, turn, norm)

        def c_pe(pe):
            credit(pe, "c_pmT c_py c_pc")

            def turn(s, u, i):
                pe.wait_ge(dma_c[u], R * 16 * (i + 1))
                chain(pe, "c", u, s, 0)
                chain(pe, "c", u, s, 1)
                pe.wait_ge(step("c_mean"), turn_end(s))
                pe.wait_ge(step("c_mnT"), turn_end(s, 1))
                for r in range(R):
                    t = pe.transpose(pb[4][:, r * P:(r + 1) * P], a_mean[:, r, :], ident[:])
                t.then_inc(step("c_pmT"), 1)
                chain(pe, "c", u, s, 2)
                chain(pe, "c", u, s, 3)
                pe.wait_ge(step("c_mnT"), turn_end(s))
                pe.wait_ge(step("c_y"), turn_end(s))
                for r in range(R):
                    t = pe.matmul(pb[7][:, r * D:(r + 1) * D], a_mnT[:, r * P:(r + 1) * P], Wn1_s[:],
                                  start=True, stop=True)
                t.then_inc(step("c_py"), 1)
            rounds(pe, turn)

        def c_sync(sp):
            store_rows(sp, "c_x1", dma_cr, x1_tab, N, 15)

        TB, UB, WB, VB, NB, CB, KB, LB = pb
        LY, LR = 0, 128
        DEN = NB[:, 0:H]
        CAR = CB[:, 0:9]
        D_LAG = dict(d_pT=0, d_xT=0, d_pU=0, d_R=0, d_a1=0, d_al=0, d_mat=0, d_pc=0, d_car=0, d_mc=0, d_d0=0, d_pa=0,
                     d_pC=0, d_max=1, d_dfx=1, d_ex=1, d_g1=1, d_g2=1, d_den=1, d_pK=1, d_pV=1, d_pL=1, d_pN=1,
                     d_vex=1, d_t1=1, d_num=1, d_o=1, d_x1k=1, d_x1c=1, d_st=2, d_bn=2, d_ln=2, d_rs=2, d_nm=2,
                     d_on=2, d_pO=2, d_onT=2, d_pY=3, d_z=3, d_e=4, d_r=4, d_w=4, d_st2=4, d_bn2=4, d_ln2=4,
                     d_rs2=4, d_nm2=4, d_o2=4)
        fx, den, ssum, amx, stt, mvv = (d_small[:, a:b] for a, b in
                                              ((4, 12), (12, 16), (16, 20), (20, 24), (24, 30), (30, 32)))
        lw, rs, nm, st2, mv2, lw2, rs2, nm2, dfx = (d_small[:, a:b] for a, b in
                                                   ((32, 33), (33, 34), (34, 35), (36, 42), (42, 44), (44, 45),
                                                    (45, 46), (46, 47), (48, 56)))
        scr = [sb(f"d_scr{k}", [P, 16]) for k in range(4)]

        def hs(t, h):
            return t[:, h * D:(h + 1) * D]

        def heads(t):
            return t.rearrange("p (h d) -> p h d", h=H)

        D_TURNS = NT + max(D_LAG.values())

        def rounds_of_tiles(eng, turn):
            with eng.Fori(0, D_TURNS // 4) as i:
                for u in range(4):
                    turn(4 * i + u, u, i)
            for it in range(4 * (D_TURNS // 4), D_TURNS):
                turn(it, it % 4, it // 4)

        def d_sync(sp):
            def load(it, u, b, n=P):
                sp.wait_ge(step("d_al"), freed(D_LAG, "d_al", it, 0, 2))
                sp.dma_start(d_ea[u % 2][0:n, :], edge_attr[bass.ds(b, n), :] if not isinstance(b, int)
                             else edge_attr[b:b + n, :]).then_inc(dma_ea[u % 2], 16)
            with sp.Fori(0, (NT - 1) // 2) as i:
                for u in range(2):
                    load(2 * i + u, u, i * (2 * P) + u * P)
            for it in range(2 * ((NT - 1) // 2), D_TURNS):
                if it < NT - 1:
                    load(it, it, it * P)
                elif it == NT - 1:
                    load(it, it, it * P, TAIL)
                else:
                    load(it, it, E - P)

        def d_pool(g):
            credit(g, "d_x1c d_x1k")

            def gather(it, u):
                t, w = it + 1, (u + 1) % 4
                g.wait_ge(step("d_a1"), freed(D_LAG, "d_a1", it, -1, 2))
                g.wait_ge(step("d_x1k"), freed(D_LAG, "d_x1k", it, -1, 4))
                g.tensor_copy(stage[:, w, 8:10].rearrange("p (a b) -> p a b", b=1),
                              look[:, 0:2, bass.ds(t + 4, 1)]).then_inc(s_stage4, 1)
                wait_apart(g, s_stage4, 2 * t + 1)
                for a, o, q in ((0, d_x1s[w % 2], dma_xs[w % 2]), (1, d_x1d[w], dma_xd[w])):
                    g.indirect_dma_start(out=o, out_offset=None, in_=x1_tab,
                                         in_offset=bass.IndirectOffsetOnAxis(ap=stage[:, w, 8 + a:9 + a], axis=0),
                                         bounds_check=N + SLOTS - 1, oob_is_err=False).then_inc(q, 16)

            gather(-1, -1)
            def turn(it, u, i):
                g.tensor_copy(stage[:, u, 10:11], look[:, 2, bass.ds(it, 1)]).then_inc(s_stage4, 1)
                gather(it, u)
                g.wait_ge(step("d_pT"), made(D_LAG, "d_pT", it, 1))
                wait_apart(g, step("d_r"), it - (1 + 4 - D_LAG["d_r"]) + CREDIT + 1)
                g.tensor_copy(d_x1k[(u - 1) % 4], d_x1d[(u - 1) % 4]).then_inc(step("d_x1k"), 1)
                g.tensor_tensor(d_x1c[(u - 1) % 4], d_x1d[(u - 1) % 4], cl[:], ALU.add).then_inc(step("d_x1c"), 1)
                wait_apart(g, step("d_o2"), turn_end(it))
                g.indirect_dma_start(out=out, out_offset=bass.IndirectOffsetOnAxis(ap=stage[:, u, 10:11], axis=0),
                                     in_=d_out[u], in_offset=None, bounds_check=N - 1,
                                     oob_is_err=False).then_inc(dma_p[u], 16)
            rounds_of_tiles(g, turn)
            past = D_TURNS
            g.wait_ge(dma_xs[past % 2], 16 * (past // 2 + 1))
            g.wait_ge(dma_xd[past % 4], 16 * (past // 4 + 1))
            for u in range(4):
                g.wait_ge(dma_p[u], landed(ROWS_FROM + len(range(u, D_TURNS, 4))))

        def d_pe(pe):
            credit(pe, "d_pc d_pa d_pC d_pT d_pK d_pO d_pU d_pV d_pL d_pN d_pY")
            def X(b, a):
                return d_xT[b][:, a * D:(a + 1) * D]
            def turn(it, u, i):
                k, q = u % 2, (u - 1) % 2
                pe.wait_ge(dma_ea[k], 16 * (2 * i + (u // 2 + 1)))
                pe.wait_ge(dma_xs[k], 16 * (2 * i + (u // 2 + 1)))
                pe.wait_ge(dma_xd[u], 16 * (i + 1))
                pe.wait_ge(step("d_onT"), turn_end(it, 1))
                for a, s_ in ((0, d_x1s[k]), (1, d_x1d[u]), (2, d_ea[k])):
                    t = pe.transpose(TB[:, a * P:(a + 1) * P], s_, ident[:])
                t.then_inc(step("d_pT"), 1)
                pe.wait_ge(step("d_o"), freed(D_LAG, "d_o", it, 1, 1))
                bias_mm(pe, KB[:], BOUT, HC)
                pe.matmul(KB[:], X(q, 1), Wskip_s[:], start=False, stop=True).then_inc(step("d_pK"), 1)
                pe.wait_ge(step("d_xT"), made(D_LAG, "d_xT", it, 0))
                pe.wait_ge(step("d_al"), freed(D_LAG, "d_al", it, 0, 1))
                pe.matmul(UB[:], X(k, 1), Aqk_s[:], start=True, stop=True)
                pe.matmul(WB[:], X(k, 1), Aqe_s[:], start=True, stop=True)
                pe.wait_ge(step("d_z"), turn_end(it, 1))
                for n, a in enumerate((1, 0, 2)):
                    t = pe.matmul(LB[:, LR:LR + H], X(k, a), small_w[:, n * H:(n + 1) * H],
                                  start=(n == 0), stop=(n == 2))
                t.then_inc(step("d_pU"), 1)
                pe.wait_ge(step("d_max"), turn_end(it))
                pe.matmul(VB[:], X(q, 0), Wv_s[:], start=True, stop=False)
                pe.matmul(VB[:], X(q, 2), We_s[:], start=False, stop=True).then_inc(step("d_pV"), 1)
                pe.wait_ge(step("d_ex"), made(D_LAG, "d_ex", it, 1))
                pe.wait_ge(step("d_num"), freed(D_LAG, "d_num", it, 1, 1))
                pe.matmul(DEN, d_same[q], fx[:, 0:H], start=True, stop=True).then_inc(step("d_pL"), 1)
                pe.wait_ge(step("d_onT"), made(D_LAG, "d_onT", it, 3))
                pe.wait_ge(step("d_R"), turn_end(it))
                for h in range(H):
                    t = pe.matmul(LB[:, LY:LY + D], hs(d_onT, h), Wg_s[:, h, :], start=(h == 0), stop=(h == H - 1))
                t.then_inc(step("d_pY"), 1)
                pe.wait_ge(step("d_mat"), made(D_LAG, "d_mat", it, 0))
                pe.wait_ge(step("d_den"), made(D_LAG, "d_den", it, 1))
                pe.wait_ge(step("d_t1"), turn_end(it))
                pe.matmul(CAR, d_last[k], d_carry[q][:, 0:9], start=True, stop=True).then_inc(step("d_pc"), 1)
                pe.wait_ge(step("d_vex"), made(D_LAG, "d_vex", it, 1))
                pe.matmul(NB[:], d_same[q], d_vex, start=True, stop=True).then_inc(step("d_pN"), 1)
                pe.wait_ge(step("d_on"), made(D_LAG, "d_on", it, 2))
                for h in range(H):
                    t = pe.transpose(hs(TB, h), hs(d_on, h), ident[:])
                t.then_inc(step("d_pO"), 1)
                pe.wait_ge(step("d_al"), made(D_LAG, "d_al", it, 0))
                for h in range(H):
                    t = pe.transpose(hs(VB, h), d_al[k][:, h:h + 1].to_broadcast([P, P]), ident[:])
                t.then_inc(step("d_pa"), 1)
                pe.wait_ge(step("d_num"), made(D_LAG, "d_num", it, 1))
                pe.wait_ge(step("d_car"), turn_end(it))
                pe.matmul(CB[:], d_last[k], d_num[q], start=True, stop=True).then_inc(step("d_pC"), 1)
            rounds_of_tiles(pe, turn)

        def d_act(act):
            credit(act, "d_xT d_ln d_rs d_on d_ex d_t1 d_onT d_vex d_e d_ln2 d_rs2 d_o2")
            def turn(it, u, i):
                k = u % 2
                act.wait_ge(step("d_z"), made(D_LAG, "d_z", it, 4))
                act.wait_ge(step("d_w"), freed(D_LAG, "d_w", it, 4, 1))
                act.activation(d_e, d_z, ACT.Exp).then_inc(step("d_e"), 1)
                act.wait_ge(step("d_pT"), made(D_LAG, "d_pT", it, 0))
                act.wait_ge(step("d_pV"), freed(D_LAG, "d_pV", it, 0, 2))
                act.activation(d_xT[k], TB[:, 0:3 * P], ACT.Copy).then_inc(step("d_xT"), 1)
                act.wait_ge(step("d_dfx"), made(D_LAG, "d_dfx", it, 1))
                act.wait_ge(step("d_den"), freed(D_LAG, "d_den", it, 1, 1))
                act.activation(fx, dfx, ACT.Exp).then_inc(step("d_ex"), 1)
                act.wait_ge(step("d_pC"), made(D_LAG, "d_pC", it, 1))
                act.wait_ge(step("d_num"), freed(D_LAG, "d_num", it, 1, 1))
                act.wait_ge(step("d_ex"), made(D_LAG, "d_ex", it, 1))
                for h in range(H):
                    t = act.activation(hs(d_t1, h), hs(CB, h), ACT.Copy, scale=fx[:, 4 + h:5 + h])
                t.then_inc(step("d_t1"), 1)
                act.wait_ge(step("d_bn"), made(D_LAG, "d_bn", it, 2))
                act.activation(lw, mvv[:, 1:2], ACT.Ln, bias=eps[:, 0:1]).then_inc(step("d_ln"), 1)
                act.wait_ge(step("d_ln"), made(D_LAG, "d_ln", it, 2))
                act.activation(rs, lw, ACT.Exp, scale=-0.5).then_inc(step("d_rs"), 1)
                act.wait_ge(step("d_bn2"), made(D_LAG, "d_bn2", it, 4))
                act.activation(lw2, mv2[:, 1:2], ACT.Ln, bias=eps[:, 0:1]).then_inc(step("d_ln2"), 1)
                act.wait_ge(step("d_ln2"), made(D_LAG, "d_ln2", it, 4))
                act.activation(rs2, lw2, ACT.Exp, scale=-0.5).then_inc(step("d_rs2"), 1)
                act.wait_ge(step("d_pV"), made(D_LAG, "d_pV", it, 1))
                act.wait_ge(step("d_pN"), freed(D_LAG, "d_pN", it, 1, 1))
                for h in range(H):
                    t = act.activation(hs(d_vex, h), hs(VB, h), ACT.Copy, scale=fx[:, h:h + 1])
                t.then_inc(step("d_vex"), 1)
                act.wait_ge(step("d_nm"), made(D_LAG, "d_nm", it, 2))
                act.wait_ge(step("d_pO"), freed(D_LAG, "d_pO", it, 2, 1))
                act.activation(d_on, d_o, ACT.Identity, scale=rs, bias=nm).then_inc(step("d_on"), 1)
                act.wait_ge(step("d_nm2"), made(D_LAG, "d_nm2", it, 4))
                act.wait_ge(dma_p[u], landed(i + ROWS_FROM))
                act.activation(d_out[u], d_w, ACT.Identity, scale=rs2, bias=nm2).then_inc(step("d_o2"), 1)
                act.wait_ge(step("d_pO"), made(D_LAG, "d_pO", it, 2))
                act.wait_ge(step("d_pY"), freed(D_LAG, "d_pY", it, 2, 1))
                act.activation(d_onT, TB[:], ACT.Copy).then_inc(step("d_onT"), 1)
            rounds_of_tiles(act, turn)

        def d_dve(v):
            for t in (*d_num, d_o, d_e, d_z, d_r, d_w, d_onT, d_small, *d_xT, *d_last, *d_neg, *d_al, *d_x1c, *d_x1k,
                      *d_x1d[2:], *scr, VB, CB):
                v.memset(t[:], 0.0)
            for t in (*d_carry, *d_rden, *d_same):
                v.memset(t, 1.0)
            v.drain()
            credit(v, "d_al d_r d_z d_den d_num d_o d_car d_max d_R d_bn d_nm d_dfx d_w d_bn2 d_nm2 d_mat d_a1 d_st "
                      "d_st2 d_mc d_d0 d_g1 d_g2")
            def turn(it, u, i):
                k, q = u % 2, (u - 1) % 2
                now, old = scr[u], scr[(u - 1) % 4]
                v.wait_ge(step("d_pa"), made(D_LAG, "d_pa", it, 1))
                wait_apart(v, step("d_d0"), it + CREDIT)
                for h in range(H):
                    t = v.tensor_tensor_reduce(hs(d_junk, h), hs(VB, h), d_neg[q], 1.0, old[:, 10 + h:11 + h],
                                               ALU.add, ALU.max, d_carry[q][:, h:h + 1])
                t.then_inc(step("d_max"), 1)
                v.wait_ge(step("d_z"), made(D_LAG, "d_z", it, 4))
                v.wait_ge(step("d_x1k"), made(D_LAG, "d_x1k", it, 4))
                v.scalar_tensor_tensor(out=d_r, in0=d_z, scalar=0.0, in1=d_x1k[u], op0=ALU.max,
                                       op1=ALU.add).then_inc(step("d_r"), 1)
                v.wait_ge(step("d_max"), made(D_LAG, "d_max", it, 1))
                v.wait_ge(step("d_ex"), freed(D_LAG, "d_ex", it, 1, 1))
                v.tensor_tensor(dfx[:, 0:4], d_al[q], d_carry[q][:, 0:4], ALU.subtract)
                v.tensor_tensor(dfx[:, 4:8], old[:, 10:14], d_carry[q][:, 0:4], ALU.subtract).then_inc(step("d_dfx"), 1)
                v.wait_ge(step("d_o"), made(D_LAG, "d_o", it, 2))
                v.bn_stats(stt, d_o).then_inc(step("d_st"), 1)
                v.wait_ge(step("d_e"), made(D_LAG, "d_e", it, 4))
                v.wait_ge(step("d_r"), made(D_LAG, "d_r", it, 4))
                v.wait_ge(step("d_o2"), freed(D_LAG, "d_o2", it, 4, 1))
                v.scalar_tensor_tensor(out=d_w, in0=d_e, scalar=1.0, in1=d_r, op0=ALU.min,
                                       op1=ALU.add).then_inc(step("d_w"), 1)
                row = dst_row[:, bass.ds(it * P, P)]
                mine, prev = dst_f[:, bass.ds(it + 1, 1)], dst_f[:, bass.ds(it, 1)]
                v.wait_ge(step("d_pN"), turn_end(it, 1))
                v.tensor_scalar(d_same[k], row, mine, None, ALU.is_equal)
                v.tensor_scalar(d_neg[k], row, mine, -BIG, ALU.not_equal, ALU.mult)
                v.tensor_scalar(d_last[k], row, prev, e127[:, 0:1], ALU.is_equal, ALU.mult).then_inc(step("d_mat"), 1)
                v.wait_ge(step("d_w"), made(D_LAG, "d_w", it, 4))
                v.bn_stats(st2, d_w).then_inc(step("d_st2"), 1)
                wait_apart(v, step("d_st2"), it + CREDIT + 1)
                v.bn_aggr(mv2, st2).then_inc(step("d_bn2"), 1)
                v.wait_ge(step("d_pU"), made(D_LAG, "d_pU", it, 0))
                v.scalar_tensor_tensor(out=ssum, in0=LB[:, LR:LR + H], scalar=SCALE, in1=alpha_c[:],
                                       op0=ALU.mult, op1=ALU.add).then_inc(step("d_R"), 1)
                wait_apart(v, step("d_st"), turn_end(it))
                v.bn_aggr(mvv, stt).then_inc(step("d_bn"), 1)
                v.wait_ge(step("d_R"), made(D_LAG, "d_R", it, 0))
                for h in range(H):
                    t = v.tensor_tensor_reduce(hs(d_junk, h), hs(UB, h), d_x1s[k], SCALE, ssum[:, h:h + 1],
                                               ALU.mult, ALU.add, amx[:, h:h + 1])
                t.then_inc(step("d_a1"), 1)
                v.wait_ge(step("d_ex"), made(D_LAG, "d_ex", it, 1))
                v.tensor_tensor(old[:, 0:4], old[:, 5:9], fx[:, 4:8], ALU.mult).then_inc(step("d_g1"), 1)
                v.wait_ge(step("d_rs"), made(D_LAG, "d_rs", it, 2))
                v.wait_ge(step("d_on"), freed(D_LAG, "d_on", it, 2, 1))
                v.scalar_tensor_tensor(out=nm, in0=mvv[:, 0:1], scalar=-1.0, in1=rs, op0=ALU.mult,
                                       op1=ALU.mult).then_inc(step("d_nm"), 1)
                v.wait_ge(step("d_rs2"), made(D_LAG, "d_rs2", it, 4))
                v.wait_ge(step("d_o2"), freed(D_LAG, "d_o2", it, 4, 1))
                v.scalar_tensor_tensor(out=nm2, in0=mv2[:, 0:1], scalar=-1.0, in1=rs2, op0=ALU.mult,
                                       op1=ALU.mult).then_inc(step("d_nm2"), 1)
                v.wait_ge(step("d_pL"), made(D_LAG, "d_pL", it, 1))
                v.wait_ge(step("d_g1"), made(D_LAG, "d_g1", it, 1))
                v.tensor_tensor(d_carry[q][:, 5:9], DEN, old[:, 0:4], ALU.add).then_inc(step("d_g2"), 1)
                v.wait_ge(step("d_g2"), made(D_LAG, "d_g2", it, 1))
                v.reciprocal(d_rden[q], d_carry[q][:, 5:9]).then_inc(step("d_den"), 1)
                v.wait_ge(step("d_pY"), made(D_LAG, "d_pY", it, 3))
                v.wait_ge(step("d_x1c"), made(D_LAG, "d_x1c", it, 3))
                v.wait_ge(step("d_e"), freed(D_LAG, "d_e", it, 3, 1))
                v.tensor_tensor(d_z, LB[:, LY:LY + D], d_x1c[(u - 3) % 4], ALU.add).then_inc(step("d_z"), 1)
                v.wait_ge(step("d_pc"), made(D_LAG, "d_pc", it, 0))
                v.tensor_copy(now[:, 0:9], CAR).then_inc(step("d_car"), 1)
                v.wait_ge(step("d_a1"), made(D_LAG, "d_a1", it, 0))
                for h in range(H):
                    t = v.tensor_tensor_reduce(hs(d_junk, h), hs(WB, h), d_ea[k], SCALE, amx[:, h:h + 1],
                                               ALU.mult, ALU.add, d_al[k][:, h:h + 1])
                t.then_inc(step("d_al"), 1)
                v.wait_ge(step("d_pN"), made(D_LAG, "d_pN", it, 1))
                v.wait_ge(step("d_t1"), made(D_LAG, "d_t1", it, 1))
                v.tensor_tensor(d_num[q], NB[:], d_t1, ALU.add).then_inc(step("d_num"), 1)
                v.wait_ge(step("d_car"), made(D_LAG, "d_car", it, 0))
                v.tensor_scalar(now[:, 9:10], now[:, 4:5], 1.0, BIG, ALU.subtract, ALU.mult).then_inc(step("d_mc"), 1)
                v.wait_ge(step("d_mc"), made(D_LAG, "d_mc", it, 0))
                v.tensor_scalar(now[:, 10:14], now[:, 0:4], now[:, 9:10], None, ALU.add).then_inc(step("d_d0"), 1)
                v.wait_ge(step("d_pK"), made(D_LAG, "d_pK", it, 1))
                v.wait_ge(step("d_num"), made(D_LAG, "d_num", it, 1))
                v.wait_ge(step("d_on"), freed(D_LAG, "d_on", it, 1, 1))
                for h in range(H):
                    t = v.scalar_tensor_tensor(out=hs(d_o, h), in0=hs(d_num[q], h), scalar=d_rden[q][:, h:h + 1],
                                               in1=hs(KB, h), op0=ALU.mult, op1=ALU.add)
                t.then_inc(step("d_o"), 1)
            rounds_of_tiles(v, turn)

        def phase(sync, pool, pe, act, dve):
            with ExitStack() as scope:
                phase_scope[0] = scope
                steps.clear()
                with nc.Block() as block:
                    block.sync(sync)
                    block.gpsimd(pool)
                    block.tensor(pe)
                    block.scalar(act)
                    block.vector(dve)
                for s in steps.values():
                    nc.gpsimd.sem_clear(s)
                nc.all_engine_barrier()

        phase(setup_sync, setup_pool, setup_pe, lambda act: act.preload_act_table_set(ACT_SET), setup_dve)
        phase(b_sync, b_pool, b_pe, b_act, b_dve)
        phase(a_sync, a_pool, a_pe, a_act, a_dve)
        phase(c_sync, c_pool, c_pe, c_act, c_dve)
        phase(d_sync, d_pool, d_pe, d_act, d_dve)


_INS = ['x', 'src', 'dst', 'edge_attr_128', 'L0_gnn_W_self0', 'L0_gnn_W_neigh0', 'L0_gnn_b0', 'L0_gnn_W_self1',
        'L0_gnn_W_neigh1', 'L0_gnn_b1', 'L1_gnn_Wq', 'L1_gnn_bq', 'L1_gnn_Wk', 'L1_gnn_bk', 'L1_gnn_Wv', 'L1_gnn_bv',
        'L1_gnn_We', 'L1_gnn_be', 'L1_gnn_Wskip', 'L1_gnn_bskip', 'L1_gnn_ln_g', 'L1_gnn_ln_b', 'L1_gnn_Wlin',
        'L1_gnn_blin']
_OUTS = [((50000, 128), 'float32')]


def kernel(**inputs):
    import numpy as _np
    import concourse.bacc as _bacc
    from concourse import mybir as _mybir
    from concourse.bass_utils import run_bass_kernel_spmd as _run

    nc = _bacc.Bacc("TRN2", target_bir_lowering=False, num_devices=1)
    arrays, args = {}, []
    for name in _INS:
        a = _np.ascontiguousarray(inputs[name])
        arrays[f"in_{name}_dram"] = a
        args.append(nc.dram_tensor(f"in_{name}_dram", a.shape, _mybir.dt.from_np(a.dtype), kind="ExternalInput").ap())
    for i, (shape, dtype) in enumerate(_OUTS):
        dt = _mybir.dt.from_np(_np.dtype(dtype))
        args.append(nc.dram_tensor(f"out_{i}_dram", shape, dt, kind="ExternalOutput").ap())
    gnn_kernel(nc, *args)
    r = _run(nc, [arrays], core_ids=[0])
    return r.results[0]["out_0_dram"]
```
